# Optimizing a Trainium2 kernel written in Bass

```python
import numpy as np
import jax
import jax.numpy as jnp

def _softmax(x, axis=-1):
    return jax.nn.softmax(x, axis=axis)

def _gelu(x):
    return jax.nn.gelu(x, approximate=True)

def _silu(x):
    return jax.nn.silu(x)

def _sigmoid(x):
    return jax.nn.sigmoid(x)

def _layernorm(x, axis=-1, eps=1e-05):
    m = jnp.mean(x, axis=axis, keepdims=True)
    v = jnp.var(x, axis=axis, keepdims=True)
    return (x - m) / jnp.sqrt(v + eps)

def _scatter_add(tgt, idx, src, axis=0):
    return tgt.at[idx].add(src)

def _segment_sum(src, seg, n):
    return jax.ops.segment_sum(src, seg, n)
kernel_name = 'mk_recurrent_d2_jaxref_r8_d84f31'

def setup_inputs(seed: int=0):
    np.random.seed(seed)
    _w = jnp.asarray

    def _L0_attn_setup():
        import jax, jax.numpy as jnp
        import numpy as np
        from jax import lax
        H = 64
        P = 64
        N = 128
        G = 8
        K = 4
        D_MODEL = 512
        I = H * P
        GN = G * N
        CONV_DIM = I + 2 * GN
        PROJ = I + CONV_DIM + H
        EPS = 1e-05
        GROUP_SIZE = I // G

        def _reference_tuple_inner(hidden_states, in_proj_w, conv_weight, conv_bias, dt_bias, A_log, D, norm_weight, out_proj_w):
            B, L, _ = hidden_states.shape
            proj = jnp.einsum('bld,pd->blp', hidden_states, in_proj_w)
            gate = proj[..., :I]
            hbc = proj[..., I:I + CONV_DIM]
            dt = proj[..., -H:]
            pad = jnp.pad(hbc, ((0, 0), (K - 1, 0), (0, 0)))
            conv = conv_bias
            for k in range(K):
                conv = conv + pad[:, k:k + L, :] * conv_weight[:, k]
            xBC = jax.nn.silu(conv)
            x = xBC[..., :I].reshape(B, L, H, P)
            Bm = xBC[..., I:I + GN].reshape(B, L, G, N)
            Cm = xBC[..., I + GN:].reshape(B, L, G, N)
            hpg = H // G
            B_h = jnp.repeat(Bm, hpg, axis=2)
            C_h = jnp.repeat(Cm, hpg, axis=2)
            dt_p = jax.nn.softplus(dt + dt_bias)
            A = -jnp.exp(A_log)
            dA = jnp.exp(dt_p * A)
            dtx = dt_p[..., None] * x

            def step(state, inp):
                dA_t, dtx_t, B_t, C_t = inp
                state = state * dA_t[..., None, None] + dtx_t[..., None] * B_t[:, :, None, :]
                y_t = jnp.einsum('bhpn,bhn->bhp', state, C_t)
                return (state, y_t)
            xs = (jnp.moveaxis(dA, 1, 0), jnp.moveaxis(dtx, 1, 0), jnp.moveaxis(B_h, 1, 0), jnp.moveaxis(C_h, 1, 0))
            state0 = jnp.zeros((B, H, P, N), jnp.float32)
            final_state, ys = lax.scan(step, state0, xs)
            y = jnp.moveaxis(ys, 0, 1) + x * D[None, None, :, None]
            y = y.reshape(B, L, I)
            yg = y.reshape(B, L, G, GROUP_SIZE)
            var = jnp.mean(yg * yg, axis=-1, keepdims=True)
            yn = (yg * lax.rsqrt(var + EPS)).reshape(B, L, I) * norm_weight
            yn = yn * jax.nn.silu(gate)
            out = jnp.einsum('bli,di->bld', yn, out_proj_w)
            conv_state_new = jnp.moveaxis(hbc[:, L - (K - 1):, :], 1, 2)
            return (out, conv_state_new, final_state)
        key = jax.random.key(seed)
        ks = jax.random.split(key, 6)
        B, L = (2, 256)
        s = 0.02
        return {'hidden_states': jax.random.normal(ks[0], (B, L, D_MODEL), jnp.float32), 'in_proj_w': jax.random.normal(ks[1], (PROJ, D_MODEL), jnp.float32) * s, 'conv_weight': jax.random.normal(ks[2], (CONV_DIM, K), jnp.float32) * s, 'conv_bias': jnp.zeros((CONV_DIM,), jnp.float32), 'dt_bias': jnp.ones((H,), jnp.float32), 'A_log': jnp.log(jnp.arange(1, H + 1, dtype=jnp.float32)), 'D': jnp.ones((H,), jnp.float32), 'norm_weight': jnp.ones((I,), jnp.float32), 'out_proj_w': jax.random.normal(ks[3], (D_MODEL, I), jnp.float32) * s}
    _L0_attn_in = _L0_attn_setup()

    def _L0_ffn_setup():
        import jax, jax.numpy as jnp
        import numpy as np
        NF4_CODE = jnp.array([-1.0, -0.6961928009986877, -0.5250730514526367, -0.39491748809814453, -0.28444138169288635, -0.18477343022823334, -0.09105003625154495, 0.0, 0.07958029955625534, 0.16093020141124725, 0.24611230194568634, 0.33791524171829224, 0.44070982933044434, 0.5626170039176941, 0.7229568362236023, 1.0], dtype=jnp.float32)
        BLOCKSIZE = 64

        def nf4_quant_dequant(w):
            shape = w.shape
            flat = w.reshape(-1, BLOCKSIZE)
            absmax = jnp.max(jnp.abs(flat), axis=1, keepdims=True)
            normalized = flat / jnp.where(absmax == 0, 1.0, absmax)
            bounds = (NF4_CODE[:-1] + NF4_CODE[1:]) * 0.5
            idx = jnp.searchsorted(bounds, normalized)
            return (NF4_CODE[idx] * absmax).reshape(shape)
        key = jax.random.key(seed)
        k1, k2, k3, kx = jax.random.split(key, 4)
        D, H = (512, 1376)
        scale = 0.02
        w1 = jax.random.normal(k1, (H, D), jnp.float32) * scale
        w2 = jax.random.normal(k2, (H, D), jnp.float32) * scale
        w3 = jax.random.normal(k3, (D, H), jnp.float32) * scale
        x = jax.random.normal(kx, (2, 256, D), jnp.float32)
        return {'x': x, 'w1': w1, 'w2': w2, 'w3': w3}
    _L0_ffn_in = _L0_ffn_setup()

    def _L1_attn_setup():
        import jax, jax.numpy as jnp
        import numpy as np
        EMB_DIM = 512
        N_HEADS = 32
        QKV_DIM = EMB_DIM // N_HEADS
        B, S = (4, 512)
        key = jax.random.key(seed)
        ks = jax.random.split(key, 7)
        std = 1.0 / np.sqrt(EMB_DIM)
        x = jax.random.normal(ks[0], (B, S, EMB_DIM), dtype=jnp.float32)
        Wq = jax.random.normal(ks[1], (EMB_DIM, QKV_DIM, N_HEADS), dtype=jnp.float32) * std
        bq = jnp.zeros((QKV_DIM, N_HEADS), dtype=jnp.float32)
        Wk = jax.random.normal(ks[2], (EMB_DIM, QKV_DIM, 1), dtype=jnp.float32) * std
        bk = jnp.zeros((QKV_DIM, 1), dtype=jnp.float32)
        Wv = jax.random.normal(ks[3], (EMB_DIM, QKV_DIM, 1), dtype=jnp.float32) * std
        bv = jnp.zeros((QKV_DIM, 1), dtype=jnp.float32)
        return {'x': x, 'Wq': Wq, 'bq': bq, 'Wk': Wk, 'bk': bk, 'Wv': Wv, 'bv': bv}
    _L1_attn_in = _L1_attn_setup()

    def _L1_ffn_setup():
        import jax, jax.numpy as jnp
        import numpy as np
        NUM_EXPERTS = 16
        TOP_K = 2
        INTER = 56
        key = jax.random.key(seed)
        k1, k2, k3, k4, k5 = jax.random.split(key, 5)
        B, S, H = (4, 256, 512)
        scale = 0.02
        return {'hid': jax.random.normal(k1, (B, S, H), dtype=jnp.float32), 'gate_w': jax.random.normal(k2, (NUM_EXPERTS, H), dtype=jnp.float32) * scale, 'u': jax.random.normal(k3, (NUM_EXPERTS * INTER, H), dtype=jnp.float32) * scale, 'g': jax.random.normal(k4, (NUM_EXPERTS * INTER, H), dtype=jnp.float32) * scale, 'd': jax.random.normal(k5, (H, NUM_EXPERTS * INTER), dtype=jnp.float32) * scale}
    _L1_ffn_in = _L1_ffn_setup()
    _d = {'L0_attn_hidden_states': _L0_attn_in['hidden_states'], 'L0_attn_in_proj_w': _L0_attn_in['in_proj_w'], 'L0_attn_conv_weight': _L0_attn_in['conv_weight'], 'L0_attn_conv_bias': _L0_attn_in['conv_bias'], 'L0_attn_dt_bias': _L0_attn_in['dt_bias'], 'L0_attn_A_log': _L0_attn_in['A_log'], 'L0_attn_D': _L0_attn_in['D'], 'L0_attn_norm_weight': _L0_attn_in['norm_weight'], 'L0_attn_out_proj_w': _L0_attn_in['out_proj_w'], 'L0_ffn_w1': _L0_ffn_in['w1'], 'L0_ffn_w2': _L0_ffn_in['w2'], 'L0_ffn_w3': _L0_ffn_in['w3'], 'L1_attn_Wq': _L1_attn_in['Wq'], 'L1_attn_bq': _L1_attn_in['bq'], 'L1_attn_Wk': _L1_attn_in['Wk'], 'L1_attn_bk': _L1_attn_in['bk'], 'L1_attn_Wv': _L1_attn_in['Wv'], 'L1_attn_bv': _L1_attn_in['bv'], 'L1_ffn_gate_w': _L1_ffn_in['gate_w'], 'L1_ffn_u': _L1_ffn_in['u'], 'L1_ffn_g': _L1_ffn_in['g'], 'L1_ffn_d': _L1_ffn_in['d']}
    _x0 = _d['L0_attn_hidden_states']
    _d['L0_attn_hidden_states'] = jax.random.normal(jax.random.fold_in(jax.random.key(seed), 1), (4, 512, 512), dtype=_x0.dtype)
    del _x0
    return _d

def reference(L0_attn_hidden_states, L0_attn_in_proj_w, L0_attn_conv_weight, L0_attn_conv_bias, L0_attn_dt_bias, L0_attn_A_log, L0_attn_D, L0_attn_norm_weight, L0_attn_out_proj_w, L0_ffn_w1, L0_ffn_w2, L0_ffn_w3, L1_attn_Wq, L1_attn_bq, L1_attn_Wk, L1_attn_bk, L1_attn_Wv, L1_attn_bv, L1_ffn_gate_w, L1_ffn_u, L1_ffn_g, L1_ffn_d):

    def _L0_attn_ref(hidden_states, in_proj_w, conv_weight, conv_bias, dt_bias, A_log, D, norm_weight, out_proj_w):
        import jax, jax.numpy as jnp
        import numpy as np
        from jax import lax
        H = 64
        P = 64
        N = 128
        G = 8
        K = 4
        D_MODEL = 512
        I = H * P
        GN = G * N
        CONV_DIM = I + 2 * GN
        PROJ = I + CONV_DIM + H
        EPS = 1e-05
        GROUP_SIZE = I // G

        def _reference_tuple_inner(hidden_states, in_proj_w, conv_weight, conv_bias, dt_bias, A_log, D, norm_weight, out_proj_w):
            B, L, _ = hidden_states.shape
            proj = jnp.einsum('bld,pd->blp', hidden_states, in_proj_w)
            gate = proj[..., :I]
            hbc = proj[..., I:I + CONV_DIM]
            dt = proj[..., -H:]
            pad = jnp.pad(hbc, ((0, 0), (K - 1, 0), (0, 0)))
            conv = conv_bias
            for k in range(K):
                conv = conv + pad[:, k:k + L, :] * conv_weight[:, k]
            xBC = jax.nn.silu(conv)
            x = xBC[..., :I].reshape(B, L, H, P)
            Bm = xBC[..., I:I + GN].reshape(B, L, G, N)
            Cm = xBC[..., I + GN:].reshape(B, L, G, N)
            hpg = H // G
            B_h = jnp.repeat(Bm, hpg, axis=2)
            C_h = jnp.repeat(Cm, hpg, axis=2)
            dt_p = jax.nn.softplus(dt + dt_bias)
            A = -jnp.exp(A_log)
            dA = jnp.exp(dt_p * A)
            dtx = dt_p[..., None] * x

            def step(state, inp):
                dA_t, dtx_t, B_t, C_t = inp
                state = state * dA_t[..., None, None] + dtx_t[..., None] * B_t[:, :, None, :]
                y_t = jnp.einsum('bhpn,bhn->bhp', state, C_t)
                return (state, y_t)
            xs = (jnp.moveaxis(dA, 1, 0), jnp.moveaxis(dtx, 1, 0), jnp.moveaxis(B_h, 1, 0), jnp.moveaxis(C_h, 1, 0))
            state0 = jnp.zeros((B, H, P, N), jnp.float32)
            final_state, ys = lax.scan(step, state0, xs)
            y = jnp.moveaxis(ys, 0, 1) + x * D[None, None, :, None]
            y = y.reshape(B, L, I)
            yg = y.reshape(B, L, G, GROUP_SIZE)
            var = jnp.mean(yg * yg, axis=-1, keepdims=True)
            yn = (yg * lax.rsqrt(var + EPS)).reshape(B, L, I) * norm_weight
            yn = yn * jax.nn.silu(gate)
            out = jnp.einsum('bli,di->bld', yn, out_proj_w)
            conv_state_new = jnp.moveaxis(hbc[:, L - (K - 1):, :], 1, 2)
            return (out, conv_state_new, final_state)
        return _reference_tuple_inner(hidden_states, in_proj_w, conv_weight, conv_bias, dt_bias, A_log, D, norm_weight, out_proj_w)[0]

    def _L0_ffn_ref(x, w1, w2, w3):
        import jax, jax.numpy as jnp
        import numpy as np
        NF4_CODE = jnp.array([-1.0, -0.6961928009986877, -0.5250730514526367, -0.39491748809814453, -0.28444138169288635, -0.18477343022823334, -0.09105003625154495, 0.0, 0.07958029955625534, 0.16093020141124725, 0.24611230194568634, 0.33791524171829224, 0.44070982933044434, 0.5626170039176941, 0.7229568362236023, 1.0], dtype=jnp.float32)
        BLOCKSIZE = 64

        def nf4_quant_dequant(w):
            shape = w.shape
            flat = w.reshape(-1, BLOCKSIZE)
            absmax = jnp.max(jnp.abs(flat), axis=1, keepdims=True)
            normalized = flat / jnp.where(absmax == 0, 1.0, absmax)
            bounds = (NF4_CODE[:-1] + NF4_CODE[1:]) * 0.5
            idx = jnp.searchsorted(bounds, normalized)
            return (NF4_CODE[idx] * absmax).reshape(shape)
        dq1 = nf4_quant_dequant(w1)
        dq2 = nf4_quant_dequant(w2)
        dq3 = nf4_quant_dequant(w3)
        gate = jnp.einsum('bsd,hd->bsh', x, dq1)
        up = jnp.einsum('bsd,hd->bsh', x, dq2)
        h = jax.nn.silu(gate) * up
        return jnp.einsum('bsh,dh->bsd', h, dq3)

    def _L1_attn_ref(x, Wq, bq, Wk, bk, Wv, bv):
        import jax, jax.numpy as jnp
        import numpy as np
        EMB_DIM = 512
        N_HEADS = 32
        QKV_DIM = EMB_DIM // N_HEADS
        B, S = (4, 512)
        q = jnp.einsum('bsD,Ddh->bsdh', x, Wq) + bq
        k = (jnp.einsum('bsD,Ddh->bsdh', x, Wk) + bk)[..., 0]
        v = (jnp.einsum('bsD,Ddh->bsdh', x, Wv) + bv)[..., 0]
        qkv_dim = q.shape[-2]
        n_heads = q.shape[-1]
        scale = 1.0 / jnp.sqrt(jnp.asarray(qkv_dim, dtype=q.dtype))
        scores = jnp.einsum('bsdh,bse->bsde', q, k) * scale
        p = jax.nn.softmax(scores, axis=-1)
        o = jnp.einsum('bsde,bse->bsd', p, v)
        out = jnp.broadcast_to(o[..., None], o.shape + (n_heads,))
        return out.reshape(x.shape[:-1] + (qkv_dim * n_heads,))

    def _L1_ffn_ref(hid, gate_w, u, g, d):
        import jax, jax.numpy as jnp
        import numpy as np
        NUM_EXPERTS = 16
        TOP_K = 2
        INTER = 56
        B, S, H = hid.shape
        x = hid.reshape(-1, H)
        bs = x.shape[0]
        logits = x @ gate_w.T
        probs = jax.nn.softmax(logits.astype(jnp.float32), axis=-1)
        vals, idx = jax.lax.top_k(probs, TOP_K)
        vals = vals / jnp.sum(vals, axis=-1, keepdims=True)
        rows = jnp.arange(bs)[:, None]
        w = jnp.zeros((bs, NUM_EXPERTS), dtype=jnp.float32).at[rows, idx].set(vals)
        w = w.astype(x.dtype)
        gate_out = (x @ g.T).reshape(bs, NUM_EXPERTS, INTER)
        up_out = (x @ u.T).reshape(bs, NUM_EXPERTS, INTER)
        h = jax.nn.silu(gate_out) * up_out
        d_r = d.reshape(H, NUM_EXPERTS, INTER)
        out = jnp.einsum('bei,hei,be->bh', h, d_r, w)
        return out.reshape(B, S, H)
    x = L0_attn_hidden_states
    xn = _layernorm(x, axis=-1)
    s = _L0_attn_ref(xn, L0_attn_in_proj_w, L0_attn_conv_weight, L0_attn_conv_bias, L0_attn_dt_bias, L0_attn_A_log, L0_attn_D, L0_attn_norm_weight, L0_attn_out_proj_w)
    g = _silu(_L0_ffn_ref(xn, L0_ffn_w1, L0_ffn_w2, L0_ffn_w3))
    x = x + s * g
    xn = _layernorm(x, axis=-1)
    s = _L1_attn_ref(xn, L1_attn_Wq, L1_attn_bq, L1_attn_Wk, L1_attn_bk, L1_attn_Wv, L1_attn_bv)
    g = _silu(_L1_ffn_ref(xn, L1_ffn_gate_w, L1_ffn_u, L1_ffn_g, L1_ffn_d))
    x = x + s * g
    return x

_drawn_inputs = setup_inputs


def setup_inputs(seed=0):
    import zlib

    import numpy as np

    out = dict(_drawn_inputs(seed))
    spreads = {'L0_attn_conv_bias': (0.0, 0.371),
     'L0_attn_dt_bias': (1.0, 0.6),
     'L0_attn_D': (1.0, 0.6),
     'L0_attn_norm_weight': (1.0, 0.6),
     'L1_attn_bq': (0.0, 0.8),
     'L1_attn_bk': (0.0, 0.8),
     'L1_attn_bv': (0.0, 0.8)}
    factors = {'L0_attn_in_proj_w': 3.652,
     'L0_attn_conv_weight': 8.0,
     'L0_attn_A_log': 8.0,
     'L0_attn_out_proj_w': 3.299,
     'L0_ffn_w1': 3.379,
     'L0_ffn_w2': 3.462,
     'L0_ffn_w3': 3.313,
     'L1_attn_Wq': 8.0,
     'L1_attn_Wk': 8.0,
     'L1_attn_Wv': 8.0,
     'L1_ffn_gate_w': 8.0,
     'L1_ffn_u': 8.0,
     'L1_ffn_g': 8.0,
     'L1_ffn_d': 8.0}
    for name, (base, spread) in spreads.items():
        noise = np.random.default_rng([zlib.crc32(name.encode()), seed]).standard_normal(out[name].shape)
        drawn = base * np.exp(spread * noise) if base else spread * noise
        out[name] = jnp.asarray(drawn.astype(out[name].dtype))
    for name, factor in factors.items():
        out[name] = (out[name] * factor).astype(out[name].dtype)
    return out
```

```python
from contextlib import ExitStack

import concourse.bass as bass
import numpy as np
from concourse import mybir

F32 = mybir.dt.float32
F32R = mybir.dt.float32r
ALU = mybir.AluOpType
ACT = mybir.ActivationFunctionType
AX_X = mybir.AxisListType.X

P = 128
T = 2048
DM = 512
KD = DM // P
SEQ = 512
NT = T // P
HEADS, HD, GROUPS = 64, 64, 8
HPG = HEADS // GROUPS
XBC = 6
HALVES = 2
HT = T // HALVES
SLOTS = HT // P
EPS = 1e-5
DT_, WDT_, EXC_, TOT_ = range(4)

NF4 = [-1.0, -0.6961928009986877, -0.5250730514526367, -0.39491748809814453, -0.28444138169288635,
       -0.18477343022823334, -0.09105003625154495, 0.0, 0.07958029955625534, 0.16093020141124725,
       0.24611230194568634, 0.33791524171829224, 0.44070982933044434, 0.5626170039176941,
       0.7229568362236023, 1.0]
BLK = 64
FF = 1376
FT = -(-FF // P)
EXPERTS, INTER = 16, 56
MF = EXPERTS * INTER
MT = MF // P
QK = 16
NQ = 4 * QK


def split3(pe, out, stat, mov, kt):
    n = 0
    for k in range(kt):
        for a, b in ((0, 0), (0, 1), (1, 0)):
            last = pe.matmul(out, stat(a, k), mov(b, k), start=(n == 0), stop=(n == 3 * kt - 1))
            n += 1
    return last


def plain_wait(eng, met_sem, met, sem, value):
    eng.compute_val(value)
    eng.wait_ge(met_sem, met)
    eng.wait_ge(sem, value)


def start_at_one(eng, *sems):
    for sem in sems:
        eng.sem_inc(sem, 1)


def norm_phase(nc, S, src_dram, xnt_dram, tag, wdt_dram=None, dtb_dram=None, dtr=None):
    with ExitStack() as ctx:
        def sb(n, s, d=F32):
            return ctx.enter_context(nc.sbuf_tensor(tag + n, s, d))

        def sem(n):
            return S(tag + n)

        x = sb("x", [P, 2, DM])
        stat = sb("stat", [P, 2, 6])
        mv = sb("mv", [P, 2, 2])
        ve = sb("ve", [P, 2, 1])
        rstd = sb("rstd", [P, 2, 1])
        half = sb("half", [P, 1])
        xn = sb("xn", [P, 2, DM])
        xh = sb("xh", [P, 2, 2, DM], F32R)
        ident = sb("ident", [P, P])
        tp = [ctx.enter_context(nc.psum_tensor(f"{tag}tp{i}", [P, DM], F32)) for i in range(2)]
        if wdt_dram is not None:
            wraw = sb("wraw", [P, KD, HEADS])
            wdt = sb("wdt", [P, 2, KD, HEADS], F32R)
            dtb = sb("dtb", [P, HEADS])
            pd = [ctx.enter_context(nc.psum_tensor(f"{tag}pd{i}", [P, 512], F32)) for i in range(2)]
        loaded = [sem(f"loaded{i}") for i in range(2)]
        consts, const_ld, wsplit = sem("consts"), sem("const_ld"), sem("wsplit")
        stats, mean_var, var_eps, rstd_ok = sem("stats"), sem("mean_var"), sem("var_eps"), sem("rstd_ok")
        normed, turned, hi_ok, lo_ok = sem("normed"), sem("turned"), sem("hi_ok"), sem("lo_ok")
        dt_mm, dt_out = sem("dt_mm"), sem("dt_out")
        stored = [sem(f"stored{i}") for i in range(2)]
        block = ctx.enter_context(nc.Block())

        @block.sync
        def _(sp):
            sp.dma_start(ident[:], S.ident_dram).then_inc(const_ld, 16)
            if wdt_dram is not None:
                sp.dma_start(wraw[:], wdt_dram).then_inc(const_ld, 16)
                sp.dma_start(dtb[:], dtb_dram.partition_broadcast(P)).then_inc(const_ld, 16)
            for r in range(2):
                sp.dma_start(x[:, r, :], src_dram[r * P:(r + 1) * P, :]).then_inc(loaded[r], 16)
            with sp.Fori(0, NT // 2 - 1) as i:
                for r in range(2):
                    plain_wait(sp, const_ld, 16, normed, 2 * i + r + 1)
                    sp.dma_start(x[:, r, :], src_dram[bass.ds((2 * i + 2 + r) * P, P), :]).then_inc(loaded[r], 16)
                    plain_wait(sp, const_ld, 16, hi_ok, 2 * i + r + 1)
                    sp.wait_ge(lo_ok, 2 * i + r + 1)
                    sp.dma_start(xnt_dram[2 * i + r], xh[:, r, :, :].bitcast(F32)).then_inc(stored[r], 16)
            for r in range(2):
                sp.wait_ge(hi_ok, NT - 1 + r)
                sp.wait_ge(lo_ok, NT - 1 + r)
                sp.dma_start(xnt_dram[NT - 2 + r], xh[:, r, :, :].bitcast(F32)).then_inc(stored[r], 16)
            for r in range(2):
                sp.wait_ge(stored[r], 16 * NT // 2 + 1)

        @block.gpsimd
        def _(pool):
            pool.memset(half[:], -0.5).then_inc(consts, 1)
            pool.wait_ge(consts, 1)
            with pool.Fori(0, NT // 2) as i:
                for r in range(2):
                    plain_wait(pool, consts, 1, mean_var, 2 * i + r + 1)
                    pool.tensor_scalar(ve[:, r, :], mv[:, r, 1:2], EPS, 1.0, ALU.add, ALU.mult).then_inc(var_eps, 1)
                    pool.wait_ge(var_eps, 2 * i + r + 1)
                    pool.tensor_tensor(rstd[:, r, :], ve[:, r, :], half[:], ALU.pow).then_inc(rstd_ok, 1)

        @block.vector
        def _(dve):
            if wdt_dram is not None:
                dve.wait_ge(const_ld, 48)
                dve.tensor_copy(wdt[:, 0, :, :], wraw[:]).then_inc(wsplit, 1)
                dve.wait_ge(wsplit, 1)
                dve.tensor_tensor(wdt[:, 1, :, :], wraw[:], wdt[:, 0, :, :].bitcast(F32), ALU.subtract).then_inc(wsplit, 1)
            with dve.Fori(0, NT // 2) as i:
                for r in range(2):
                    n = 2 * i + r
                    dve.wait_ge(loaded[r], 16 * i + 16)
                    dve.bn_stats(stat[:, r, :], x[:, r, :]).then_inc(stats, 1)
                    plain_wait(dve, const_ld, 16, stats, n + 1)
                    dve.bn_aggr(mv[:, r, :], stat[:, r, :]).then_inc(mean_var, 1)
                    dve.wait_ge(rstd_ok, n + 1)
                    dve.tensor_scalar(xn[:, r, :], x[:, r, :], mv[:, r, 0:1], rstd[:, r, :],
                                      ALU.subtract, ALU.mult).then_inc(normed, 1)
                    dve.wait_ge(turned, n + 1)
                    dve.wait_ge(hi_ok, n + 1)
                    dve.tensor_tensor(xh[:, r, 1, :], tp[r][:], xh[:, r, 0, :].bitcast(F32), ALU.subtract).then_inc(lo_ok, 1)
                    if wdt_dram is not None:
                        dve.wait_ge(dt_mm, n + 1)
                        dve.tensor_tensor(dtr[:, bass.ds(n, 1), :], pd[r][:, 0:HEADS].rearrange("p (o h) -> p o h", o=1),
                                          dtb[:].rearrange("p (o h) -> p o h", o=1), ALU.add).then_inc(dt_out, 1)

        @block.scalar
        def _(act):
            start_at_one(act, *stored)
            with act.Fori(0, NT // 2) as i:
                for r in range(2):
                    act.wait_ge(turned, 2 * i + r + 1)
                    act.wait_ge(stored[r], 16 * i + 1)
                    act.activation(xh[:, r, 0, :], tp[r][:], ACT.Copy).then_inc(hi_ok, 1)

        @block.tensor
        def _(pe):
            pe.wait_ge(const_ld, 48 if wdt_dram is not None else 16)
            if wdt_dram is not None:
                pe.wait_ge(wsplit, 2)
            with pe.Fori(0, NT // 2) as i:
                for r in range(2):
                    n = 2 * i + r
                    pe.wait_ge(normed, n + 1)
                    for k in range(KD):
                        last = pe.transpose(tp[r][:, k * P:(k + 1) * P], xn[:, r, k * P:(k + 1) * P], ident[:])
                    last.then_inc(turned, 1)
                    if wdt_dram is not None:
                        pe.wait_ge(hi_ok, n + 1)
                        pe.wait_ge(lo_ok, n + 1)
                        split3(pe, pd[r][:, 0:HEADS], lambda a, k: xh[:, r, a, k * P:(k + 1) * P],
                               lambda b, k: wdt[:, b, k, :], KD).then_inc(dt_mm, 1)


def step_phase(nc, S, dtr, alog_dram, par_dram, dat_dram):
    with ExitStack() as ctx:
        def sb(n, s, d=F32):
            return ctx.enter_context(nc.sbuf_tensor("st_" + n, s, d))

        N = NT * HEADS
        z = dtr[:].rearrange("p a h -> p (a h)")
        e, u, t1, t2, dt, a = (sb(n, [P, N]) for n in ("e", "u", "t1", "t2", "dt", "a"))
        al, an = sb("al", [P, HEADS]), sb("an", [P, HEADS])
        par = sb("par", [P, GROUPS, NT, 4, HPG])
        masks = sb("masks", [P, 4, P])
        dat = sb("dat", [HEADS, NT, P])
        pc = [ctx.enter_context(nc.psum_tensor(f"st_pc{i}", [P, 512], F32)) for i in range(6)]
        pt = [ctx.enter_context(nc.psum_tensor(f"st_pt{i}", [P, 512], F32)) for i in range(2)]
        ld, v, ac, mm, tr, dtc, out = (S("st_" + n) for n in ("ld", "v", "ac", "mm", "tr", "dtc", "out"))
        block = ctx.enter_context(nc.Block())

        def by_head(t):
            return t[:].rearrange("p (a g h) -> p a g h", a=NT, g=GROUPS)

        def par_of(i, lo=0, n=NT):
            return par[:, :, lo:lo + n, i, :].rearrange("p g a h -> p a g h")

        @block.sync
        def _(sp):
            sp.dma_start(al[:], alog_dram.partition_broadcast(P)).then_inc(ld, 16)
            sp.dma_start(masks[:], S.masks_dram).then_inc(ld, 16)
            sp.wait_ge(dtc, 5)
            sp.dma_start(dat_dram, dat[:].rearrange("h a t -> h (a t)")).then_inc(out, 16)
            sp.wait_ge(v, 13)
            sp.wait_ge(ac, 10)
            sp.dma_start(par_dram.rearrange("g p a k h -> p g (a k h)"),
                         par[:].rearrange("p g a k h -> p g (a k h)")).then_inc(out, 16)
            sp.wait_ge(out, 32)

        @block.vector
        def _(dve):
            dve.tensor_scalar(t1[:], z, -1.0, None, ALU.mult).then_inc(v, 1)
            dve.wait_ge(v, 1)
            dve.tensor_tensor(t1[:], t1[:], z, ALU.min).then_inc(v, 1)
            dve.wait_ge(ac, 1)
            dve.tensor_scalar(u[:], e[:], 1.0, None, ALU.add).then_inc(v, 1)
            dve.wait_ge(v, 3)
            dve.tensor_scalar(t2[:], u[:], -1.0, None, ALU.add).then_inc(v, 1)
            dve.wait_ge(v, 4)
            dve.tensor_tensor(t2[:], e[:], t2[:], ALU.subtract).then_inc(v, 1)
            dve.reciprocal(t1[:], u[:]).then_inc(v, 1)
            dve.wait_ge(v, 6)
            dve.tensor_tensor(t2[:], t2[:], t1[:], ALU.mult).then_inc(v, 1)
            dve.wait_ge(v, 7)
            dve.wait_ge(ac, 2)
            dve.tensor_tensor(t2[:], t2[:], dt[:], ALU.add).then_inc(v, 1)
            dve.wait_ge(v, 8)
            dve.scalar_tensor_tensor(out=dt[:], in0=z, scalar=0.0, in1=t2[:], op0=ALU.max, op1=ALU.add).then_inc(v, 1)
            dve.wait_ge(ac, 3)
            dve.tensor_scalar(al[:], an[:], -1.0, None, ALU.mult).then_inc(v, 1)
            dve.wait_ge(v, 10)
            dve.tensor_tensor(a[:].rearrange("p (a h) -> p a h", a=NT), dt[:].rearrange("p (a h) -> p a h", a=NT),
                              al[:].rearrange("p (o h) -> p o h", o=1).to_broadcast([P, NT, HEADS]), ALU.mult).then_inc(v, 1)
            dve.tensor_copy(par_of(DT_), by_head(dt)).then_inc(v, 1)
            for j in range(4):
                dve.wait_ge(tr, j + 1)
                dve.tensor_copy(dat[:, 4 * j:4 * j + 4, :].rearrange("h a t -> h (a t)"), pt[j % 2][0:HEADS, :]).then_inc(dtc, 1)
            dve.wait_ge(dtc, 4)
            dve.memset(dat[:, :, 0:1], 0.0).then_inc(dtc, 1)
            dve.wait_ge(ac, 6)
            dve.tensor_tensor(par_of(WDT_), by_head(t1), by_head(dt), ALU.mult).then_inc(v, 1)

        @block.scalar
        def _(act):
            act.wait_ge(v, 2)
            act.activation(e[:], t1[:], ACT.Exp).then_inc(ac, 1)
            act.wait_ge(v, 3)
            act.activation(dt[:], u[:], ACT.Ln).then_inc(ac, 1)
            act.wait_ge(ld, 32)
            act.activation(an[:], al[:], ACT.Exp).then_inc(ac, 1)
            act.wait_ge(v, 11)
            act.activation(e[:], a[:], ACT.Exp).then_inc(ac, 1)
            act.wait_ge(mm, 2)
            for h in range(2):
                act.activation(t1[:, h * 512:(h + 1) * 512], pc[h][:], ACT.Exp).then_inc(ac, 1)
            for i, kind in ((2, EXC_), (4, TOT_)):
                act.wait_ge(mm, i + 2)
                for h in range(2):
                    act.activation(par_of(kind, 8 * h, 8), pc[i + h][:].rearrange("p (a g h) -> p a g h", a=8, g=GROUPS),
                                   ACT.Exp).then_inc(ac, 1)

        @block.tensor
        def _(pe):
            pe.wait_ge(ld, 32)
            pe.wait_ge(v, 11)
            for i, m in ((0, 2), (2, 1), (4, 3)):
                for h in range(2):
                    pe.matmul(pc[i + h][:], masks[:, m, :], a[:, h * 512:(h + 1) * 512], start=True, stop=True).then_inc(mm, 1)
            pe.wait_ge(ac, 4)
            for j in range(4):
                if j >= 2:
                    pe.wait_ge(dtc, j - 1)
                for i in range(4):
                    last = pe.transpose(pt[j % 2][0:HEADS, i * P:(i + 1) * P],
                                        e[:, (4 * j + i) * HEADS:(4 * j + i + 1) * HEADS], masks[:, 0, :])
                last.then_inc(tr, 1)


IN_TILES = {0: [0, 1, 2], 1: [3, 4, 5], 2: [], 3: [], 4: [0, 1], 5: [2, 3], 6: [4, 5], 7: []}
GATES = {0: [0, 1], 1: [2], 2: [3, 4], 3: [5, 6], 4: [7], 5: [], 6: [], 7: []}
OW_SLOT, XW_SLOTS, GW_SLOTS = 1, (2, 3), (5, 6)


def ssm_phase(nc, S, xnt_dram, wx_dram, wg_dram, ow_dram, cp_dram, d_dram, par_dram, dat_dram, s_dram):
    with ExitStack() as ctx:
        def sb(n, s, d=F32):
            return ctx.enter_context(nc.sbuf_tensor("m_" + n, s, d))

        def ps(n):
            return ctx.enter_context(nc.psum_tensor("m_" + n, [P, 512], F32))

        def sem(n):
            return S("m_" + n)

        xn = sb("xn", [P, 2, KD, HT], F32R)
        wx = sb("wx", [P, 2, KD, XBC * P], F32R)
        wg = sb("wg", [P, 2, KD, 512], F32R)
        ow = sb("ow", [P, 2, KD, DM], F32R)
        raw = sb("raw", [P, 2, XBC * P])
        cp = sb("cp", [P, XBC, 5])
        par = sb("par", [P, 2, 4, 4, HPG])
        dpar = sb("dpar", [P, 2, HPG])
        cv = sb("cv", [P, 2, XBC, SEQ])
        sg = sb("sg", [P, 4, 512])
        dab = sb("dab", [P, 2, HPG * P])
        dec = sb("dec", [P, 2, HPG * P])
        eye8 = sb("eye8", [P, HPG, P])
        xs, dtx, xw, xd = (sb(n, [P, 2, 512]) for n in ("xs", "dtx", "xw", "xd"))
        bt = sb("bt", [P, 2, P])
        state = sb("state", [P, 512])
        t1 = sb("t1", [P, 512])
        y = sb("y", [P, 2, 512])
        junk = sb("junk", [P, 512])
        yt = sb("yt", [P, 2, KD * P], F32R)
        ss = sb("ss", [P, 2])
        ve = sb("ve", [P, 2])
        rs = sb("rs", [P, 2])
        half = sb("half", [P, 1])
        sacc = sb("sacc", [P, SLOTS, DM])
        ident = eye8[:, 0, :]

        p_in = [ps("p_in0"), ps("p_in1")]
        p_gate, p_turn, p_bg, p_yi, p_ye, p_ou = (ps(n) for n in ("p_gate", "p_turn", "p_bg", "p_yi", "p_ye", "p_ou"))

        eye_ld, xn_ld, cp_ld = sem("eye_ld"), sem("xn_ld"), sem("cp_ld")
        raw_ld = [sem(f"raw_ld{i}") for i in range(2)]
        raw_scaled, raw_hi, split_ok = sem("raw_scaled"), sem("raw_hi"), sem("split_ok")
        par_ld = [sem(f"par_ld{i}") for i in range(2)]
        dab_ld = [sem(f"dab_ld{i}") for i in range(2)]
        in_done, cev, ctap, silu_cv = sem("in_done"), sem("cev"), sem("ctap"), sem("silu_cv")
        a_done, xs_done, bt_done = sem("a_done"), sem("xs_done"), sem("bt_done")
        dtx_done, scan_done, m_done = sem("dtx_done"), sem("scan_done"), sem("m_done")
        xw_done, xd_done = sem("xw_done"), sem("xd_done")
        b_done, st_done, s_done = sem("b_done"), sem("st_done"), sem("s_done")
        t1_done, y0_done, y_done = sem("t1_done"), sem("y0_done"), sem("y_done")
        sq_done, ve_done, rs_done = sem("sq_done"), sem("ve_done"), sem("rs_done")
        g_done, sg_done, yn_done = sem("g_done"), sem("sg_done"), sem("yn_done")
        c_done, hi_done, lo_done, d_done = sem("c_done"), sem("hi_done"), sem("lo_done"), sem("d_done")
        sacc_done, sacc_zero, s_stored, half_ok = sem("sacc_done"), sem("sacc_zero"), sem("s_stored"), sem("half_ok")
        block = ctx.enter_context(nc.Block())

        GU, GQ, GP = SLOTS, 2, 12
        HU, HQ, HP = GROUPS * GU, GROUPS * GQ, GROUPS * GP

        def walk(eng, prologue, slot, drain):
            with eng.Fori(0, HALVES) as hf:
                prologue(hf)
                slot(hf, 0, 0, "first")
                with eng.Fori(0, GROUPS - 1) as g:
                    for s in range(1, SLOTS):
                        slot(hf, g, s, "")
                    slot(hf, g + 1, 0, "")
                for s in range(1, SLOTS):
                    slot(hf, GROUPS - 1, s, "last")
                drain(hf)

        def at(hf, g, s):
            return hf * HU + g * GU + s, hf * HQ + g * GQ + s // 4, hf * GROUPS + g

        def tiles_of(s, kind):
            return [] if kind == "last" and s >= 4 else IN_TILES[s]

        def has_next(s, kind):
            return not (kind == "last" and s == SLOTS - 1)

        def bc(ap, n):
            return ap.rearrange("p (a o) -> p a o", o=1).to_broadcast([P, ap.shape[1], n])

        def heads(ap):
            return ap.rearrange("p (h d) -> p h d", h=HPG)

        @block.sync
        def _(sp):
            sp.dma_start(eye8[:], S.eye8_dram).then_inc(eye_ld, 16)
            start_at_one(sp, s_stored)

            def load_dab(hf, g, s):
                sp.dma_start(dab[:, s % 2, :].rearrange("p (h t) -> p h t", h=HPG),
                             dat_dram[bass.ds(g * HPG, HPG), bass.ds(hf * HT + s * P, P)].partition_broadcast(P))\
                    .then_inc(dab_ld[s % 2], 16)

            def load_par(hf, g, b):
                sp.dma_start(par[:, b, :, :, :].rearrange("p a k h -> p (a k h)"),
                             par_dram[g, :, bass.ds(hf * SLOTS + 4 * b, 4), :, :].rearrange("p a k h -> p (a k h)"))\
                    .then_inc(par_ld[b], 16)
                sp.dma_start(dpar[:, b, :], d_dram[bass.ds(g * HPG, HPG)].partition_broadcast(P)).then_inc(par_ld[b], 16)

            def piece(it, i, src, free):
                plain_wait(sp, eye_ld, 16, split_ok, GP * it + free + 1)
                sp.dma_start(raw[:, i % 2, 0:src.shape[-1]], src).then_inc(raw_ld[i % 2], 16)

            def prologue(hf):
                u, q, it = at(hf, 0, 0)
                plain_wait(sp, eye_ld, 16, in_done, q * XBC + 1)
                sp.wait_ge(g_done, u + 1)
                for s in range(SLOTS):
                    sp.dma_start(xn[:, :, :, s * P:(s + 1) * P].bitcast(F32),
                                 xnt_dram[hf * SLOTS + s].rearrange("p a (k t) -> p a k t", k=KD)).then_inc(xn_ld, 16)
                for i in range(4):
                    piece(it, i, wx_dram[0, :, i, :], max(i - 1, 0))
                sp.wait_ge(ctap, 3 * XBC * q + 1)
                sp.dma_start(cp[:], cp_dram[0]).then_inc(cp_ld, 16)
                plain_wait(sp, eye_ld, 16, yn_done, u + 1)
                sp.wait_ge(scan_done, u + 1)
                load_par(hf, 0, 0)
                load_dab(hf, 0, 0)
                load_dab(hf, 0, 1)
                for i in range(4):
                    piece(it, 4 + i, wg_dram[0, :, i, :], 3 + i)

            def slot(hf, g, s, kind):
                u, q, it = at(hf, g, s)
                if not (kind == "last" and s >= SLOTS - 2):
                    plain_wait(sp, eye_ld, 16, scan_done, u + 2)
                    load_dab(hf, g + (s + 2) // SLOTS, (s + 2) % SLOTS)
                if s == 1 or (s == 5 and kind != "last"):
                    plain_wait(sp, eye_ld, 16, yn_done, u)
                    load_par(hf, g if s == 1 else g + 1, 1 if s == 1 else 0)
                if s == 2 and kind != "last":
                    plain_wait(sp, eye_ld, 16, ctap, 3 * XBC * (q + 2) + 1)
                    sp.dma_start(cp[:], cp_dram[g + 1]).then_inc(cp_ld, 16)
                if s in (0, 1):
                    for i in (2 * s, 2 * s + 1):
                        piece(it, 8 + i, ow_dram[g, :, i, :], 7 + i)
                if s in XW_SLOTS and kind != "last":
                    for i in (2 * (s - 2), 2 * (s - 2) + 1):
                        piece(it + 1, i, wx_dram[g + 1, :, i, :], i - 1)
                if s in GW_SLOTS and kind != "last":
                    for i in (2 * (s - 5), 2 * (s - 5) + 1):
                        piece(it + 1, 4 + i, wg_dram[g + 1, :, i, :], 3 + i)

            def drain(hf):
                plain_wait(sp, eye_ld, 16, sacc_done, hf * HU + HU + 1)
                sp.dma_start(s_dram[bass.ds(hf * SLOTS, SLOTS), :, :].rearrange("a p d -> p a d"), sacc[:]).then_inc(s_stored, 16)

            walk(sp, prologue, slot, drain)
            sp.wait_ge(s_stored, 16 * HALVES + 1)

        @block.gpsimd
        def _(pool):
            start_at_one(pool, raw_scaled, raw_hi, split_ok, xw_done, xd_done, st_done, y_done, ve_done, rs_done)
            pool.memset(half[:], -0.5).then_inc(half_ok, 1)
            pool.wait_ge(half_ok, 1)

            def split(it, i, dst, w, scaled=False):
                n, src = GP * it + i, raw[:, i % 2, 0:w]
                plain_wait(pool, half_ok, 1, raw_ld[i % 2], 16 * (GP // 2) * it + 16 * (i // 2 + 1))
                if scaled:
                    pool.tensor_scalar(src, src, raw[:, i % 2, w:w + 1], 1.0, ALU.mult, ALU.mult).then_inc(raw_scaled, 1)
                    plain_wait(pool, half_ok, 1, raw_scaled, 4 * it + i - 7 + 1)
                pool.tensor_copy(dst[:, 0, i % 4, :], src).then_inc(raw_hi, 1)
                pool.wait_ge(raw_hi, n + 2)
                pool.tensor_tensor(dst[:, 1, i % 4, :], src, dst[:, 0, i % 4, :].bitcast(F32), ALU.subtract).then_inc(split_ok, 1)

            def x_parts(u, it, s):
                b, c, r = s // 4, s % 4, s % 2
                if c == 0:
                    pool.wait_ge(par_ld[b], 32 * it + 32)
                pool.wait_ge(xs_done, u + 2)
                pool.tensor_tensor(heads(xw[:, r, :]), heads(xs[:, r, :]), bc(par[:, b, c, WDT_, :], HD), ALU.mult).then_inc(xw_done, 1)
                pool.tensor_tensor(heads(xd[:, r, :]), heads(xs[:, r, :]), bc(dpar[:, b, :], HD), ALU.mult).then_inc(xd_done, 1)

            def prologue(hf):
                u, q, it = at(hf, 0, 0)
                plain_wait(pool, half_ok, 1, in_done, XBC * q + 1)
                for i in range(4):
                    split(it, i, wx, XBC * P)
                plain_wait(pool, half_ok, 1, g_done, u + 1)
                for i in range(4, 8):
                    split(it, i, wg, 512)
                plain_wait(pool, half_ok, 1, s_stored, 16 * hf + 1)
                pool.memset(sacc[:], 0.0).then_inc(sacc_zero, 1)
                pool.wait_ge(b_done, u + 1)
                pool.wait_ge(y0_done, u + 1)
                x_parts(u, it, 0)

            def slot(hf, g, s, kind):
                u, q, it = at(hf, g, s)
                b, c, r = s // 4, s % 4, s % 2
                pool.wait_ge(b_done, u + 2)
                if c in (1, 2):
                    pool.wait_ge(s_done, 3 * q + c + 1)
                    pool.tensor_tensor(heads(state[:]), heads(state[:]), bc(par[:, b, c, TOT_, :], HD), ALU.mult).then_inc(st_done, 1)
                pool.wait_ge(y0_done, u + 2)
                if c > 0:
                    pool.wait_ge(t1_done, 3 * q + c + 1)
                    pool.tensor_tensor(y[:, r, :], y[:, r, :], t1[:], ALU.add).then_inc(y_done, 1)
                if has_next(s, kind):
                    x_parts(u + 1, it + (s + 1) // SLOTS, (s + 1) % SLOTS)
                plain_wait(pool, half_ok, 1, sq_done, u + 2)
                pool.tensor_scalar(ve[:, r:r + 1], ss[:, r:r + 1], 1.0 / 512, EPS, ALU.mult, ALU.add).then_inc(ve_done, 1)
                pool.wait_ge(ve_done, u + 2)
                pool.tensor_tensor(rs[:, r:r + 1], ve[:, r:r + 1], half[:], ALU.pow).then_inc(rs_done, 1)
                if s == OW_SLOT:
                    plain_wait(pool, half_ok, 1, d_done, u)
                    for i in range(8, 12):
                        split(it, i, ow, DM, True)
                if s in XW_SLOTS and kind != "last":
                    plain_wait(pool, half_ok, 1, in_done, XBC * (q + 2) + 1)
                    for i in (2 * (s - 2), 2 * (s - 2) + 1):
                        split(it + 1, i, wx, XBC * P)
                if s in GW_SLOTS and kind != "last":
                    plain_wait(pool, half_ok, 1, g_done, GU * (it + 1) + 1)
                    for i in (2 * (s - 5), 2 * (s - 5) + 1):
                        split(it + 1, 4 + i, wg, 512)

            walk(pool, prologue, slot, lambda hf: None)

        @block.vector
        def _(dve):
            start_at_one(dve, ctap, dtx_done, scan_done, m_done, s_done, t1_done, y0_done, yn_done, lo_done, sacc_done)

            def conv(q, j, b):
                m = XBC * q + j
                dve.wait_ge(cev, m + 2)
                for d in (1, 2, 3):
                    if d > 1:
                        dve.wait_ge(ctap, 3 * m + d)
                    dve.scalar_tensor_tensor(out=cv[:, b, j, d:SEQ], in0=p_in[j % 2][:, 0:SEQ - d],
                                             scalar=cp[:, j, 3 - d:4 - d], in1=cv[:, b, j, d:SEQ],
                                             op0=ALU.mult, op1=ALU.add).then_inc(ctap, 1)

            def scan(hf, g, s, free):
                r = s % 2
                dve.wait_ge(dab_ld[r], hf * (16 * HU // 2) + g * (16 * GU // 2) + 16 * (s // 2 + 1))
                dve.wait_ge(b_done, free + 1)
                dve.tensor_tensor_scan(out=dec[:, r, :], data0=dab[:, r, :], data1=eye8[:].rearrange("p h t -> p (h t)"),
                                       initial=0.0, op0=ALU.mult, op1=ALU.add).then_inc(scan_done, 1)

            def x_and_m(u, it, s):
                b, c, r = s // 4, s % 4, s % 2
                dve.wait_ge(xs_done, u + 2)
                if c == 0:
                    dve.wait_ge(par_ld[b], 32 * it + 32)
                dve.tensor_tensor(heads(dtx[:, r, :]), heads(p_turn[:]), bc(par[:, b, c, DT_, :], HD), ALU.mult).then_inc(dtx_done, 1)
                dve.wait_ge(bt_done, u + 2)
                dve.wait_ge(scan_done, u + 2)
                d = dec[:, r, :].rearrange("p (h t) -> p h t", h=HPG)
                dve.tensor_tensor(d, d, p_bg[:, P:2 * P].rearrange("p (o t) -> p o t", o=1).to_broadcast([P, HPG, P]),
                                  ALU.mult).then_inc(m_done, 1)

            def low_part(v):
                dve.wait_ge(c_done, v + 2)
                dve.wait_ge(hi_done, v + 2)
                dve.tensor_tensor(yt[:, 1, :], p_turn[:], yt[:, 0, :].bitcast(F32), ALU.subtract).then_inc(lo_done, 1)

            def add_out(v, s):
                dve.wait_ge(d_done, v + 2)
                dve.wait_ge(sacc_done, v + 1)
                dve.tensor_tensor(sacc[:, s, :], sacc[:, s, :], p_ou[:], ALU.add).then_inc(sacc_done, 1)

            def prologue(hf):
                u, q, it = at(hf, 0, 0)
                dve.wait_ge(eye_ld, 16)
                for j in range(XBC):
                    conv(q, j, 0)
                scan(hf, 0, 0, u)
                x_and_m(u, it, 0)

            def slot(hf, g, s, kind):
                u, q, it = at(hf, g, s)
                b, c, r = s // 4, s % 4, s % 2
                tiles = tiles_of(s, kind)
                for j in tiles[:1]:
                    conv(q + 1, j, 1 - b)
                if has_next(s, kind):
                    scan(hf, g + (s + 1) // SLOTS, (s + 1) % SLOTS, u)
                if kind != "first":
                    low_part(u - 1)
                dve.wait_ge(b_done, u + 2)
                dve.wait_ge(xd_done, u + 2)
                dve.wait_ge(c_done, (u if kind == "first" else u - 1) + 1)
                dve.tensor_tensor(y[:, r, :], p_yi[:], xd[:, r, :], ALU.add).then_inc(y0_done, 1)
                if c > 0:
                    dve.wait_ge(y_done, 3 * q + c)
                    dve.tensor_tensor(heads(t1[:]), heads(p_ye[:]), bc(par[:, b, c, EXC_, :], HD), ALU.mult).then_inc(t1_done, 1)
                if c == 0:
                    dve.tensor_copy(state[:], p_ou[:]).then_inc(s_done, 1)
                elif c < 3:
                    dve.wait_ge(st_done, 2 * q + c + 1)
                    dve.tensor_tensor(state[:], state[:], p_ou[:], ALU.add).then_inc(s_done, 1)
                for j in tiles[1:]:
                    conv(q + 1, j, 1 - b)
                if has_next(s, kind):
                    x_and_m(u + 1, it + (s + 1) // SLOTS, (s + 1) % SLOTS)
                dve.wait_ge(rs_done, u + 2)
                dve.wait_ge(sg_done, u + 2)
                dve.scalar_tensor_tensor(out=y[:, r, :], in0=y[:, r, :], scalar=rs[:, r:r + 1], in1=sg[:, s % 4, :],
                                         op0=ALU.mult, op1=ALU.mult).then_inc(yn_done, 1)
                if kind != "first":
                    add_out(u - 1, (s - 1) % SLOTS)
                else:
                    plain_wait(dve, eye_ld, 16, sacc_zero, hf + 1)

            def drain(hf):
                low_part(hf * HU + HU - 1)
                add_out(hf * HU + HU - 1, SLOTS - 1)

            walk(dve, prologue, slot, drain)

        @block.scalar
        def _(act):
            start_at_one(act, cev, silu_cv, xs_done, bt_done, sq_done, sg_done, hi_done)

            def evac(q, j, b, free):
                act.wait_ge(in_done, XBC * q + j + 2)
                act.wait_ge(b_done, free + 1)
                act.activation(cv[:, b, j, :], p_in[j % 2][:], ACT.Identity, bias=cp[:, j, 4:5], scale=cp[:, j, 3:4])\
                    .then_inc(cev, 1)

            def silu_conv(q, b):
                act.wait_ge(ctap, 3 * XBC * q + 3 * XBC + 1)
                act.activation(cv[:, b, :, :], cv[:, b, :, :], ACT.Silu).then_inc(silu_cv, 1)

            def tokens(u, s, free):
                r = s % 2
                act.wait_ge(a_done, u + 2)
                act.wait_ge(xw_done, free + 1)
                act.wait_ge(xd_done, free + 1)
                act.activation(xs[:, r, :], p_turn[:], ACT.Copy).then_inc(xs_done, 1)
                act.wait_ge(b_done, free + 1)
                act.activation(bt[:, r, :], p_bg[:, 0:P], ACT.Copy).then_inc(bt_done, 1)

            def high_part(v):
                act.wait_ge(c_done, v + 2)
                act.wait_ge(d_done, v + 1)
                act.activation(yt[:, 0, :], p_turn[:], ACT.Copy).then_inc(hi_done, 1)

            def prologue(hf):
                u, q, it = at(hf, 0, 0)
                act.wait_ge(cp_ld, 16 * it + 16)
                for j in range(XBC):
                    evac(q, j, 0, u)
                silu_conv(q, 0)
                tokens(u, 0, u)

            def slot(hf, g, s, kind):
                u, q, it = at(hf, g, s)
                b, c, r = s // 4, s % 4, s % 2
                tiles = tiles_of(s, kind)
                if tiles and s >= 4:
                    act.wait_ge(cp_ld, 16 * it + 32)
                for j in tiles[:1]:
                    evac(q + 1, j, 1 - b, u)
                if kind != "first":
                    high_part(u - 1)
                for j in tiles[1:]:
                    evac(q + 1, j, 1 - b, u)
                for w in GATES[s]:
                    act.wait_ge(g_done, GU * it + w + 2)
                    act.wait_ge(yn_done, GU * it + max(w - 3, 0) + 1)
                    act.activation(sg[:, w % 4, :], p_gate[:], ACT.Silu).then_inc(sg_done, 1)
                if has_next(s, kind):
                    tokens(u + 1, (s + 1) % SLOTS, u)
                if tiles and tiles[-1] == XBC - 1:
                    silu_conv(q + 1, 1 - b)
                if c > 0:
                    act.wait_ge(y_done, 3 * q + c + 1)
                else:
                    act.wait_ge(y0_done, u + 2)
                act.wait_ge(ve_done, (u if kind == "first" else u - 1) + 1)
                act.activation(junk[:], y[:, r, :], ACT.Square, accum_out=ss[:, r:r + 1]).then_inc(sq_done, 1)

            walk(act, prologue, slot, lambda hf: high_part(hf * HU + HU - 1))

        @block.tensor
        def _(pe):
            start_at_one(pe, in_done, a_done, b_done, g_done, c_done, d_done)

            def conv_in(q, it, j, free):
                b = q_parity[0]
                pe.wait_ge(split_ok, GP * it + 4 + 1)
                pe.wait_ge(ctap, free + 1)
                split3(pe, p_in[j % 2][:], lambda a, k: wx[:, a, k, j * P:(j + 1) * P],
                       lambda a, k: xn[:, a, k, b * SEQ:(b + 1) * SEQ], KD).then_inc(in_done, 1)

            def gate(it, w):
                pe.wait_ge(split_ok, GP * it + 8 + 1)
                pe.wait_ge(sg_done, GU * it + w + 1)
                split3(pe, p_gate[:], lambda a, k: xn[:, a, k, w * P:(w + 1) * P],
                       lambda a, k: wg[:, a, k, :], KD).then_inc(g_done, 1)

            def turn_in(u, q, s, turned):
                b, c = s // 4, s % 4
                ch = slice(c * P, (c + 1) * P)
                pe.wait_ge(silu_cv, q + 2)
                pe.wait_ge(hi_done, turned + 1)
                pe.wait_ge(lo_done, turned + 1)
                pe.wait_ge(xs_done, u + 1)
                pe.wait_ge(dtx_done, u + 1)
                for k in range(4):
                    pe.transpose(p_turn[:, k * P:(k + 1) * P], cv[:, b, k, ch], ident)
                pe.wait_ge(m_done, u + 1)
                pe.wait_ge(bt_done, u + 1)
                pe.transpose(p_bg[:, 0:P], cv[:, b, 4, ch], ident)
                pe.matmul(p_bg[:, P:2 * P], cv[:, b, 4, ch], cv[:, b, 5, ch], start=True, stop=True).then_inc(a_done, 1)

            def turn_out(v, s):
                pe.wait_ge(yn_done, v + 2)
                for k in range(KD):
                    last = pe.transpose(p_turn[:, k * P:(k + 1) * P], y[:, s % 2, k * P:(k + 1) * P], ident)
                last.then_inc(c_done, 1)

            def project(v, it):
                pe.wait_ge(hi_done, v + 2)
                pe.wait_ge(lo_done, v + 2)
                pe.wait_ge(split_ok, GP * it + 12 + 1)
                split3(pe, p_ou[:], lambda a, k: yt[:, a, k * P:(k + 1) * P], lambda a, k: ow[:, a, k, :], KD).then_inc(d_done, 1)

            q_parity = [0]

            def prologue(hf):
                u, q, it = at(hf, 0, 0)
                pe.wait_ge(eye_ld, 16)
                pe.wait_ge(xn_ld, 16 * SLOTS * hf + 16 * SLOTS)
                q_parity[0] = 0
                for j in range(XBC):
                    conv_in(q, it, j, 3 * (XBC * q + j - 1) if j >= 2 else 3 * XBC * q)
                turn_in(u, q, 0, u)

            def slot(hf, g, s, kind):
                u, q, it = at(hf, g, s)
                b, c, r = s // 4, s % 4, s % 2
                tiles = tiles_of(s, kind)
                q_parity[0] = 1 - b
                for j in tiles[:1]:
                    conv_in(q + 1, it + b, j, 3 * (XBC * (q + 1) + j - 1))
                if kind != "first":
                    pe.wait_ge(xs_done, u + 2)
                    pe.wait_ge(dtx_done, u + 2)
                    turn_out(u - 1, (s - 1) % SLOTS)
                pe.wait_ge(m_done, u + 2)
                pe.wait_ge(dtx_done, u + 2)
                pe.wait_ge(y0_done, u + 1)
                for h in range(HPG):
                    last = pe.matmul(p_yi[:, h * HD:(h + 1) * HD], dec[:, r, h * P:(h + 1) * P], dtx[:, r, h * HD:(h + 1) * HD],
                                     start=True, stop=True)
                if c > 0:
                    pe.wait_ge(s_done, 3 * q + c + 1)
                    pe.wait_ge(t1_done, 3 * q + c)
                    last = pe.matmul(p_ye[:], cv[:, b, 5, c * P:(c + 1) * P], state[:], start=True, stop=True)
                if c < 3:
                    pe.wait_ge(bt_done, u + 2)
                    pe.wait_ge(xw_done, u + 2)
                    pe.wait_ge(sacc_done, (u if kind == "first" else u - 1) + 1)
                    last = pe.matmul(p_ou[:], bt[:, r, :], xw[:, r, :], start=True, stop=True)
                last.then_inc(b_done, 1)
                for j in tiles[1:]:
                    conv_in(q + 1, it + b, j, 3 * (XBC * (q + 1) + j - 1))
                for w in GATES[s]:
                    gate(it, w)
                if has_next(s, kind):
                    turn_in(u + 1, hf * HQ + g * GQ + (s + 1) // 4, (s + 1) % SLOTS, u if kind != "first" else u)
                if kind != "first":
                    pe.wait_ge(s_done, 3 * q + min(c + 1, 3) + 1)
                    pe.wait_ge(sacc_done, u)
                    project(u - 1, it - (1 if s == 0 else 0))

            def drain(hf):
                v = hf * HU + HU - 1
                turn_out(v, SLOTS - 1)
                pe.wait_ge(sacc_done, v + 1)
                project(v, hf * GROUPS + GROUPS - 1)

            walk(pe, prologue, slot, drain)


def nf4_phase(nc, S, weights):
    with ExitStack() as ctx:
        nb = weights[0][0].shape[1] // 2
        pieces = [(src[:, h * nb:(h + 1) * nb, :], dst[:, h * nb:(h + 1) * nb, :]) for src, dst in weights for h in range(2)]

        def sb(n, s, d=F32):
            return ctx.enter_context(nc.sbuf_tensor("q_" + n, s, d))

        w = sb("w", [P, 2, nb, BLK])
        norm = sb("norm", [P, nb, BLK])
        above = sb("above", [P, 2, nb, BLK])
        acc = sb("acc", [P, 2, nb, BLK])
        amax, safe, inv = (sb(n, [P, nb]) for n in ("amax", "safe", "inv"))
        ld = [S(f"q_ld{i}") for i in range(2)]
        st = [S(f"q_st{i}") for i in range(2)]
        seq, done = S("q_seq"), S("q_done")
        block = ctx.enter_context(nc.Block())
        code = np.array(NF4, np.float32)
        bound = (code[:-1] + code[1:]) * np.float32(0.5)

        @block.sync
        def _(sp):
            for n, (src, dst) in enumerate(pieces):
                if n >= 2:
                    sp.wait_ge(done, n - 1)
                sp.dma_start(w[:, n % 2, :, :], src).then_inc(ld[n % 2], 16)
                if n >= 1:
                    sp.wait_ge(done, n)
                    sp.dma_start(pieces[n - 1][1], acc[:, (n - 1) % 2, :, :]).then_inc(st[(n - 1) % 2], 16)
            sp.wait_ge(done, len(pieces))
            sp.dma_start(pieces[-1][1], acc[:, (len(pieces) - 1) % 2, :, :]).then_inc(st[(len(pieces) - 1) % 2], 16)
            for i in range(2):
                sp.wait_ge(st[i], 16 * len(pieces) // 2)

        @block.vector
        def _(dve):
            k = 0
            for n in range(len(pieces)):
                x, a = w[:, n % 2, :, :], acc[:, n % 2, :, :]
                dve.wait_ge(ld[n % 2], 16 * (n // 2 + 1))
                if n >= 1:
                    dve.wait_ge(done, n)
                dve.tensor_reduce(amax[:], x, AX_X, ALU.max, apply_absolute_value=True).then_inc(seq, 1)
                dve.wait_ge(seq, k + 1)
                dve.scalar_tensor_tensor(out=safe[:], in0=amax[:], scalar=0.0, in1=amax[:], op0=ALU.is_equal, op1=ALU.add).then_inc(seq, 1)
                dve.wait_ge(seq, k + 2)
                dve.reciprocal(inv[:], safe[:]).then_inc(seq, 1)
                dve.wait_ge(seq, k + 3)
                dve.tensor_tensor(norm[:], x, inv[:].rearrange("p (b o) -> p b o", o=1).to_broadcast([P, nb, BLK]), ALU.mult).then_inc(seq, 1)
                k += 4
                if n >= 2:
                    dve.wait_ge(st[n % 2], 16 * (n // 2))
                dve.wait_ge(seq, k)
                dve.tensor_scalar(a, norm[:], float(bound[0]), float(code[1] - code[0]), ALU.is_gt, ALU.mult).then_inc(seq, 1)
                k += 1
                for j in range(1, len(bound)):
                    m = above[:, j % 2, :, :]
                    dve.tensor_scalar(m, norm[:], float(bound[j]), float(code[j + 1] - code[j]), ALU.is_gt, ALU.mult).then_inc(seq, 1)
                    dve.wait_ge(seq, k + 1)
                    dve.tensor_tensor(a, a, m, ALU.add).then_inc(seq, 1)
                    k += 2
                dve.wait_ge(seq, k)
                dve.tensor_scalar(a, a, float(code[0]), None, ALU.add).then_inc(seq, 1)
                dve.wait_ge(seq, k + 1)
                dve.tensor_tensor(a, a, amax[:].rearrange("p (b o) -> p b o", o=1).to_broadcast([P, nb, BLK]), ALU.mult).then_inc(done, 1)
                k += 1


def ffn_phase(nc, S, tag, xnt_dram, hidden, weights, x_dram, s_dram, out_dram, turn, experts=None):
    gate_dram, up_dram, down_dram = weights
    nf = -(-hidden // P)
    width = [min(P, hidden - f * P) for f in range(nf)]
    with ExitStack() as ctx:
        def sb(n, s, d=F32):
            return ctx.enter_context(nc.sbuf_tensor(tag + n, s, d))

        def sem(n):
            return S(tag + n)

        wg = sb("wg", [P, 2, KD, nf * P], F32R)
        wu = sb("wu", [P, 2, KD, nf * P], F32R)
        wd = sb("wd", [P, 2, nf, DM], F32R)
        raw = sb("raw", [P, 2, max(DM, 0 if turn else hidden)])
        xn = sb("xn", [P, 2, 2, KD, SEQ], F32R)
        gs = sb("gs", [P, 2, SEQ])
        h = sb("h", [P, 2, SEQ])
        ht = sb("ht", [P, 2, 2, SEQ], F32R)
        ge, xi, xo = (sb(n, [P, 2, DM]) for n in ("ge", "xi", "xo"))
        si = sb("si", [P, 2, s_dram.shape[-1]])
        ident = sb("ident", [P, P])
        bank = [ctx.enter_context(nc.psum_tensor(f"{tag}bank{i}", [P, 512], F32)) for i in range(8)]
        pg, pu, pw, po = bank[0:2], bank[2], bank[3], bank[4:8]
        if experts is not None:
            rep = sb("rep", [EXPERTS, hidden])
            wt = sb("wt", [EXPERTS, 2, SEQ])
        raw_ld = [sem(f"raw_ld{i}") for i in range(2)]
        id_ld, turned, w_hi, w_lo = sem("id_ld"), sem("turned"), sem("w_hi"), sem("w_lo")
        xn_ld = [sem(f"xn_ld{i}") for i in range(2)]
        in_ld = [sem(f"in_ld{i}") for i in range(2)]
        stored = [sem(f"stored{i}") for i in range(2)]
        g_done, u_done, w_done, silu_ok, h_ok = sem("g_done"), sem("u_done"), sem("w_done"), sem("silu_ok"), sem("h_ok")
        hw_ok, hi_ok, lo_ok, d_done, o_done = sem("hw_ok"), sem("hi_ok"), sem("lo_ok"), sem("d_done"), sem("o_done")
        ge_ok, sg_ok, res_ok = sem("ge_ok"), sem("sg_ok"), sem("res_ok")
        block = ctx.enter_context(nc.Block())

        LX = 16 * 4 * (2 if experts is not None else 1)
        pieces = []
        if turn:
            for src, dst in ((gate_dram, wg), (up_dram, wu)):
                for f, w in enumerate(width):
                    pieces.append((src[f * P:f * P + w, :], w, DM, dst[:, :, :, f * P:f * P + w]))
            for f, w in enumerate(width):
                pieces.append((down_dram[:, f * P:f * P + w].rearrange("(k p) n -> p k n", p=P), P, KD * w, wd[0:w, :, f, :]))
        else:
            for src, dst in ((gate_dram, wg), (up_dram, wu)):
                for k in range(KD):
                    pieces.append((src[:, k, :], P, hidden, dst[:, :, k, 0:hidden]))
            for f in range(nf):
                pieces.append((down_dram[:, f, :], P, DM, wd[:, :, f, :]))

        def turned_view(n):
            _, rows, cols, _ = pieces[n]
            if n < 2 * nf:
                return pg[n % 2][:].rearrange("p (k n) -> p k n", k=KD)[:, :, 0:rows]
            return pg[n % 2][0:cols // KD, :]

        @block.sync
        def _(sp):
            sp.dma_start(ident[:], S.ident_dram).then_inc(id_ld, 16)
            start_at_one(sp, *xn_ld, *in_ld, *stored)
            if experts is not None:
                sp.dma_start(rep[:], S.rep_dram).then_inc(id_ld, 16)

            def load_xn(tile, r):
                for c in range(4):
                    sp.dma_start(xn[:, r, :, :, c * P:(c + 1) * P].bitcast(F32),
                                 xnt_dram[tile + c].rearrange("p a (k t) -> p a k t", k=KD)).then_inc(xn_ld[r], 16)
                    if experts is not None:
                        sp.dma_start(wt[:, r, c * P:(c + 1) * P], experts[tile + c]).then_inc(xn_ld[r], 16)

            load_xn(0, 0)
            for n, (src, rows, cols, _) in enumerate(pieces):
                if n >= 2:
                    sp.wait_ge(w_lo, n - 1)
                dst = raw[0:rows, n % 2, 0:cols]
                if turn and n >= 2 * nf:
                    dst = dst.rearrange("p (k n) -> p k n", k=KD)
                sp.dma_start(dst, src).then_inc(raw_ld[n % 2], 16)
            load_xn(4, 1)
            with sp.Fori(0, 2) as i:
                for r in range(2):
                    t0 = 8 * i + 4 * r
                    for c in range(4):
                        plain_wait(sp, id_ld, 16, res_ok, t0 + max(c - 1, 0) + 1)
                        sp.dma_start(xi[:, c % 2, :], x_dram[t0 + c]).then_inc(in_ld[c % 2], 16)
                        sp.dma_start(si[:, c % 2, :], s_dram[t0 + c]).then_inc(in_ld[c % 2], 16)
                        if c >= 1:
                            plain_wait(sp, id_ld, 16, res_ok, t0 + c + 1)
                            sp.dma_start(out_dram[t0 + c - 1], xo[:, (c - 1) % 2, :]).then_inc(stored[(c - 1) % 2], 16)
                    plain_wait(sp, id_ld, 16, res_ok, t0 + 4 + 1)
                    sp.dma_start(out_dram[t0 + 3], xo[:, 1, :]).then_inc(stored[1], 16)
                    load_xn(8 - 8 * i + 4 * r, r)
            for r in range(2):
                sp.wait_ge(stored[r], 16 * NT // 2 + 1)
                sp.wait_ge(xn_ld[r], 3 * LX + 1)

        @block.scalar
        def _(act):
            start_at_one(act, silu_ok, hi_ok, ge_ok)
            for n, (_, rows, _, dst) in enumerate(pieces):
                if turn:
                    act.wait_ge(turned, n + 1)
                    act.activation(dst[:, 0], turned_view(n), ACT.Copy).then_inc(w_hi, 1)
                else:
                    act.wait_ge(raw_ld[n % 2], 16 * (n // 2 + 1))
                    act.activation(dst[:, 0], raw[0:rows, n % 2, 0:dst.shape[-1]], ACT.Copy).then_inc(w_hi, 1)

            def high(n, f):
                act.wait_ge(hw_ok if experts is not None else h_ok, n + 1 + 1)
                act.wait_ge(d_done, n - min(f, 1) + 1)
                act.activation(ht[0:width[f], f % 2, 0, :], h[0:width[f], f % 2, :], ACT.Copy).then_inc(hi_ok, 1)

            with act.Fori(0, 2) as i:
                for r in range(2):
                    n0 = (2 * i + r) * nf
                    for f in range(nf):
                        act.wait_ge(g_done, n0 + f + 1 + 1)
                        act.wait_ge(h_ok, n0 + f - min(f, 1) + 1)
                        act.activation(gs[0:width[f], f % 2, :], pg[f % 2][0:width[f], :], ACT.Silu).then_inc(silu_ok, 1)
                        if f >= 1:
                            high(n0 + f - 1, f - 1)
                    high(n0 + nf - 1, nf - 1)
                    for c in range(4):
                        act.wait_ge(d_done, n0 + nf + 1)
                        act.wait_ge(res_ok, 8 * i + 4 * r + max(c - 1, 0) + 1)
                        act.activation(ge[:, c % 2, :], po[c][:], ACT.Silu).then_inc(ge_ok, 1)

        @block.vector
        def _(dve):
            start_at_one(dve, h_ok, hw_ok, lo_ok, sg_ok, res_ok)
            for n, (_, rows, _, dst) in enumerate(pieces):
                dve.wait_ge(w_hi, n + 1)
                src = turned_view(n) if turn else raw[0:rows, n % 2, 0:dst.shape[-1]]
                dve.tensor_tensor(dst[:, 1], src, dst[:, 0].bitcast(F32), ALU.subtract).then_inc(w_lo, 1)

            def low(n, f):
                dve.wait_ge(hi_ok, n + 1 + 1)
                w = width[f]
                dve.tensor_tensor(ht[0:w, f % 2, 1, :], h[0:w, f % 2, :], ht[0:w, f % 2, 0, :].bitcast(F32), ALU.subtract)\
                    .then_inc(lo_ok, 1)

            with dve.Fori(0, 2) as i:
                for r in range(2):
                    n0 = (2 * i + r) * nf
                    for f in range(nf):
                        w, n = width[f], n0 + f
                        dve.wait_ge(silu_ok, n + 1 + 1)
                        dve.wait_ge(u_done, n + 1 + 1)
                        dve.wait_ge(lo_ok, n - min(f, 1) + 1)
                        dve.tensor_tensor(h[0:w, f % 2, :], pu[0:w, :], gs[0:w, f % 2, :], ALU.mult).then_inc(h_ok, 1)
                        if experts is not None:
                            dve.wait_ge(w_done, n + 1 + 1)
                            dve.wait_ge(h_ok, n + 1 + 1)
                            dve.tensor_tensor(h[0:w, f % 2, :], pw[0:w, :], h[0:w, f % 2, :], ALU.mult).then_inc(hw_ok, 1)
                        if f >= 1:
                            low(n - 1, f - 1)
                    low(n0 + nf - 1, nf - 1)
                    for c in range(4):
                        t = 8 * i + 4 * r + c
                        dve.wait_ge(ge_ok, t + 1 + 1)
                        dve.wait_ge(in_ld[c % 2], 32 * (4 * i + 2 * r + c // 2 + 1) + 1)
                        g3, s3 = ge[:, c % 2, :], si[:, c % 2, :]
                        if experts is not None:
                            g3 = g3.rearrange("p (d h) -> p d h", d=QK)
                            s3 = s3.rearrange("p (d o) -> p d o", o=1).to_broadcast([P, QK, DM // QK])
                        dve.tensor_tensor(g3, g3, s3, ALU.mult).then_inc(sg_ok, 1)
                        dve.wait_ge(sg_ok, t + 1 + 1)
                        dve.wait_ge(stored[c % 2], 16 * (4 * i + 2 * r + c // 2) + 1)
                        dve.tensor_tensor(xo[:, c % 2, :], ge[:, c % 2, :], xi[:, c % 2, :], ALU.add).then_inc(res_ok, 1)

        @block.tensor
        def _(pe):
            start_at_one(pe, g_done, u_done, w_done, d_done)
            pe.wait_ge(id_ld, 32 if experts is not None else 16)
            if turn:
                for n, (_, rows, cols, _) in enumerate(pieces):
                    pe.wait_ge(raw_ld[n % 2], 16 * (n // 2 + 1))
                    if n >= 2:
                        pe.wait_ge(w_lo, n - 1)
                    for k in range(KD):
                        if n < 2 * nf:
                            last = pe.transpose(pg[n % 2][:, k * P:k * P + rows], raw[0:rows, n % 2, k * P:(k + 1) * P], ident[0:rows, 0:rows])
                        else:
                            w = cols // KD
                            last = pe.transpose(pg[n % 2][0:w, k * P:(k + 1) * P], raw[:, n % 2, k * w:(k + 1) * w], ident[:])
                    last.then_inc(turned, 1)
            pe.wait_ge(w_lo, len(pieces))

            def hidden_in(i, r, f):
                w, n = width[f], (2 * i + r) * nf + f
                cols = slice(f * P, f * P + w)
                pe.wait_ge(silu_ok, n - min(f, 1) + 1)
                split3(pe, pg[f % 2][0:w, :], lambda a, k: wg[:, a, k, cols], lambda a, k: xn[:, r, a, k, :], KD).then_inc(g_done, 1)
                pe.wait_ge(h_ok, n + 1)
                split3(pe, pu[0:w, :], lambda a, k: wu[:, a, k, cols], lambda a, k: xn[:, r, a, k, :], KD).then_inc(u_done, 1)
                if experts is not None:
                    pe.wait_ge(hw_ok, n + 1)
                    pe.matmul(pw[0:w, :], rep[:, cols], wt[:, r, :], start=True, stop=True).then_inc(w_done, 1)

            def hidden_out(i, r, f):
                w, n = width[f], (2 * i + r) * nf + f
                pe.wait_ge(hi_ok, n + 1 + 1)
                pe.wait_ge(lo_ok, n + 1 + 1)
                if f == 0:
                    pe.wait_ge(ge_ok, 8 * i + 4 * r + 1)
                for c in range(4):
                    for m, (a, b) in enumerate(((0, 0), (0, 1), (1, 0))):
                        last = pe.matmul(po[c][:], ht[0:w, f % 2, a, c * P:(c + 1) * P], wd[0:w, b, f, :],
                                         start=(f == 0 and m == 0), stop=(f == nf - 1 and m == 2))
                last.then_inc(d_done, 1)

            with pe.Fori(0, 2) as i:
                for r in range(2):
                    pe.wait_ge(xn_ld[r], LX * i + LX + 1)
                    hidden_in(i, r, 0)
                    for f in range(1, nf):
                        hidden_in(i, r, f)
                        hidden_out(i, r, f - 1)
                    hidden_out(i, r, nf - 1)


def attention_phase(nc, S, xnt_dram, wq_dram, wkv_dram, b_dram, o_dram, wt_dram):
    with ExitStack() as ctx:
        def sb(n, s, d=F32):
            return ctx.enter_context(nc.sbuf_tensor("a_" + n, s, d))

        wq = sb("wq", [P, KD, QK, DM // QK])
        w = sb("w", [P, KD, NQ])
        wr = sb("wr", [P, 2, KD, NQ], F32R)
        bq = sb("bq", [P, QK, DM // QK])
        bias = sb("bias", [P, NQ])
        xh = sb("xh", [P, 2, 2, DM], F32R)
        qk = sb("qk", [P, NT, NQ])
        sc = sb("sc", [P, NT, QK, QK])
        mx, sm, so = (sb(n, [P, NT, QK]) for n in ("mx", "sm", "so"))
        pr, one, eq, p2 = (sb(n, [P, NT, EXPERTS]) for n in ("pr", "one", "eq", "p2"))
        top = sb("top", [P, NT])
        desc = sb("desc", [P, EXPERTS])
        ident = sb("ident", [P, P])
        wt = sb("wt", [EXPERTS, NT, P])
        pq = [ctx.enter_context(nc.psum_tensor(f"a_pq{i}", [P, 512], F32)) for i in range(2)]
        pt = [ctx.enter_context(nc.psum_tensor(f"a_pt{i}", [P, 512], F32)) for i in range(4)]
        ld, xh_ld = S("a_ld"), [S(f"a_xh_ld{i}") for i in range(2)]
        prep, mm, qk_ok, seq, ac, tr, wt_ok, out = (S("a_" + n) for n in ("prep", "mm", "qk_ok", "seq", "ac", "tr", "wt_ok", "out"))
        block = ctx.enter_context(nc.Block())

        @block.sync
        def _(sp):
            sp.dma_start(wq[:].rearrange("p k d h -> p k (d h)"), wq_dram).then_inc(ld, 16)
            sp.dma_start(w[:, :, QK:NQ], wkv_dram).then_inc(ld, 16)
            sp.dma_start(bq[:].rearrange("p d h -> p (d h)"), b_dram[0].partition_broadcast(P)).then_inc(ld, 16)
            sp.dma_start(bias[:, QK:2 * QK], b_dram[1].partition_broadcast(P)).then_inc(ld, 16)
            sp.dma_start(bias[:, 2 * QK:3 * QK], b_dram[2].partition_broadcast(P)).then_inc(ld, 16)
            sp.dma_start(desc[:], S.desc_dram).then_inc(ld, 16)
            sp.dma_start(ident[:], S.ident_dram).then_inc(ld, 16)
            for n in range(NT):
                if n >= 2:
                    sp.wait_ge(mm, n - 1)
                sp.dma_start(xh[:, n % 2, :, :].bitcast(F32), xnt_dram[n]).then_inc(xh_ld[n % 2], 16)
            sp.wait_ge(seq, O_READY)
            sp.dma_start(o_dram.rearrange("a p d -> p a d"), so[:]).then_inc(out, 16)
            sp.wait_ge(wt_ok, 4)
            sp.dma_start(wt_dram.rearrange("a e t -> e a t"), wt[:]).then_inc(out, 16)
            sp.wait_ge(out, 32)

        def pair(ap):
            return ap.rearrange("p a (d o) -> p a d o", o=1).to_broadcast([P, NT, QK, QK])

        def along(ap):
            return ap.rearrange("p a (o e) -> p a o e", o=1).to_broadcast([P, NT, QK, QK])

        def per_tile(ap):
            return ap.rearrange("p (a o) -> p a o", o=1).to_broadcast([P, NT, EXPERTS])

        @block.vector
        def _(dve):
            dve.wait_ge(ld, 16 * 7)
            dve.tensor_reduce(w[:, :, 0:QK], wq[:], AX_X, ALU.add).then_inc(prep, 1)
            dve.tensor_reduce(bias[:, 0:QK], bq[:], AX_X, ALU.add).then_inc(prep, 1)
            dve.memset(bias[:, 3 * QK:NQ], 0.0).then_inc(prep, 1)
            dve.wait_ge(prep, 3)
            dve.tensor_copy(wr[:, 0], w[:]).then_inc(prep, 1)
            dve.wait_ge(prep, 4)
            dve.tensor_tensor(wr[:, 1], w[:], wr[:, 0].bitcast(F32), ALU.subtract).then_inc(prep, 1)
            for n in range(NT):
                dve.wait_ge(mm, n + 1)
                dve.tensor_tensor(qk[:, n, :], pq[n % 2][:, 0:NQ], bias[:], ALU.add).then_inc(qk_ok, 1)
            dve.wait_ge(qk_ok, NT)
            q, k, v, lg = (qk[:, :, i * QK:(i + 1) * QK] for i in range(4))
            dve.tensor_tensor(sc[:], pair(q), along(k), ALU.mult).then_inc(seq, 1)
            dve.wait_ge(seq, 1)
            dve.tensor_reduce(mx[:], sc[:], AX_X, ALU.max).then_inc(seq, 1)
            dve.wait_ge(seq, 2)
            dve.tensor_tensor(sc[:], sc[:], pair(mx[:]), ALU.subtract).then_inc(seq, 1)
            dve.tensor_reduce(top[:], lg, AX_X, ALU.max).then_inc(seq, 1)
            dve.wait_ge(seq, 4)
            dve.tensor_tensor(pr[:], lg, per_tile(top[:]), ALU.subtract).then_inc(seq, 1)
            dve.wait_ge(ac, 1)
            dve.tensor_reduce(sm[:], sc[:], AX_X, ALU.add).then_inc(seq, 1)
            dve.wait_ge(seq, 6)
            dve.tensor_tensor(sc[:], sc[:], along(v), ALU.mult).then_inc(seq, 1)
            dve.wait_ge(seq, 7)
            dve.tensor_reduce(so[:], sc[:], AX_X, ALU.add).then_inc(seq, 1)
            dve.reciprocal(mx[:], sm[:]).then_inc(seq, 1)
            dve.wait_ge(seq, 9)
            dve.tensor_tensor(so[:], so[:], mx[:], ALU.mult).then_inc(seq, 1)
            dve.wait_ge(ac, 2)
            dve.tensor_reduce(top[:], pr[:], AX_X, ALU.add).then_inc(seq, 1)
            dve.wait_ge(seq, 11)
            dve.reciprocal(top[:], top[:]).then_inc(seq, 1)
            dve.wait_ge(seq, 12)
            dve.tensor_tensor(pr[:], pr[:], per_tile(top[:]), ALU.mult).then_inc(seq, 1)
            n = 13
            first = desc[:].rearrange("p (o e) -> p o e", o=1).to_broadcast([P, NT, EXPERTS])
            for rank, (left, mark) in enumerate(((pr, one), (p2, eq))):
                dve.wait_ge(seq, n)
                dve.tensor_reduce(top[:], left[:], AX_X, ALU.max).then_inc(seq, 1)
                dve.wait_ge(seq, n + 1)
                dve.tensor_tensor(mark[:], left[:], per_tile(top[:]), ALU.is_ge).then_inc(seq, 1)
                dve.wait_ge(seq, n + 2)
                dve.tensor_tensor(mark[:], mark[:], first, ALU.mult).then_inc(seq, 1)
                dve.wait_ge(seq, n + 3)
                dve.tensor_reduce(top[:], mark[:], AX_X, ALU.max).then_inc(seq, 1)
                dve.wait_ge(seq, n + 4)
                dve.tensor_tensor(mark[:], mark[:], per_tile(top[:]), ALU.is_equal).then_inc(seq, 1)
                n += 5
                if rank == 0:
                    dve.wait_ge(seq, n)
                    dve.scalar_tensor_tensor(out=p2[:], in0=one[:], scalar=-4.0, in1=pr[:], op0=ALU.mult, op1=ALU.add).then_inc(seq, 1)
                    n += 1
            dve.wait_ge(seq, n)
            dve.tensor_tensor(one[:], one[:], eq[:], ALU.add).then_inc(seq, 1)
            dve.wait_ge(seq, n + 1)
            dve.tensor_tensor(pr[:], pr[:], one[:], ALU.mult).then_inc(seq, 1)
            dve.wait_ge(seq, n + 2)
            dve.tensor_reduce(top[:], pr[:], AX_X, ALU.add).then_inc(seq, 1)
            dve.wait_ge(seq, n + 3)
            dve.reciprocal(top[:], top[:]).then_inc(seq, 1)
            dve.wait_ge(seq, n + 4)
            dve.tensor_tensor(pr[:], pr[:], per_tile(top[:]), ALU.mult).then_inc(seq, 1)
            assert n + 5 == W_READY
            for j in range(4):
                dve.wait_ge(tr, j + 1)
                dve.tensor_copy(wt[:, 4 * j:4 * j + 4, :].rearrange("e a t -> e (a t)"), pt[j][0:EXPERTS, :]).then_inc(wt_ok, 1)

        @block.scalar
        def _(act):
            act.wait_ge(seq, 3)
            act.activation(sc[:], sc[:], ACT.Exp, scale=float(QK) ** -0.5).then_inc(ac, 1)
            act.wait_ge(seq, 5)
            act.activation(pr[:], pr[:], ACT.Exp).then_inc(ac, 1)

        @block.tensor
        def _(pe):
            pe.wait_ge(prep, 5)
            for n in range(NT):
                pe.wait_ge(xh_ld[n % 2], 16 * (n // 2 + 1))
                if n >= 2:
                    pe.wait_ge(qk_ok, n - 1)
                split3(pe, pq[n % 2][:, 0:NQ], lambda a, k: xh[:, n % 2, a, k * P:(k + 1) * P],
                       lambda a, k: wr[:, a, k, :], KD).then_inc(mm, 1)
            pe.wait_ge(seq, W_READY)
            for j in range(4):
                for c in range(4):
                    last = pe.transpose(pt[j][0:EXPERTS, c * P:(c + 1) * P], pr[:, 4 * j + c, :], ident[:])
                last.then_inc(tr, 1)


O_READY, W_READY = 10, 29



_OUTS = [((4, 512, 512), 'float32')]


class Scope:

    def __init__(self, nc, ctx):
        self.nc, self.ctx = nc, ctx

    def __call__(self, name):
        return self.ctx.enter_context(self.nc.semaphore(name))


def program(nc, ins, out):
    with ExitStack() as ctx:
        S = Scope(nc, ctx)
        S.ident_dram, S.masks_dram, S.eye8_dram = ins["ident"], ins["masks"], ins["eye8"]
        S.desc_dram, S.rep_dram = ins["desc"], ins["rep"]

        def dram(n, s, d=F32):
            return nc.dram_tensor(n, s, d, kind="Internal").ap()

        xnt = dram("xnt", [NT, P, 2, DM])
        par = dram("par", [GROUPS, P, NT, 4, HPG])
        dat = dram("dat", [HEADS, T])
        with nc.sbuf_tensor("dtr", [P, NT, HEADS], F32) as dtr:
            norm_phase(nc, S, ins["x"], xnt, "n0_", ins["wdt"], ins["dt_bias"], dtr)
            step_phase(nc, S, dtr, ins["A_log"], par, dat)
        x0 = ins["x"].rearrange("(a p) d -> a p d", p=P)
        s0, x1, xnt1 = dram("s0", [NT, P, DM]), dram("x1", [NT, P, DM]), dram("xnt1", [NT, P, 2, DM])
        ssm_phase(nc, S, xnt, ins["wx"], ins["wg"], ins["ow"], ins["cp"], ins["D"], par, dat, s0)
        flat = [ins[n].rearrange("r c -> (r c)").rearrange("(p b k) -> p b k", p=P, k=BLK) for n in ("w1", "w2", "w3")]
        dq = [dram("dq1", [FF, DM]), dram("dq2", [FF, DM]), dram("dq3", [DM, FF])]
        nf4_phase(nc, S, [(src, dst.rearrange("r c -> (r c)").rearrange("(p b k) -> p b k", p=P, k=BLK))
                          for src, dst in zip(flat, dq)])
        ffn_phase(nc, S, "f_", xnt, FF, dq, x0, s0, x1, True)
        norm_phase(nc, S, x1.rearrange("a p d -> (a p) d"), xnt1, "n1_")
        o1, wt1 = dram("o1", [NT, P, QK]), dram("wt1", [NT, EXPERTS, P])
        attention_phase(nc, S, xnt1, ins["wq"], ins["wkvr"], (ins["bq"], ins["bk"], ins["bv"]), o1, wt1)
        ffn_phase(nc, S, "e_", xnt1, MF, (ins["eg"], ins["eu"], ins["ed"]), x1, o1,
                  out.rearrange("b (a p) d -> (b a) p d", p=P), False, wt1)


def kernel(**inputs):
    import concourse.bacc as _bacc
    from concourse import mybir as _mybir
    from concourse.bass_utils import run_bass_kernel_spmd as _run

    f = {k: np.asarray(v) for k, v in inputs.items()}
    a = {"x": f["L0_attn_hidden_states"].reshape(T, DM)}
    w = f["L0_attn_in_proj_w"].T
    inner = HEADS * HD
    kd = lambda m: m.reshape(m.shape[0] // P, P, m.shape[1]).transpose(1, 0, 2)
    gate, xb = w[:, :inner], w[:, inner:2 * inner]
    bb, cc, dt = w[:, 2 * inner:2 * inner + GROUPS * P], w[:, 2 * inner + GROUPS * P:-HEADS], w[:, -HEADS:]
    a["wx"] = np.stack([kd(np.concatenate([xb[:, g * 512:(g + 1) * 512], bb[:, g * P:(g + 1) * P], cc[:, g * P:(g + 1) * P]], 1))
                        for g in range(GROUPS)])
    a["wg"] = np.stack([kd(gate[:, g * 512:(g + 1) * 512]) for g in range(GROUPS)])
    a["wdt"] = kd(dt)
    cw = np.concatenate([f["L0_attn_conv_weight"], f["L0_attn_conv_bias"][:, None]], 1)
    a["cp"] = np.stack([np.concatenate([cw[g * 512:(g + 1) * 512], cw[inner + g * P:inner + (g + 1) * P],
                                        cw[inner + (GROUPS + g) * P:inner + (GROUPS + g + 1) * P]]).reshape(XBC, P, 5).transpose(1, 0, 2)
                        for g in range(GROUPS)])
    owt = np.concatenate([f["L0_attn_out_proj_w"].T, f["L0_attn_norm_weight"][:, None]], 1)
    a["ow"] = np.stack([kd(owt[g * 512:(g + 1) * 512]) for g in range(GROUPS)])
    a["dt_bias"], a["A_log"], a["D"] = f["L0_attn_dt_bias"], f["L0_attn_A_log"], f["L0_attn_D"]
    a["w1"], a["w2"], a["w3"] = f["L0_ffn_w1"], f["L0_ffn_w2"], f["L0_ffn_w3"]
    a["wq"] = kd(f["L1_attn_Wq"].reshape(DM, DM))
    a["wkvr"] = kd(np.concatenate([f["L1_attn_Wk"][..., 0], f["L1_attn_Wv"][..., 0], f["L1_ffn_gate_w"].T], 1))
    a["bq"], a["bk"], a["bv"] = f["L1_attn_bq"].reshape(DM), f["L1_attn_bk"].reshape(QK), f["L1_attn_bv"].reshape(QK)
    a["eg"], a["eu"], a["ed"] = kd(f["L1_ffn_g"].T), kd(f["L1_ffn_u"].T), kd(f["L1_ffn_d"].T)
    a["desc"] = np.tile(np.arange(EXPERTS, 0, -1, dtype=np.float32), (P, 1))
    a["rep"] = np.repeat(np.eye(EXPERTS, dtype=np.float32), INTER, 1)
    eye = np.eye(P, dtype=np.float32)
    i = np.arange(P)
    a["ident"] = eye
    a["eye8"] = np.repeat(eye[:, None, :], HPG, 1)
    a["masks"] = np.stack([eye, (i[:, None] <= i[None]).astype(np.float32), (i[:, None] > i[None]).astype(np.float32),
                           np.ones((P, P), np.float32)], 1)
    nc = _bacc.Bacc("TRN2", target_bir_lowering=False, num_devices=1)
    arrays, ins = {}, {}
    for name, v in a.items():
        v = np.ascontiguousarray(v)
        arrays[f"in_{name}_dram"] = v
        ins[name] = nc.dram_tensor(f"in_{name}_dram", v.shape, _mybir.dt.from_np(v.dtype), kind="ExternalInput").ap()
    shape, dtype = _OUTS[0]
    out = nc.dram_tensor("out_0_dram", shape, _mybir.dt.from_np(np.dtype(dtype)), kind="ExternalOutput").ap()
    program(nc, ins, out)
    r = _run(nc, [arrays], core_ids=[0])
    return r.results[0]["out_0_dram"]
```

```python
from contextlib import ExitStack

import concourse.bass as bass
import numpy as np
from concourse import mybir

F32 = mybir.dt.float32
F32R = mybir.dt.float32r
ALU = mybir.AluOpType
ACT = mybir.ActivationFunctionType
AX_X = mybir.AxisListType.X

P = 128
T = 2048
DM = 512
KD = DM // P
SEQ = 512
NT = T // P
HEADS, HD, GROUPS = 64, 64, 8
HPG = HEADS // GROUPS
XBC = 6
HALVES = 2
HT = T // HALVES
SLOTS = HT // P
EPS = 1e-5
DT_, WDT_, EXC_, TOT_ = range(4)

NF4 = [-1.0, -0.6961928009986877, -0.5250730514526367, -0.39491748809814453, -0.28444138169288635,
       -0.18477343022823334, -0.09105003625154495, 0.0, 0.07958029955625534, 0.16093020141124725,
       0.24611230194568634, 0.33791524171829224, 0.44070982933044434, 0.5626170039176941,
       0.7229568362236023, 1.0]
BLK = 64
FF = 1376
FT = -(-FF // P)
QB = 9
QPIECES = 32
assert QPIECES * P * QB * BLK >= 3 * FF * DM
EXPERTS, INTER = 16, 56
MF = EXPERTS * INTER
MT = MF // P
QK = 16
NQ = 4 * QK


def split3(pe, out, stat, mov, kt):
    n = 0
    for k in range(kt):
        for a, b in ((0, 0), (0, 1), (1, 0)):
            last = pe.matmul(out, stat(a, k), mov(b, k), start=(n == 0), stop=(n == 3 * kt - 1))
            n += 1
    return last


def plain_wait(eng, met_sem, met, sem, value):
    if isinstance(value, int):
        eng.wait_ge(sem, value)
        return
    eng.compute_val(value)
    eng.wait_ge(met_sem, met)
    eng.wait_ge(sem, value)


def start_at_one(eng, *sems):
    for sem in sems:
        eng.sem_inc(sem, 1)


def norm_phase(nc, S, src_dram, xnt_dram, tag, wdt_dram=None, dtb_dram=None, dtr=None):
    with ExitStack() as ctx:
        def sb(n, s, d=F32):
            return ctx.enter_context(nc.sbuf_tensor(tag + n, s, d))

        def sem(n):
            return S(tag + n)

        x = sb("x", [P, 2, DM])
        stat = sb("stat", [P, 2, 6])
        mv = sb("mv", [P, 2, 2])
        ve = sb("ve", [P, 2, 1])
        rstd = sb("rstd", [P, 2, 1])
        half = sb("half", [P, 1])
        xn = sb("xn", [P, 2, DM])
        xh = sb("xh", [P, 2, 2, DM], F32R)
        ident = sb("ident", [P, P])
        tp = [ctx.enter_context(nc.psum_tensor(f"{tag}tp{i}", [P, DM], F32)) for i in range(2)]
        if wdt_dram is not None:
            wraw = sb("wraw", [P, KD, HEADS])
            wdt = sb("wdt", [P, 2, KD, HEADS], F32R)
            dtb = sb("dtb", [P, HEADS])
            pd = [ctx.enter_context(nc.psum_tensor(f"{tag}pd{i}", [P, 512], F32)) for i in range(2)]
        loaded = [sem(f"loaded{i}") for i in range(2)]
        consts, const_ld, wsplit = sem("consts"), sem("const_ld"), sem("wsplit")
        stats, mean_var, var_eps, rstd_ok = sem("stats"), sem("mean_var"), sem("var_eps"), sem("rstd_ok")
        normed, turned, hi_ok, lo_ok = sem("normed"), sem("turned"), sem("hi_ok"), sem("lo_ok")
        dt_mm, dt_out = sem("dt_mm"), sem("dt_out")
        stored = [sem(f"stored{i}") for i in range(2)]
        block = ctx.enter_context(nc.Block())

        @block.sync
        def _(sp):
            sp.dma_start(ident[:], S.ident_dram).then_inc(const_ld, 16)
            if wdt_dram is not None:
                sp.dma_start(wraw[:], wdt_dram).then_inc(const_ld, 16)
                sp.dma_start(dtb[:], dtb_dram.partition_broadcast(P)).then_inc(const_ld, 16)
            for r in range(2):
                sp.dma_start(x[:, r, :], src_dram[r * P:(r + 1) * P, :]).then_inc(loaded[r], 16)
            with sp.Fori(0, NT // 2 - 1) as i:
                for r in range(2):
                    plain_wait(sp, const_ld, 16, normed, 2 * i + r + 1)
                    sp.dma_start(x[:, r, :], src_dram[bass.ds((2 * i + 2 + r) * P, P), :]).then_inc(loaded[r], 16)
                    plain_wait(sp, const_ld, 16, hi_ok, 2 * i + r + 1)
                    sp.wait_ge(lo_ok, 2 * i + r + 1)
                    sp.dma_start(xnt_dram[2 * i + r], xh[:, r, :, :].bitcast(F32)).then_inc(stored[r], 16)
            for r in range(2):
                sp.wait_ge(hi_ok, NT - 1 + r)
                sp.wait_ge(lo_ok, NT - 1 + r)
                sp.dma_start(xnt_dram[NT - 2 + r], xh[:, r, :, :].bitcast(F32)).then_inc(stored[r], 16)
            for r in range(2):
                sp.wait_ge(stored[r], 16 * NT // 2 + 1)

        @block.gpsimd
        def _(pool):
            pool.memset(half[:], -0.5).then_inc(consts, 1)
            pool.wait_ge(consts, 1)
            with pool.Fori(0, NT // 2) as i:
                for r in range(2):
                    plain_wait(pool, consts, 1, mean_var, 2 * i + r + 1)
                    pool.tensor_scalar(ve[:, r, :], mv[:, r, 1:2], EPS, 1.0, ALU.add, ALU.mult).then_inc(var_eps, 1)
                    pool.wait_ge(var_eps, 2 * i + r + 1)
                    pool.tensor_tensor(rstd[:, r, :], ve[:, r, :], half[:], ALU.pow).then_inc(rstd_ok, 1)

        @block.vector
        def _(dve):
            if wdt_dram is not None:
                dve.wait_ge(const_ld, 48)
                dve.tensor_copy(wdt[:, 0, :, :], wraw[:]).then_inc(wsplit, 1)
                dve.wait_ge(wsplit, 1)
                dve.tensor_tensor(wdt[:, 1, :, :], wraw[:], wdt[:, 0, :, :].bitcast(F32), ALU.subtract).then_inc(wsplit, 1)
            with dve.Fori(0, NT // 2) as i:
                for r in range(2):
                    n = 2 * i + r
                    dve.wait_ge(loaded[r], 16 * i + 16)
                    dve.bn_stats(stat[:, r, :], x[:, r, :]).then_inc(stats, 1)
                    plain_wait(dve, const_ld, 16, stats, n + 1)
                    dve.bn_aggr(mv[:, r, :], stat[:, r, :]).then_inc(mean_var, 1)
                    dve.wait_ge(rstd_ok, n + 1)
                    dve.tensor_scalar(xn[:, r, :], x[:, r, :], mv[:, r, 0:1], rstd[:, r, :],
                                      ALU.subtract, ALU.mult).then_inc(normed, 1)
                    dve.wait_ge(turned, n + 1)
                    dve.wait_ge(hi_ok, n + 1)
                    dve.tensor_tensor(xh[:, r, 1, :], tp[r][:], xh[:, r, 0, :].bitcast(F32), ALU.subtract).then_inc(lo_ok, 1)
                    if wdt_dram is not None:
                        dve.wait_ge(dt_mm, n + 1)
                        dve.tensor_tensor(dtr[:, bass.ds(n, 1), :], pd[r][:, 0:HEADS].rearrange("p (o h) -> p o h", o=1),
                                          dtb[:].rearrange("p (o h) -> p o h", o=1), ALU.add).then_inc(dt_out, 1)

        @block.scalar
        def _(act):
            start_at_one(act, *stored)
            with act.Fori(0, NT // 2) as i:
                for r in range(2):
                    act.wait_ge(turned, 2 * i + r + 1)
                    act.wait_ge(stored[r], 16 * i + 1)
                    act.activation(xh[:, r, 0, :], tp[r][:], ACT.Copy).then_inc(hi_ok, 1)

        @block.tensor
        def _(pe):
            pe.wait_ge(const_ld, 48 if wdt_dram is not None else 16)
            if wdt_dram is not None:
                pe.wait_ge(wsplit, 2)
            with pe.Fori(0, NT // 2) as i:
                for r in range(2):
                    n = 2 * i + r
                    pe.wait_ge(normed, n + 1)
                    for k in range(KD):
                        last = pe.transpose(tp[r][:, k * P:(k + 1) * P], xn[:, r, k * P:(k + 1) * P], ident[:])
                    last.then_inc(turned, 1)
                    if wdt_dram is not None:
                        pe.wait_ge(hi_ok, n + 1)
                        pe.wait_ge(lo_ok, n + 1)
                        split3(pe, pd[r][:, 0:HEADS], lambda a, k: xh[:, r, a, k * P:(k + 1) * P],
                               lambda b, k: wdt[:, b, k, :], KD).then_inc(dt_mm, 1)


def step_phase(nc, S, dtr, alog_dram, par_dram, dat_dram):
    with ExitStack() as ctx:
        def sb(n, s, d=F32):
            return ctx.enter_context(nc.sbuf_tensor("st_" + n, s, d))

        N = NT * HEADS
        z = dtr[:].rearrange("p a h -> p (a h)")
        e, u, t1, t2, dt, a = (sb(n, [P, N]) for n in ("e", "u", "t1", "t2", "dt", "a"))
        al, an = sb("al", [P, HEADS]), sb("an", [P, HEADS])
        par = sb("par", [P, GROUPS, NT, 4, HPG])
        masks = sb("masks", [P, 4, P])
        dat = sb("dat", [HEADS, NT, P])
        pc = [ctx.enter_context(nc.psum_tensor(f"st_pc{i}", [P, 512], F32)) for i in range(6)]
        pt = [ctx.enter_context(nc.psum_tensor(f"st_pt{i}", [P, 512], F32)) for i in range(2)]
        ld, v, ac, mm, tr, dtc, out = (S("st_" + n) for n in ("ld", "v", "ac", "mm", "tr", "dtc", "out"))
        block = ctx.enter_context(nc.Block())

        def by_head(t):
            return t[:].rearrange("p (a g h) -> p a g h", a=NT, g=GROUPS)

        def par_of(i, lo=0, n=NT):
            return par[:, :, lo:lo + n, i, :].rearrange("p g a h -> p a g h")

        @block.sync
        def _(sp):
            sp.dma_start(al[:], alog_dram.partition_broadcast(P)).then_inc(ld, 16)
            sp.dma_start(masks[:], S.masks_dram).then_inc(ld, 16)
            sp.wait_ge(dtc, 5)
            sp.dma_start(dat_dram, dat[:].rearrange("h a t -> h (a t)")).then_inc(out, 16)
            sp.wait_ge(v, 13)
            sp.wait_ge(ac, 10)
            sp.dma_start(par_dram.rearrange("g p a k h -> p g (a k h)"),
                         par[:].rearrange("p g a k h -> p g (a k h)")).then_inc(out, 16)
            sp.wait_ge(out, 32)

        @block.vector
        def _(dve):
            dve.tensor_scalar(t1[:], z, -1.0, None, ALU.mult).then_inc(v, 1)
            dve.wait_ge(v, 1)
            dve.tensor_tensor(t1[:], t1[:], z, ALU.min).then_inc(v, 1)
            dve.wait_ge(ac, 1)
            dve.tensor_scalar(u[:], e[:], 1.0, None, ALU.add).then_inc(v, 1)
            dve.wait_ge(v, 3)
            dve.tensor_scalar(t2[:], u[:], -1.0, None, ALU.add).then_inc(v, 1)
            dve.wait_ge(v, 4)
            dve.tensor_tensor(t2[:], e[:], t2[:], ALU.subtract).then_inc(v, 1)
            dve.reciprocal(t1[:], u[:]).then_inc(v, 1)
            dve.wait_ge(v, 6)
            dve.tensor_tensor(t2[:], t2[:], t1[:], ALU.mult).then_inc(v, 1)
            dve.wait_ge(v, 7)
            dve.wait_ge(ac, 2)
            dve.tensor_tensor(t2[:], t2[:], dt[:], ALU.add).then_inc(v, 1)
            dve.wait_ge(v, 8)
            dve.scalar_tensor_tensor(out=dt[:], in0=z, scalar=0.0, in1=t2[:], op0=ALU.max, op1=ALU.add).then_inc(v, 1)
            dve.wait_ge(ac, 3)
            dve.tensor_scalar(al[:], an[:], -1.0, None, ALU.mult).then_inc(v, 1)
            dve.wait_ge(v, 10)
            dve.tensor_tensor(a[:].rearrange("p (a h) -> p a h", a=NT), dt[:].rearrange("p (a h) -> p a h", a=NT),
                              al[:].rearrange("p (o h) -> p o h", o=1).to_broadcast([P, NT, HEADS]), ALU.mult).then_inc(v, 1)
            dve.tensor_copy(par_of(DT_), by_head(dt)).then_inc(v, 1)
            for j in range(4):
                dve.wait_ge(tr, j + 1)
                dve.tensor_copy(dat[:, 4 * j:4 * j + 4, :].rearrange("h a t -> h (a t)"), pt[j % 2][0:HEADS, :]).then_inc(dtc, 1)
            dve.wait_ge(dtc, 4)
            dve.memset(dat[:, :, 0:1], 0.0).then_inc(dtc, 1)
            dve.wait_ge(ac, 6)
            dve.tensor_tensor(par_of(WDT_), by_head(t1), by_head(dt), ALU.mult).then_inc(v, 1)

        @block.scalar
        def _(act):
            act.wait_ge(v, 2)
            act.activation(e[:], t1[:], ACT.Exp).then_inc(ac, 1)
            act.wait_ge(v, 3)
            act.activation(dt[:], u[:], ACT.Ln).then_inc(ac, 1)
            act.wait_ge(ld, 32)
            act.activation(an[:], al[:], ACT.Exp).then_inc(ac, 1)
            act.wait_ge(v, 11)
            act.activation(e[:], a[:], ACT.Exp).then_inc(ac, 1)
            act.wait_ge(mm, 2)
            for h in range(2):
                act.activation(t1[:, h * 512:(h + 1) * 512], pc[h][:], ACT.Exp).then_inc(ac, 1)
            for i, kind in ((2, EXC_), (4, TOT_)):
                act.wait_ge(mm, i + 2)
                for h in range(2):
                    act.activation(par_of(kind, 8 * h, 8), pc[i + h][:].rearrange("p (a g h) -> p a g h", a=8, g=GROUPS),
                                   ACT.Exp).then_inc(ac, 1)

        @block.tensor
        def _(pe):
            pe.wait_ge(ld, 32)
            pe.wait_ge(v, 11)
            for i, m in ((0, 2), (2, 1), (4, 3)):
                for h in range(2):
                    pe.matmul(pc[i + h][:], masks[:, m, :], a[:, h * 512:(h + 1) * 512], start=True, stop=True).then_inc(mm, 1)
            pe.wait_ge(ac, 4)
            for j in range(4):
                if j >= 2:
                    pe.wait_ge(dtc, j - 1)
                for i in range(4):
                    last = pe.transpose(pt[j % 2][0:HEADS, i * P:(i + 1) * P],
                                        e[:, (4 * j + i) * HEADS:(4 * j + i + 1) * HEADS], masks[:, 0, :])
                last.then_inc(tr, 1)


PLAN = [([("x", 0)], [("x", 1)]), ([("x", 2), ("g", 3)], [("x", 3)]), ([("x", 4), ("x", 5)], [("g", 4)]),
        ([("g", 5)], [("g", 6)]), ([("g", 7)], [("x", 0), ("x", 1)]), ([("x", 2)], [("x", 3)]),
        ([("x", 4), ("x", 5)], [("g", 0)]), ([("g", 1)], [("g", 2)])]
GATES_AHEAD = 3
X_SPLIT, G_SPLIT = {2: (0, 1), 3: (2, 3), 4: (4, 5)}, {5: (0, 1), 6: (2, 3)}


def ssm_phase(nc, S, xnt_dram, wx_dram, wg_dram, ow_dram, cp_dram, d_dram, par_dram, dat_dram, s_dram, q_src, q_dst):
    with ExitStack() as ctx:
        def sb(n, s, d=F32):
            return ctx.enter_context(nc.sbuf_tensor("m_" + n, s, d))

        def ps(n):
            return ctx.enter_context(nc.psum_tensor("m_" + n, [P, 512], F32))

        def sem(n):
            return S("m_" + n)

        xn = sb("xn", [P, 2, KD, HT], F32R)
        wx = sb("wx", [P, 2, XBC, KD * P], F32R)
        wg = sb("wg", [P, 2, KD, 512], F32R)
        ow = sb("ow", [P, 2, KD, DM], F32R)
        raw = sb("raw", [P, 2, DM + 1])
        cp = sb("cp", [P, XBC, 5])
        par = sb("par", [P, 2, 4, 4, HPG])
        dpar = sb("dpar", [P, 2, HPG])
        cv = sb("cv", [P, 2, XBC, SEQ])
        sg = sb("sg", [P, 4, 512])
        dab = sb("dab", [P, 2, HPG * P])
        dec = sb("dec", [P, 2, HPG * P])
        eye8 = sb("eye8", [P, HPG, P])
        xs, dtx, xw, xd = (sb(n, [P, 2, 512]) for n in ("xs", "dtx", "xw", "xd"))
        bt = sb("bt", [P, 2, P])
        state = sb("state", [P, 512])
        t1 = sb("t1", [P, 512])
        y = sb("y", [P, 2, 512])
        junk = sb("junk", [P, 512])
        yt = sb("yt", [P, 2, KD * P], F32R)
        ss = sb("ss", [P, 2])
        ve = sb("ve", [P, 2])
        rs = sb("rs", [P, 2])
        half = sb("half", [P, 1])
        sacc = sb("sacc", [P, SLOTS, DM])
        q_w, q_mask = (sb(n, [P, 2, QB, BLK]) for n in ("q_w", "q_mask"))
        q_acc, q_res = (sb(n, [P, QB, BLK]) for n in ("q_acc", "q_res"))
        q_max, q_safe, q_inv = (sb(n, [P, QB]) for n in ("q_max", "q_safe", "q_inv"))
        ident = eye8[:, 0, :]

        p_in = [ps("p_in0"), ps("p_in1")]
        p_gate, p_turn, p_bg, p_yi, p_ye, p_ou = (ps(n) for n in ("p_gate", "p_turn", "p_bg", "p_yi", "p_ye", "p_ou"))

        eye_ld, cp_ld = sem("eye_ld"), sem("cp_ld")
        xn_ld = [sem(f"xn_ld{i}") for i in range(2)]
        raw_ld = [sem(f"raw_ld{i}") for i in range(2)]
        w_hi, w_lo, o_lo = sem("w_hi"), sem("w_lo"), sem("o_lo")
        par_ld = [sem(f"par_ld{i}") for i in range(2)]
        dab_ld = [sem(f"dab_ld{i}") for i in range(2)]
        in_done, cev, ctap, silu_cv = sem("in_done"), sem("cev"), sem("ctap"), sem("silu_cv")
        a_done, xs_done, bt_done = sem("a_done"), sem("xs_done"), sem("bt_done")
        dtx_done, scan_done, m_done = sem("dtx_done"), sem("scan_done"), sem("m_done")
        xw_done, xd_done = sem("xw_done"), sem("xd_done")
        b_done, st_done, s_done = sem("b_done"), sem("st_done"), sem("s_done")
        t1_done, y0_done, y_done = sem("t1_done"), sem("y0_done"), sem("y_done")
        sq_done, ve_done, rs_done = sem("sq_done"), sem("ve_done"), sem("rs_done")
        g_done, sg_done, yn_done = sem("g_done"), sem("sg_done"), sem("yn_done")
        c_done, hi_done, lo_done, d_done = sem("c_done"), sem("hi_done"), sem("lo_done"), sem("d_done")
        sacc_done, sacc_zero, s_stored, half_ok = sem("sacc_done"), sem("sacc_zero"), sem("s_stored"), sem("half_ok")
        q_ld = [sem(f"q_ld{i}") for i in range(2)]
        q_seq, q_above, q_add, q_done, q_st = (sem(n) for n in ("q_seq", "q_above", "q_add", "q_done", "q_st"))
        block = ctx.enter_context(nc.Block())

        code = np.array(NF4, np.float32)
        bound = (code[:-1] + code[1:]) * np.float32(0.5)
        QM = len(bound) - 1
        q_plan = [((), (1, 2)), ((3, 4), (5, 6)), ((7, 8), (9, 10)), ((11, 12), (13, 14))]

        GU, GQ = SLOTS, 2
        HU, HQ = GROUPS * GU, GROUPS * GQ
        OWP, WP = KD, XBC + KD
        GP = OWP + WP

        def walk(eng, prologue, slot, drain):
            prologue()
            slot(0, 0, 0, "first")
            for hf in range(HALVES):
                with eng.Fori(0, GROUPS - 1) as g:
                    for s in range(1, SLOTS):
                        slot(hf, g, s, "")
                    slot(hf, g + 1, 0, "")
                for s in range(1, SLOTS):
                    slot(hf, GROUPS - 1, s, "last" if hf == HALVES - 1 else "switch")
                if hf < HALVES - 1:
                    slot(hf + 1, 0, 0, "head")
            drain(HALVES * HU - 1)

        def at(hf, g, s):
            return hf * HU + g * GU + s, hf * HQ + g * GQ + s // 4, hf * GROUPS + g

        def after(hf, g, kind):
            return (hf + 1, 0) if kind == "switch" else (hf, g + 1)

        def plan(s, kind):
            return [[w for w in part if not (kind == "last" and (s >= 5 or (s == 4 and w[0] == "x")))] for part in PLAN[s]]

        def gates_before(it, s, w):
            return GU * (it + (1 if s >= 6 else 0)) + w

        def has_next(s, kind):
            return not (kind == "last" and s == SLOTS - 1)

        def bc(ap, n):
            return ap.rearrange("p (a o) -> p a o", o=1).to_broadcast([P, ap.shape[1], n])

        def heads(ap):
            return ap.rearrange("p (h d) -> p h d", h=HPG)

        def raw_count(it, i):
            return 16 * (i // 2 + 1) if it is None else 16 * (GP // 2) * it + 16 * (WP // 2 + i // 2 + 1)

        def piece_of(it, i):
            i, before = (i, 0) if it is None else (i - OWP, WP * it + WP)
            dst = wx[:, :, i, :] if i < XBC else wg[:, :, i - XBC, :]
            return dst, before + i

        def split_at(s, kind):
            return [] if kind == "last" else [OWP + j for j in X_SPLIT.get(s, ())] + [OWP + XBC + j for j in G_SPLIT.get(s, ())]

        @block.sync
        def _(sp):
            sp.dma_start(eye8[:], S.eye8_dram).then_inc(eye_ld, 16)
            start_at_one(sp, s_stored, q_st)
            sp.dma_start(q_w[:, 0, :, :].rearrange("p b k -> p (b k)"), q_src[0]).then_inc(q_ld[0], 16)

            def load_dab(hf, g, s):
                sp.dma_start(dab[:, s % 2, :].rearrange("p (h t) -> p h t", h=HPG),
                             dat_dram[bass.ds(g * HPG, HPG), bass.ds(hf * HT + s * P, P)].partition_broadcast(P))\
                    .then_inc(dab_ld[s % 2], 16)

            def load_par(hf, g, b):
                sp.dma_start(par[:, b, :, :, :].rearrange("p a k h -> p (a k h)"),
                             par_dram[g, :, bass.ds(hf * SLOTS + 4 * b, 4), :, :].rearrange("p a k h -> p (a k h)"))\
                    .then_inc(par_ld[b], 16)
                sp.dma_start(dpar[:, b, :], d_dram[bass.ds(g * HPG, HPG)].partition_broadcast(P)).then_inc(par_ld[b], 16)

            def load_xn(hf, b):
                for s in range(4 * b, 4 * b + 4):
                    sp.dma_start(xn[:, :, :, s * P:(s + 1) * P].bitcast(F32),
                                 xnt_dram[hf * SLOTS + s].rearrange("p a (k t) -> p a k t", k=KD)).then_inc(xn_ld[b], 16)

            def piece(it, i, src):
                if it is None:
                    if i >= 2:
                        sp.wait_ge(w_lo, i)
                elif i < 2:
                    plain_wait(sp, eye_ld, 16, w_lo, WP * it + WP - 1 + i + 1)
                elif i < OWP + 2:
                    plain_wait(sp, eye_ld, 16, o_lo, OWP * it + i - 1 + 1)
                else:
                    plain_wait(sp, eye_ld, 16, w_lo, WP * it + WP + i - OWP - 1 + 1)
                sp.dma_start(raw[:, i % 2, 0:src.shape[-1]], src).then_inc(raw_ld[i % 2], 16)

            def store_sum(hf, s, v):
                sp.wait_ge(sacc_done, v + 2)
                sp.wait_ge(s_stored, 16 * (hf * SLOTS + s) + 1)
                sp.dma_start(s_dram[hf * SLOTS + s], sacc[:, s, :]).then_inc(s_stored, 16)

            def prologue():
                piece(None, 0, wx_dram[0, 0])
                piece(None, 1, wx_dram[0, 1])
                load_xn(0, 0)
                sp.dma_start(cp[:], cp_dram[0]).then_inc(cp_ld, 16)
                for i in range(2, XBC):
                    piece(None, i, wx_dram[0, i])
                for s in range(3):
                    if s == 2:
                        sp.wait_ge(scan_done, 1 + 1)
                    load_dab(0, 0, s)
                load_par(0, 0, 0)
                for i in range(KD):
                    piece(None, XBC + i, wg_dram[0, :, i, :])
                load_xn(0, 1)

            def slot(hf, g, s, kind):
                u, q, it = at(hf, g, s)
                hn, gn = after(hf, g, kind)
                if not (kind == "last" and s >= SLOTS - 3):
                    plain_wait(sp, eye_ld, 16, scan_done, u + 3)
                    load_dab(*((hf, g, s + 3) if s + 3 < SLOTS else (hn, gn, s + 3 - SLOTS)))
                if s == 1 or (s == 5 and kind != "last"):
                    plain_wait(sp, eye_ld, 16, yn_done, u)
                    load_par(*((hf, g, 1) if s == 1 else (hn, gn, 0)))
                if s == 0:
                    for i in range(2):
                        piece(it, i, ow_dram[g, :, i, :])
                if s == 1:
                    for i in range(2, OWP):
                        piece(it, i, ow_dram[g, :, i, :])
                if kind == "switch" and s in (2, 5):
                    sp.wait_ge(g_done, GU * it + (4 if s == 2 else 8) + 1)
                    sp.wait_ge(in_done, XBC * (GQ * it + (1 if s == 2 else 2)) + 1)
                    load_xn(hn, s // 4)
                if kind != "last":
                    if s == 3:
                        plain_wait(sp, eye_ld, 16, ctap, 3 * XBC * (q + 2) + 1)
                        sp.dma_start(cp[:], cp_dram[gn]).then_inc(cp_ld, 16)
                    for i in split_at(s + 1, kind):
                        piece(it, i, wx_dram[gn, i - OWP] if i < OWP + XBC else wg_dram[gn, :, i - OWP - XBC, :])
                if s % 4 == 0:
                    n, m = 2 * it + s // 4, 1 - s // 4
                    if kind != "first":
                        plain_wait(sp, eye_ld, 16, q_done, n + 1)
                        sp.dma_start(q_dst[n - 1], q_res[:].rearrange("p b k -> p (b k)")).then_inc(q_st, 16)
                    if not (kind == "last" and s == 4):
                        sp.dma_start(q_w[:, m, :, :].rearrange("p b k -> p (b k)"), q_src[n + 1]).then_inc(q_ld[m], 16)
                if kind in ("switch", "last") and s >= 2:
                    store_sum(hf, s - 2, u - 2)
                if kind == "head":
                    store_sum(hf - 1, SLOTS - 2, u - 2)
                    store_sum(hf - 1, SLOTS - 1, u - 1)

            def drain(v):
                sp.wait_ge(q_done, QPIECES + 1)
                sp.dma_start(q_dst[QPIECES - 1], q_res[:].rearrange("p b k -> p (b k)")).then_inc(q_st, 16)
                for s in (SLOTS - 2, SLOTS - 1):
                    store_sum(HALVES - 1, s, v - (SLOTS - 1 - s))

            walk(sp, prologue, slot, drain)
            sp.wait_ge(s_stored, 16 * NT + 1)
            sp.wait_ge(q_st, 16 * QPIECES + 1)

        @block.gpsimd
        def _(pool):
            start_at_one(pool, q_add, w_lo, xw_done, xd_done, st_done, y_done, ve_done, rs_done)
            pool.memset(half[:], -0.5).then_inc(half_ok, 1)
            pool.memset(sacc[:], 0.0).then_inc(sacc_zero, 1)
            pool.wait_ge(half_ok, 1)

            def low_piece(it, i):
                dst, n = piece_of(it, i)
                plain_wait(pool, half_ok, 1, w_hi, i + 1 if it is None else GP * it + WP + i + 1)
                pool.tensor_tensor(dst[:, 1], raw[:, i % 2, 0:DM], dst[:, 0].bitcast(F32), ALU.subtract).then_inc(w_lo, 1)

            def q_adds(it, s, place):
                for j in q_plan[s % 4][place]:
                    m = QM * (2 * it + s // 4) + j - 1
                    pool.wait_ge(q_above, m + 2)
                    pool.wait_ge(q_add, m + 1)
                    pool.tensor_tensor(q_acc[:], q_acc[:], q_mask[:, j % 2, :, :], ALU.add).then_inc(q_add, 1)

            def x_parts(u, it, s):
                b, c, r = s // 4, s % 4, s % 2
                if c == 0:
                    pool.wait_ge(par_ld[b], 32 * it + 32)
                pool.wait_ge(xs_done, u + 2)
                pool.tensor_tensor(heads(xw[:, r, :]), heads(xs[:, r, :]), bc(par[:, b, c, WDT_, :], HD), ALU.mult).then_inc(xw_done, 1)
                pool.tensor_tensor(heads(xd[:, r, :]), heads(xs[:, r, :]), bc(dpar[:, b, :], HD), ALU.mult).then_inc(xd_done, 1)

            def prologue():
                for i in range(WP):
                    low_piece(None, i)
                x_parts(0, 0, 0)

            def slot(hf, g, s, kind):
                u, q, it = at(hf, g, s)
                b, c, r = s // 4, s % 4, s % 2
                if c in (1, 2):
                    pool.wait_ge(b_done, u + 2)
                    pool.wait_ge(s_done, 3 * q + c + 1)
                    pool.tensor_tensor(heads(state[:]), heads(state[:]), bc(par[:, b, c, TOT_, :], HD), ALU.mult).then_inc(st_done, 1)
                if c > 0:
                    pool.wait_ge(y0_done, u + 2)
                    pool.wait_ge(t1_done, 3 * q + c + 1)
                    pool.tensor_tensor(y[:, r, :], y[:, r, :], t1[:], ALU.add).then_inc(y_done, 1)
                q_adds(it, s, 0)
                plain_wait(pool, half_ok, 1, sq_done, u + 2)
                pool.tensor_scalar(ve[:, r:r + 1], ss[:, r:r + 1], 1.0 / 512, EPS, ALU.mult, ALU.add).then_inc(ve_done, 1)
                pool.wait_ge(ve_done, u + 2)
                pool.tensor_tensor(rs[:, r:r + 1], ve[:, r:r + 1], half[:], ALU.pow).then_inc(rs_done, 1)
                for i in split_at(s, kind):
                    low_piece(it, i)
                if has_next(s, kind):
                    x_parts(u + 1, it + (s + 1) // SLOTS, (s + 1) % SLOTS)
                q_adds(it, s, 1)
                for k in range(5, SLOTS) if kind == "head" else [s - 3] if kind == "switch" and s >= 3 else []:
                    pool.wait_ge(s_stored, 16 * (k + 1) + 1)
                    pool.memset(sacc[:, k, :], 0.0).then_inc(sacc_zero, 1)

            walk(pool, prologue, slot, lambda v: None)

        @block.vector
        def _(dve):
            start_at_one(dve, q_seq, q_above, q_done, ctap, dtx_done, scan_done, m_done, s_done, t1_done, y0_done, yn_done, lo_done, sacc_done, o_lo)

            def conv(q, j, b):
                m = XBC * q + j
                dve.wait_ge(cev, m + 2)
                for d in (1, 2, 3):
                    if d > 1:
                        dve.wait_ge(ctap, 3 * m + d)
                    dve.scalar_tensor_tensor(out=cv[:, b, j, d:SEQ], in0=p_in[j % 2][:, 0:SEQ - d],
                                             scalar=cp[:, j, 3 - d:4 - d], in1=cv[:, b, j, d:SEQ],
                                             op0=ALU.mult, op1=ALU.add).then_inc(ctap, 1)

            def scan(n, it, s, free):
                r = s % 2
                dve.wait_ge(dab_ld[r], it * (16 * GU // 2) + 16 * (s // 2 + 1))
                dve.wait_ge(b_done, free + 1)
                dve.tensor_tensor_scan(out=dec[:, r, :], data0=dab[:, r, :], data1=eye8[:].rearrange("p h t -> p (h t)"),
                                       initial=0.0, op0=ALU.mult, op1=ALU.add).then_inc(scan_done, 1)

            def x_and_m(u, it, s):
                b, c, r = s // 4, s % 4, s % 2
                dve.wait_ge(xs_done, u + 2)
                if c == 0:
                    dve.wait_ge(par_ld[b], 32 * it + 32)
                dve.tensor_tensor(heads(dtx[:, r, :]), heads(p_turn[:]), bc(par[:, b, c, DT_, :], HD), ALU.mult).then_inc(dtx_done, 1)
                dve.wait_ge(bt_done, u + 2)
                dve.wait_ge(scan_done, u + 2)
                d = dec[:, r, :].rearrange("p (h t) -> p h t", h=HPG)
                dve.tensor_tensor(d, d, p_bg[:, P:2 * P].rearrange("p (o t) -> p o t", o=1).to_broadcast([P, HPG, P]),
                                  ALU.mult).then_inc(m_done, 1)

            def low_part(v):
                dve.wait_ge(c_done, v + 2)
                dve.wait_ge(hi_done, v + 2)
                dve.tensor_tensor(yt[:, 1, :], p_turn[:], yt[:, 0, :].bitcast(F32), ALU.subtract).then_inc(lo_done, 1)

            def scales(vec):
                return vec[:].rearrange("p (b o) -> p b o", o=1).to_broadcast([P, QB, BLK])

            def q_masks(it, s, place):
                for j in q_plan[s % 4][place]:
                    m = QM * (2 * it + s // 4) + j - 1
                    dve.wait_ge(q_add, m)
                    dve.tensor_scalar(q_mask[:, j % 2, :, :], q_w[:, s // 4, :, :], float(bound[j]),
                                      float(code[j + 1] - code[j]), ALU.is_gt, ALU.mult).then_inc(q_above, 1)

            def q_end(n):
                dve.wait_ge(q_add, QM * (n + 1) + 1)
                dve.wait_ge(q_st, 16 * n + 1)
                dve.scalar_tensor_tensor(out=q_res[:], in0=q_acc[:], scalar=float(code[0]), in1=scales(q_max),
                                         op0=ALU.add, op1=ALU.mult).then_inc(q_done, 1)

            def q_scale(it, s):
                n = 2 * it + s // 4
                dve.wait_ge(q_ld[s // 4], 16 * it + 16)
                dve.wait_ge(q_done, n + 1)
                dve.tensor_reduce(q_max[:], q_w[:, s // 4, :, :], AX_X, ALU.max, apply_absolute_value=True).then_inc(q_seq, 1)
                dve.wait_ge(q_seq, 4 * n + 2)
                dve.scalar_tensor_tensor(out=q_safe[:], in0=q_max[:], scalar=0.0, in1=q_max[:],
                                         op0=ALU.is_equal, op1=ALU.add).then_inc(q_seq, 1)
                dve.wait_ge(q_seq, 4 * n + 3)
                dve.reciprocal(q_inv[:], q_safe[:]).then_inc(q_seq, 1)

            def q_start(it, s):
                n, w = 2 * it + s // 4, q_w[:, s // 4, :, :]
                dve.wait_ge(q_seq, 4 * n + 4)
                dve.tensor_tensor(w, w, scales(q_inv), ALU.mult).then_inc(q_seq, 1)
                dve.wait_ge(q_seq, 4 * n + 5)
                dve.tensor_scalar(q_acc[:], w, float(bound[0]), float(code[1] - code[0]), ALU.is_gt, ALU.mult)

            def add_out(v, s):
                dve.wait_ge(d_done, v + 2)
                dve.wait_ge(sacc_done, v + 1)
                dve.tensor_tensor(sacc[:, s, :], sacc[:, s, :], p_ou[:], ALU.add).then_inc(sacc_done, 1)

            def low_output(it, pieces):
                for i in pieces:
                    dve.wait_ge(w_hi, GP * it + WP + i + 1)
                    src = raw[:, i % 2, :]
                    dve.scalar_tensor_tensor(out=ow[:, 1, i, :], in0=src[:, 0:DM], scalar=src[:, DM:DM + 1],
                                             in1=ow[:, 0, i, :].bitcast(F32), op0=ALU.mult, op1=ALU.subtract).then_inc(o_lo, 1)

            def prologue():
                dve.wait_ge(eye_ld, 16)
                for j in range(XBC):
                    conv(0, j, 0)
                scan(0, 0, 0, 0)
                scan(1, 0, 1, 0)
                x_and_m(0, 0, 0)

            def slot(hf, g, s, kind):
                u, q, it = at(hf, g, s)
                b, c, r = s // 4, s % 4, s % 2
                mid, end = plan(s, kind)
                dve.wait_ge(b_done, u + 2)
                dve.wait_ge(xd_done, u + 2)
                dve.wait_ge(c_done, (u if kind == "first" else u - 1) + 1)
                dve.tensor_tensor(y[:, r, :], p_yi[:], xd[:, r, :], ALU.add).then_inc(y0_done, 1)
                if c > 0:
                    dve.wait_ge(y_done, 3 * q + c)
                    dve.tensor_tensor(heads(t1[:]), heads(p_ye[:]), bc(par[:, b, c, EXC_, :], HD), ALU.mult).then_inc(t1_done, 1)
                if c == 0:
                    if kind != "first":
                        q_end(2 * it + s // 4 - 1)
                    q_scale(it, s)
                q_masks(it, s, 0)
                if c == 0:
                    dve.wait_ge(s_done, 3 * q + 1)
                    dve.tensor_copy(state[:], p_ou[:]).then_inc(s_done, 1)
                elif c < 3:
                    dve.wait_ge(st_done, 2 * q + c + 1)
                    dve.tensor_tensor(state[:], state[:], p_ou[:], ALU.add).then_inc(s_done, 1)
                if s == 1:
                    low_output(it, (0, 1))
                if kind != "first":
                    low_part(u - 1)
                if not (kind == "last" and s >= SLOTS - 2):
                    scan(u + 2, it + (s + 2) // SLOTS, (s + 2) % SLOTS, u + 1)
                if s == 1:
                    low_output(it, (2, 3))
                for what, j in mid:
                    if what == "x":
                        conv(q + 1, j, 1 - b)
                if has_next(s, kind):
                    x_and_m(u + 1, it + (s + 1) // SLOTS, (s + 1) % SLOTS)
                dve.wait_ge(rs_done, u + 2)
                dve.wait_ge(sg_done, u + 2)
                dve.scalar_tensor_tensor(out=y[:, r, :], in0=y[:, r, :], scalar=rs[:, r:r + 1], in1=sg[:, s % 4, :],
                                         op0=ALU.mult, op1=ALU.mult).then_inc(yn_done, 1)
                if kind != "first":
                    dve.wait_ge(sacc_zero, 1 if hf == 0 or s == 0 and kind == "head" else 1 + ((s - 1) % SLOTS + 1))
                    add_out(u - 1, (s - 1) % SLOTS)
                if c == 0:
                    q_start(it, s)
                q_masks(it, s, 1)
                for what, j in end:
                    if what == "x":
                        conv(q + 1, j, 1 - b)

            def drain(v):
                q_end(QPIECES - 1)
                low_part(v)
                add_out(v, SLOTS - 1)

            walk(dve, prologue, slot, drain)

        @block.scalar
        def _(act):
            start_at_one(act, cev, silu_cv, xs_done, bt_done, sq_done, sg_done, hi_done)

            def high_piece(it, i):
                dst, _ = piece_of(it, i)
                act.wait_ge(raw_ld[i % 2], raw_count(it, i))
                act.activation(dst[:, 0], raw[:, i % 2, 0:DM], ACT.Copy).then_inc(w_hi, 1)

            def high_output(it, pieces):
                for i in pieces:
                    act.wait_ge(raw_ld[i % 2], raw_count(it, i))
                    act.activation(ow[:, 0, i, :], raw[:, i % 2, 0:DM], ACT.Copy, scale=raw[:, i % 2, DM:DM + 1]).then_inc(w_hi, 1)

            def evac(q, j, b, free):
                act.wait_ge(in_done, XBC * q + j + 2)
                act.wait_ge(b_done, free + 1)
                act.activation(cv[:, b, j, :], p_in[j % 2][:], ACT.Identity, bias=cp[:, j, 4:5], scale=cp[:, j, 3:4])\
                    .then_inc(cev, 1)

            def silu_conv(q, b):
                act.wait_ge(ctap, 3 * XBC * q + 3 * XBC + 1)
                act.activation(cv[:, b, :, :], cv[:, b, :, :], ACT.Silu).then_inc(silu_cv, 1)

            def silu_gate(n, w):
                act.wait_ge(g_done, n + 2)
                act.wait_ge(yn_done, max(n - 3, 0) + 1 if isinstance(n, int) else n - 3 + 1)
                act.activation(sg[:, w % 4, :], p_gate[:], ACT.Silu).then_inc(sg_done, 1)

            def tokens(u, s, free):
                r = s % 2
                act.wait_ge(a_done, u + 2)
                act.wait_ge(xw_done, free + 1)
                act.wait_ge(xd_done, free + 1)
                act.activation(xs[:, r, :], p_turn[:], ACT.Copy).then_inc(xs_done, 1)
                act.wait_ge(b_done, free + 1)
                act.activation(bt[:, r, :], p_bg[:, 0:P], ACT.Copy).then_inc(bt_done, 1)

            def high_part(v):
                act.wait_ge(c_done, v + 2)
                act.wait_ge(d_done, v + 1)
                act.activation(yt[:, 0, :], p_turn[:], ACT.Copy).then_inc(hi_done, 1)

            def prologue():
                for i in range(XBC):
                    high_piece(None, i)
                act.wait_ge(cp_ld, 16)
                for j in range(XBC):
                    evac(0, j, 0, 0)
                for i in range(XBC, WP):
                    high_piece(None, i)
                for w in range(GATES_AHEAD):
                    silu_gate(w, w)
                silu_conv(0, 0)
                tokens(0, 0, 0)

            def slot(hf, g, s, kind):
                u, q, it = at(hf, g, s)
                b, c, r = s // 4, s % 4, s % 2
                mid, end = plan(s, kind)

                def extra(part):
                    for what, j in part:
                        if what == "x":
                            if s == 4:
                                act.wait_ge(cp_ld, 16 * it + 32)
                            evac(q + 1, j, 1 - b, u)
                        else:
                            silu_gate(gates_before(it, s, j), j)

                if s == 1:
                    act.wait_ge(d_done, u)
                    high_output(it, (0, 1))
                for i in split_at(s, kind):
                    if i < OWP + XBC:
                        act.wait_ge(in_done, XBC * (GQ * it + 1) + i - OWP + 2)
                    else:
                        act.wait_ge(g_done, GU * it + GU + 1)
                    high_piece(it, i)
                if kind != "first":
                    high_part(u - 1)
                if s == 1:
                    high_output(it, (2, 3))
                if c > 0:
                    act.wait_ge(y_done, 3 * q + c + 1)
                else:
                    act.wait_ge(y0_done, u + 2)
                act.wait_ge(ve_done, (u if kind == "first" else u - 1) + 1)
                act.activation(junk[:], y[:, r, :], ACT.Square, accum_out=ss[:, r:r + 1]).then_inc(sq_done, 1)
                extra(mid)
                if has_next(s, kind):
                    tokens(u + 1, (s + 1) % SLOTS, u)
                if ("x", XBC - 1) in mid:
                    silu_conv(q + 1, 1 - b)
                extra(end)

            walk(act, prologue, slot, high_part)

        @block.tensor
        def _(pe):
            start_at_one(pe, in_done, a_done, b_done, g_done, c_done, d_done)

            def conv_in(q, it, j, b, free):
                if b == 0:
                    pe.wait_ge(w_lo, WP * it + j + 1 + 1)
                pe.wait_ge(ctap, free + 1)
                split3(pe, p_in[j % 2][:], lambda a, k: wx[:, a, j, k * P:(k + 1) * P],
                       lambda a, k: xn[:, a, k, b * SEQ:(b + 1) * SEQ], KD).then_inc(in_done, 1)

            def gate(n, it, w):
                if w == 0:
                    pe.wait_ge(w_lo, WP * it + WP + 1)
                pe.wait_ge(sg_done, n + 1)
                split3(pe, p_gate[:], lambda a, k: xn[:, a, k, w * P:(w + 1) * P],
                       lambda a, k: wg[:, a, k, :], KD).then_inc(g_done, 1)

            def turn_in(u, q, s, turned):
                b, c = s // 4, s % 4
                ch = slice(c * P, (c + 1) * P)
                pe.wait_ge(silu_cv, q + 2)
                pe.wait_ge(hi_done, turned + 1)
                pe.wait_ge(lo_done, turned + 1)
                pe.wait_ge(xs_done, u + 1)
                pe.wait_ge(dtx_done, u + 1)
                for k in range(4):
                    pe.transpose(p_turn[:, k * P:(k + 1) * P], cv[:, b, k, ch], ident)
                pe.wait_ge(m_done, u + 1)
                pe.wait_ge(bt_done, u + 1)
                pe.transpose(p_bg[:, 0:P], cv[:, b, 4, ch], ident)
                pe.matmul(p_bg[:, P:2 * P], cv[:, b, 4, ch], cv[:, b, 5, ch], start=True, stop=True).then_inc(a_done, 1)

            def turn_out(v, s):
                pe.wait_ge(yn_done, v + 2)
                for k in range(KD):
                    last = pe.transpose(p_turn[:, k * P:(k + 1) * P], y[:, s % 2, k * P:(k + 1) * P], ident)
                last.then_inc(c_done, 1)

            def project(v, it):
                pe.wait_ge(hi_done, v + 2)
                pe.wait_ge(lo_done, v + 2)
                pe.wait_ge(o_lo, OWP * it + OWP + 1)
                split3(pe, p_ou[:], lambda a, k: yt[:, a, k * P:(k + 1) * P], lambda a, k: ow[:, a, k, :], KD).then_inc(d_done, 1)

            def prologue():
                pe.wait_ge(eye_ld, 16)
                pe.wait_ge(xn_ld[0], 16 * 4)
                for j in range(XBC):
                    conv_in(0, 0, j, 0, max(3 * (j - 1), 0))
                for w in range(GATES_AHEAD):
                    gate(w, 0, w)
                turn_in(0, 0, 0, 0)

            def slot(hf, g, s, kind):
                u, q, it = at(hf, g, s)
                b, c, r = s // 4, s % 4, s % 2
                mid, end = plan(s, kind)

                def extra(part):
                    for what, j in part:
                        if what == "x":
                            conv_in(q + 1, it + b, j, 1 - b, 3 * (XBC * (q + 1) + j - 1))
                        else:
                            gate(gates_before(it, s, j), it + (1 if s >= 6 else 0), j)

                if kind in ("first", "head"):
                    pe.wait_ge(xn_ld[1], 16 * 4 * (hf + 1))
                pe.wait_ge(m_done, u + 2)
                pe.wait_ge(dtx_done, u + 2)
                pe.wait_ge(y0_done, u + 1)
                for h in range(HPG):
                    last = pe.matmul(p_yi[:, h * HD:(h + 1) * HD], dec[:, r, h * P:(h + 1) * P], dtx[:, r, h * HD:(h + 1) * HD],
                                     start=True, stop=True)
                if c > 0:
                    pe.wait_ge(s_done, 3 * q + c + 1)
                    pe.wait_ge(t1_done, 3 * q + c)
                    last = pe.matmul(p_ye[:], cv[:, b, 5, c * P:(c + 1) * P], state[:], start=True, stop=True)
                if c < 3:
                    pe.wait_ge(bt_done, u + 2)
                    pe.wait_ge(xw_done, u + 2)
                    pe.wait_ge(sacc_done, (u if kind == "first" else u - 1) + 1)
                    last = pe.matmul(p_ou[:], bt[:, r, :], xw[:, r, :], start=True, stop=True)
                last.then_inc(b_done, 1)
                if kind != "first":
                    pe.wait_ge(xs_done, u + 2)
                    pe.wait_ge(dtx_done, u + 2)
                    turn_out(u - 1, (s - 1) % SLOTS)
                extra(mid)
                if has_next(s, kind):
                    turn_in(u + 1, hf * HQ + g * GQ + (s + 1) // 4, (s + 1) % SLOTS, u)
                if kind != "first":
                    pe.wait_ge(s_done, 3 * q + min(c + 1, 3) + 1)
                    pe.wait_ge(sacc_done, u)
                    project(u - 1, it - (1 if s == 0 else 0))
                if kind == "switch" and s == 4:
                    pe.wait_ge(xn_ld[0], 16 * 4 * (hf + 2))
                extra(end)

            def drain(v):
                turn_out(v, SLOTS - 1)
                pe.wait_ge(sacc_done, v + 1)
                project(v, HALVES * GROUPS - 1)

            walk(pe, prologue, slot, drain)


def ffn_phase(nc, S, tag, xnt_dram, hidden, weights, x_dram, s_dram, out_dram, turn, experts=None):
    gate_dram, up_dram, down_dram = weights
    nf = -(-hidden // P)
    width = [min(P, hidden - f * P) for f in range(nf)]
    with ExitStack() as ctx:
        def sb(n, s, d=F32):
            return ctx.enter_context(nc.sbuf_tensor(tag + n, s, d))

        def sem(n):
            return S(tag + n)

        wg = sb("wg", [P, 2, KD, nf * P], F32R)
        wu = sb("wu", [P, 2, KD, nf * P], F32R)
        wd = sb("wd", [P, 2, nf, DM], F32R)
        raw = sb("raw", [P, 2, max(DM, 0 if turn else hidden)])
        xn = sb("xn", [P, 2, 2, KD, SEQ], F32R)
        gs = sb("gs", [P, 2, SEQ])
        h = sb("h", [P, 2, SEQ])
        ht = sb("ht", [P, 2, 2, SEQ], F32R)
        ge, xi, xo = (sb(n, [P, 2, DM]) for n in ("ge", "xi", "xo"))
        si = sb("si", [P, 2, s_dram.shape[-1]])
        ident = sb("ident", [P, P])
        bank = [ctx.enter_context(nc.psum_tensor(f"{tag}bank{i}", [P, 512], F32)) for i in range(8)]
        pg, pu, pw, po = bank[0:2], bank[2], bank[3], bank[4:8]
        if experts is not None:
            rep = sb("rep", [EXPERTS, hidden])
            wt = sb("wt", [EXPERTS, 2, SEQ])
        raw_ld = [sem(f"raw_ld{i}") for i in range(2)]
        id_ld, turned, w_hi, w_lo = sem("id_ld"), sem("turned"), sem("w_hi"), sem("w_lo")
        xn_ld = [sem(f"xn_ld{i}") for i in range(2)]
        in_ld = [sem(f"in_ld{i}") for i in range(2)]
        stored = [sem(f"stored{i}") for i in range(2)]
        g_done, u_done, w_done, silu_ok, h_ok = sem("g_done"), sem("u_done"), sem("w_done"), sem("silu_ok"), sem("h_ok")
        hw_ok, hi_ok, lo_ok, d_done, o_done = sem("hw_ok"), sem("hi_ok"), sem("lo_ok"), sem("d_done"), sem("o_done")
        ge_ok, sg_ok, res_ok = sem("ge_ok"), sem("sg_ok"), sem("res_ok")
        block = ctx.enter_context(nc.Block())

        LX = 16 * 4 * (2 if experts is not None else 1)
        pieces = []
        if turn:
            for src, dst in ((gate_dram, wg), (up_dram, wu)):
                for f, w in enumerate(width):
                    pieces.append((src[f * P:f * P + w, :], w, DM, dst[:, :, :, f * P:f * P + w]))
            for f, w in enumerate(width):
                pieces.append((down_dram[:, f * P:f * P + w].rearrange("(k p) n -> p k n", p=P), P, KD * w, wd[0:w, :, f, :]))
        else:
            for src, dst in ((gate_dram, wg), (up_dram, wu)):
                for k in range(KD):
                    pieces.append((src[:, k, :], P, hidden, dst[:, :, k, 0:hidden]))
            for f in range(nf):
                pieces.append((down_dram[:, f, :], P, DM, wd[:, :, f, :]))

        def turned_view(n):
            _, rows, cols, _ = pieces[n]
            if n < 2 * nf:
                return pg[n % 2][:].rearrange("p (k n) -> p k n", k=KD)[:, :, 0:rows]
            return pg[n % 2][0:cols // KD, :]

        @block.sync
        def _(sp):
            sp.dma_start(ident[:], S.ident_dram).then_inc(id_ld, 16)
            start_at_one(sp, *xn_ld, *in_ld, *stored)
            if experts is not None:
                sp.dma_start(rep[:], S.rep_dram).then_inc(id_ld, 16)

            def load_xn(tile, r):
                for c in range(4):
                    sp.dma_start(xn[:, r, :, :, c * P:(c + 1) * P].bitcast(F32),
                                 xnt_dram[tile + c].rearrange("p a (k t) -> p a k t", k=KD)).then_inc(xn_ld[r], 16)
                    if experts is not None:
                        sp.dma_start(wt[:, r, c * P:(c + 1) * P], experts[tile + c]).then_inc(xn_ld[r], 16)

            load_xn(0, 0)
            for n, (src, rows, cols, _) in enumerate(pieces):
                if n >= 2:
                    sp.wait_ge(w_lo, n - 1)
                dst = raw[0:rows, n % 2, 0:cols]
                if turn and n >= 2 * nf:
                    dst = dst.rearrange("p (k n) -> p k n", k=KD)
                sp.dma_start(dst, src).then_inc(raw_ld[n % 2], 16)
            load_xn(4, 1)
            with sp.Fori(0, 2) as i:
                for r in range(2):
                    t0 = 8 * i + 4 * r
                    for c in range(4):
                        plain_wait(sp, id_ld, 16, res_ok, t0 + max(c - 1, 0) + 1)
                        sp.dma_start(xi[:, c % 2, :], x_dram[t0 + c]).then_inc(in_ld[c % 2], 16)
                        sp.dma_start(si[:, c % 2, :], s_dram[t0 + c]).then_inc(in_ld[c % 2], 16)
                        if c >= 1:
                            plain_wait(sp, id_ld, 16, res_ok, t0 + c + 1)
                            sp.dma_start(out_dram[t0 + c - 1], xo[:, (c - 1) % 2, :]).then_inc(stored[(c - 1) % 2], 16)
                    plain_wait(sp, id_ld, 16, res_ok, t0 + 4 + 1)
                    sp.dma_start(out_dram[t0 + 3], xo[:, 1, :]).then_inc(stored[1], 16)
                    load_xn(8 - 8 * i + 4 * r, r)
            for r in range(2):
                sp.wait_ge(stored[r], 16 * NT // 2 + 1)
                sp.wait_ge(xn_ld[r], 3 * LX + 1)

        @block.scalar
        def _(act):
            start_at_one(act, silu_ok, hi_ok, ge_ok)
            for n, (_, rows, _, dst) in enumerate(pieces):
                if turn:
                    act.wait_ge(turned, n + 1)
                    act.activation(dst[:, 0], turned_view(n), ACT.Copy).then_inc(w_hi, 1)
                else:
                    act.wait_ge(raw_ld[n % 2], 16 * (n // 2 + 1))
                    act.activation(dst[:, 0], raw[0:rows, n % 2, 0:dst.shape[-1]], ACT.Copy).then_inc(w_hi, 1)

            def high(n, f):
                act.wait_ge(hw_ok if experts is not None else h_ok, n + 1 + 1)
                act.wait_ge(d_done, n - min(f, 1) + 1)
                act.activation(ht[0:width[f], f % 2, 0, :], h[0:width[f], f % 2, :], ACT.Copy).then_inc(hi_ok, 1)

            with act.Fori(0, 2) as i:
                for r in range(2):
                    n0 = (2 * i + r) * nf
                    for f in range(nf):
                        act.wait_ge(g_done, n0 + f + 1 + 1)
                        act.wait_ge(h_ok, n0 + f - min(f, 1) + 1)
                        act.activation(gs[0:width[f], f % 2, :], pg[f % 2][0:width[f], :], ACT.Silu).then_inc(silu_ok, 1)
                        if f >= 1:
                            high(n0 + f - 1, f - 1)
                    high(n0 + nf - 1, nf - 1)
                    for c in range(4):
                        act.wait_ge(d_done, n0 + nf + 1)
                        act.wait_ge(res_ok, 8 * i + 4 * r + max(c - 1, 0) + 1)
                        act.activation(ge[:, c % 2, :], po[c][:], ACT.Silu).then_inc(ge_ok, 1)

        @block.vector
        def _(dve):
            start_at_one(dve, h_ok, hw_ok, lo_ok, sg_ok, res_ok)
            for n, (_, rows, _, dst) in enumerate(pieces):
                dve.wait_ge(w_hi, n + 1)
                src = turned_view(n) if turn else raw[0:rows, n % 2, 0:dst.shape[-1]]
                dve.tensor_tensor(dst[:, 1], src, dst[:, 0].bitcast(F32), ALU.subtract).then_inc(w_lo, 1)

            def low(n, f):
                dve.wait_ge(hi_ok, n + 1 + 1)
                w = width[f]
                dve.tensor_tensor(ht[0:w, f % 2, 1, :], h[0:w, f % 2, :], ht[0:w, f % 2, 0, :].bitcast(F32), ALU.subtract)\
                    .then_inc(lo_ok, 1)

            with dve.Fori(0, 2) as i:
                for r in range(2):
                    n0 = (2 * i + r) * nf
                    for f in range(nf):
                        w, n = width[f], n0 + f
                        dve.wait_ge(silu_ok, n + 1 + 1)
                        dve.wait_ge(u_done, n + 1 + 1)
                        dve.wait_ge(lo_ok, n - min(f, 1) + 1)
                        dve.tensor_tensor(h[0:w, f % 2, :], pu[0:w, :], gs[0:w, f % 2, :], ALU.mult).then_inc(h_ok, 1)
                        if experts is not None:
                            dve.wait_ge(w_done, n + 1 + 1)
                            dve.wait_ge(h_ok, n + 1 + 1)
                            dve.tensor_tensor(h[0:w, f % 2, :], pw[0:w, :], h[0:w, f % 2, :], ALU.mult).then_inc(hw_ok, 1)
                        if f >= 1:
                            low(n - 1, f - 1)
                    low(n0 + nf - 1, nf - 1)
                    for c in range(4):
                        t = 8 * i + 4 * r + c
                        dve.wait_ge(ge_ok, t + 1 + 1)
                        dve.wait_ge(in_ld[c % 2], 32 * (4 * i + 2 * r + c // 2 + 1) + 1)
                        g3, s3 = ge[:, c % 2, :], si[:, c % 2, :]
                        if experts is not None:
                            g3 = g3.rearrange("p (d h) -> p d h", d=QK)
                            s3 = s3.rearrange("p (d o) -> p d o", o=1).to_broadcast([P, QK, DM // QK])
                        dve.tensor_tensor(g3, g3, s3, ALU.mult).then_inc(sg_ok, 1)
                        dve.wait_ge(sg_ok, t + 1 + 1)
                        dve.wait_ge(stored[c % 2], 16 * (4 * i + 2 * r + c // 2) + 1)
                        dve.tensor_tensor(xo[:, c % 2, :], ge[:, c % 2, :], xi[:, c % 2, :], ALU.add).then_inc(res_ok, 1)

        @block.tensor
        def _(pe):
            start_at_one(pe, g_done, u_done, w_done, d_done)
            pe.wait_ge(id_ld, 32 if experts is not None else 16)
            if turn:
                for n, (_, rows, cols, _) in enumerate(pieces):
                    pe.wait_ge(raw_ld[n % 2], 16 * (n // 2 + 1))
                    if n >= 2:
                        pe.wait_ge(w_lo, n - 1)
                    for k in range(KD):
                        if n < 2 * nf:
                            last = pe.transpose(pg[n % 2][:, k * P:k * P + rows], raw[0:rows, n % 2, k * P:(k + 1) * P], ident[0:rows, 0:rows])
                        else:
                            w = cols // KD
                            last = pe.transpose(pg[n % 2][0:w, k * P:(k + 1) * P], raw[:, n % 2, k * w:(k + 1) * w], ident[:])
                    last.then_inc(turned, 1)
            pe.wait_ge(w_lo, len(pieces))

            def hidden_in(i, r, f):
                w, n = width[f], (2 * i + r) * nf + f
                cols = slice(f * P, f * P + w)
                pe.wait_ge(silu_ok, n - min(f, 1) + 1)
                split3(pe, pg[f % 2][0:w, :], lambda a, k: wg[:, a, k, cols], lambda a, k: xn[:, r, a, k, :], KD).then_inc(g_done, 1)
                pe.wait_ge(h_ok, n + 1)
                split3(pe, pu[0:w, :], lambda a, k: wu[:, a, k, cols], lambda a, k: xn[:, r, a, k, :], KD).then_inc(u_done, 1)
                if experts is not None:
                    pe.wait_ge(hw_ok, n + 1)
                    pe.matmul(pw[0:w, :], rep[:, cols], wt[:, r, :], start=True, stop=True).then_inc(w_done, 1)

            def hidden_out(i, r, f):
                w, n = width[f], (2 * i + r) * nf + f
                pe.wait_ge(hi_ok, n + 1 + 1)
                pe.wait_ge(lo_ok, n + 1 + 1)
                if f == 0:
                    pe.wait_ge(ge_ok, 8 * i + 4 * r + 1)
                for c in range(4):
                    for m, (a, b) in enumerate(((0, 0), (0, 1), (1, 0))):
                        last = pe.matmul(po[c][:], ht[0:w, f % 2, a, c * P:(c + 1) * P], wd[0:w, b, f, :],
                                         start=(f == 0 and m == 0), stop=(f == nf - 1 and m == 2))
                last.then_inc(d_done, 1)

            with pe.Fori(0, 2) as i:
                for r in range(2):
                    pe.wait_ge(xn_ld[r], LX * i + LX + 1)
                    hidden_in(i, r, 0)
                    for f in range(1, nf):
                        hidden_in(i, r, f)
                        hidden_out(i, r, f - 1)
                    hidden_out(i, r, nf - 1)


def attention_phase(nc, S, xnt_dram, wq_dram, wkv_dram, b_dram, o_dram, wt_dram):
    with ExitStack() as ctx:
        def sb(n, s, d=F32):
            return ctx.enter_context(nc.sbuf_tensor("a_" + n, s, d))

        wq = sb("wq", [P, KD, QK, DM // QK])
        w = sb("w", [P, KD, NQ])
        wr = sb("wr", [P, 2, KD, NQ], F32R)
        bq = sb("bq", [P, QK, DM // QK])
        bias = sb("bias", [P, NQ])
        xh = sb("xh", [P, 2, 2, DM], F32R)
        qk = sb("qk", [P, NT, NQ])
        sc = sb("sc", [P, NT, QK, QK])
        mx, sm, so = (sb(n, [P, NT, QK]) for n in ("mx", "sm", "so"))
        pr, one, eq, p2 = (sb(n, [P, NT, EXPERTS]) for n in ("pr", "one", "eq", "p2"))
        top = sb("top", [P, NT])
        desc = sb("desc", [P, EXPERTS])
        ident = sb("ident", [P, P])
        wt = sb("wt", [EXPERTS, NT, P])
        pq = [ctx.enter_context(nc.psum_tensor(f"a_pq{i}", [P, 512], F32)) for i in range(2)]
        pt = [ctx.enter_context(nc.psum_tensor(f"a_pt{i}", [P, 512], F32)) for i in range(4)]
        ld, xh_ld = S("a_ld"), [S(f"a_xh_ld{i}") for i in range(2)]
        prep, mm, qk_ok, seq, ac, tr, wt_ok, out = (S("a_" + n) for n in ("prep", "mm", "qk_ok", "seq", "ac", "tr", "wt_ok", "out"))
        block = ctx.enter_context(nc.Block())

        @block.sync
        def _(sp):
            sp.dma_start(wq[:].rearrange("p k d h -> p k (d h)"), wq_dram).then_inc(ld, 16)
            sp.dma_start(w[:, :, QK:NQ], wkv_dram).then_inc(ld, 16)
            sp.dma_start(bq[:].rearrange("p d h -> p (d h)"), b_dram[0].partition_broadcast(P)).then_inc(ld, 16)
            sp.dma_start(bias[:, QK:2 * QK], b_dram[1].partition_broadcast(P)).then_inc(ld, 16)
            sp.dma_start(bias[:, 2 * QK:3 * QK], b_dram[2].partition_broadcast(P)).then_inc(ld, 16)
            sp.dma_start(desc[:], S.desc_dram).then_inc(ld, 16)
            sp.dma_start(ident[:], S.ident_dram).then_inc(ld, 16)
            for n in range(NT):
                if n >= 2:
                    sp.wait_ge(mm, n - 1)
                sp.dma_start(xh[:, n % 2, :, :].bitcast(F32), xnt_dram[n]).then_inc(xh_ld[n % 2], 16)
            sp.wait_ge(seq, O_READY)
            sp.dma_start(o_dram.rearrange("a p d -> p a d"), so[:]).then_inc(out, 16)
            sp.wait_ge(wt_ok, 4)
            sp.dma_start(wt_dram.rearrange("a e t -> e a t"), wt[:]).then_inc(out, 16)
            sp.wait_ge(out, 32)

        def pair(ap):
            return ap.rearrange("p a (d o) -> p a d o", o=1).to_broadcast([P, NT, QK, QK])

        def along(ap):
            return ap.rearrange("p a (o e) -> p a o e", o=1).to_broadcast([P, NT, QK, QK])

        def per_tile(ap):
            return ap.rearrange("p (a o) -> p a o", o=1).to_broadcast([P, NT, EXPERTS])

        @block.vector
        def _(dve):
            dve.wait_ge(ld, 16 * 7)
            dve.tensor_reduce(w[:, :, 0:QK], wq[:], AX_X, ALU.add).then_inc(prep, 1)
            dve.tensor_reduce(bias[:, 0:QK], bq[:], AX_X, ALU.add).then_inc(prep, 1)
            dve.memset(bias[:, 3 * QK:NQ], 0.0).then_inc(prep, 1)
            dve.wait_ge(prep, 3)
            dve.tensor_copy(wr[:, 0], w[:]).then_inc(prep, 1)
            dve.wait_ge(prep, 4)
            dve.tensor_tensor(wr[:, 1], w[:], wr[:, 0].bitcast(F32), ALU.subtract).then_inc(prep, 1)
            for n in range(NT):
                dve.wait_ge(mm, n + 1)
                dve.tensor_tensor(qk[:, n, :], pq[n % 2][:, 0:NQ], bias[:], ALU.add).then_inc(qk_ok, 1)
            dve.wait_ge(qk_ok, NT)
            q, k, v, lg = (qk[:, :, i * QK:(i + 1) * QK] for i in range(4))
            dve.tensor_tensor(sc[:], pair(q), along(k), ALU.mult).then_inc(seq, 1)
            dve.wait_ge(seq, 1)
            dve.tensor_reduce(mx[:], sc[:], AX_X, ALU.max).then_inc(seq, 1)
            dve.wait_ge(seq, 2)
            dve.tensor_tensor(sc[:], sc[:], pair(mx[:]), ALU.subtract).then_inc(seq, 1)
            dve.tensor_reduce(top[:], lg, AX_X, ALU.max).then_inc(seq, 1)
            dve.wait_ge(seq, 4)
            dve.tensor_tensor(pr[:], lg, per_tile(top[:]), ALU.subtract).then_inc(seq, 1)
            dve.wait_ge(ac, 1)
            dve.tensor_reduce(sm[:], sc[:], AX_X, ALU.add).then_inc(seq, 1)
            dve.wait_ge(seq, 6)
            dve.tensor_tensor(sc[:], sc[:], along(v), ALU.mult).then_inc(seq, 1)
            dve.wait_ge(seq, 7)
            dve.tensor_reduce(so[:], sc[:], AX_X, ALU.add).then_inc(seq, 1)
            dve.reciprocal(mx[:], sm[:]).then_inc(seq, 1)
            dve.wait_ge(seq, 9)
            dve.tensor_tensor(so[:], so[:], mx[:], ALU.mult).then_inc(seq, 1)
            dve.wait_ge(ac, 2)
            dve.tensor_reduce(top[:], pr[:], AX_X, ALU.add).then_inc(seq, 1)
            dve.wait_ge(seq, 11)
            dve.reciprocal(top[:], top[:]).then_inc(seq, 1)
            dve.wait_ge(seq, 12)
            dve.tensor_tensor(pr[:], pr[:], per_tile(top[:]), ALU.mult).then_inc(seq, 1)
            n = 13
            first = desc[:].rearrange("p (o e) -> p o e", o=1).to_broadcast([P, NT, EXPERTS])
            for rank, (left, mark) in enumerate(((pr, one), (p2, eq))):
                dve.wait_ge(seq, n)
                dve.tensor_reduce(top[:], left[:], AX_X, ALU.max).then_inc(seq, 1)
                dve.wait_ge(seq, n + 1)
                dve.tensor_tensor(mark[:], left[:], per_tile(top[:]), ALU.is_ge).then_inc(seq, 1)
                dve.wait_ge(seq, n + 2)
                dve.tensor_tensor(mark[:], mark[:], first, ALU.mult).then_inc(seq, 1)
                dve.wait_ge(seq, n + 3)
                dve.tensor_reduce(top[:], mark[:], AX_X, ALU.max).then_inc(seq, 1)
                dve.wait_ge(seq, n + 4)
                dve.tensor_tensor(mark[:], mark[:], per_tile(top[:]), ALU.is_equal).then_inc(seq, 1)
                n += 5
                if rank == 0:
                    dve.wait_ge(seq, n)
                    dve.scalar_tensor_tensor(out=p2[:], in0=one[:], scalar=-4.0, in1=pr[:], op0=ALU.mult, op1=ALU.add).then_inc(seq, 1)
                    n += 1
            dve.wait_ge(seq, n)
            dve.tensor_tensor(one[:], one[:], eq[:], ALU.add).then_inc(seq, 1)
            dve.wait_ge(seq, n + 1)
            dve.tensor_tensor(pr[:], pr[:], one[:], ALU.mult).then_inc(seq, 1)
            dve.wait_ge(seq, n + 2)
            dve.tensor_reduce(top[:], pr[:], AX_X, ALU.add).then_inc(seq, 1)
            dve.wait_ge(seq, n + 3)
            dve.reciprocal(top[:], top[:]).then_inc(seq, 1)
            dve.wait_ge(seq, n + 4)
            dve.tensor_tensor(pr[:], pr[:], per_tile(top[:]), ALU.mult).then_inc(seq, 1)
            assert n + 5 == W_READY
            for j in range(4):
                dve.wait_ge(tr, j + 1)
                dve.tensor_copy(wt[:, 4 * j:4 * j + 4, :].rearrange("e a t -> e (a t)"), pt[j][0:EXPERTS, :]).then_inc(wt_ok, 1)

        @block.scalar
        def _(act):
            act.wait_ge(seq, 3)
            act.activation(sc[:], sc[:], ACT.Exp, scale=float(QK) ** -0.5).then_inc(ac, 1)
            act.wait_ge(seq, 5)
            act.activation(pr[:], pr[:], ACT.Exp).then_inc(ac, 1)

        @block.tensor
        def _(pe):
            pe.wait_ge(prep, 5)
            for n in range(NT):
                pe.wait_ge(xh_ld[n % 2], 16 * (n // 2 + 1))
                if n >= 2:
                    pe.wait_ge(qk_ok, n - 1)
                split3(pe, pq[n % 2][:, 0:NQ], lambda a, k: xh[:, n % 2, a, k * P:(k + 1) * P],
                       lambda a, k: wr[:, a, k, :], KD).then_inc(mm, 1)
            pe.wait_ge(seq, W_READY)
            for j in range(4):
                for c in range(4):
                    last = pe.transpose(pt[j][0:EXPERTS, c * P:(c + 1) * P], pr[:, 4 * j + c, :], ident[:])
                last.then_inc(tr, 1)


O_READY, W_READY = 10, 29



_OUTS = [((4, 512, 512), 'float32')]


class Scope:

    def __init__(self, nc, ctx):
        self.nc, self.ctx = nc, ctx

    def __call__(self, name):
        return self.ctx.enter_context(self.nc.semaphore(name))


def program(nc, ins, out):
    with ExitStack() as ctx:
        S = Scope(nc, ctx)
        S.ident_dram, S.masks_dram, S.eye8_dram = ins["ident"], ins["masks"], ins["eye8"]
        S.desc_dram, S.rep_dram = ins["desc"], ins["rep"]

        def dram(n, s, d=F32):
            return nc.dram_tensor(n, s, d, kind="Internal").ap()

        xnt = dram("xnt", [NT, P, 2, DM])
        par = dram("par", [GROUPS, P, NT, 4, HPG])
        dat = dram("dat", [HEADS, T])
        with nc.sbuf_tensor("dtr", [P, NT, HEADS], F32) as dtr:
            norm_phase(nc, S, ins["x"], xnt, "n0_", ins["wdt"], ins["dt_bias"], dtr)
            step_phase(nc, S, dtr, ins["A_log"], par, dat)
        x0 = ins["x"].rearrange("(a p) d -> a p d", p=P)
        s0, x1, xnt1 = dram("s0", [NT, P, DM]), dram("x1", [NT, P, DM]), dram("xnt1", [NT, P, 2, DM])
        dq_all = dram("dq", [QPIECES, P, QB * BLK])
        ssm_phase(nc, S, xnt, ins["wx"], ins["wg"], ins["ow"], ins["cp"], ins["D"], par, dat, s0, ins["w123"], dq_all)
        flat = dq_all.rearrange("n p k -> (n p k)")
        dq = [flat[i * FF * DM:(i + 1) * FF * DM].rearrange("(r c) -> r c", c=c) for i, c in enumerate((DM, DM, FF))]
        ffn_phase(nc, S, "f_", xnt, FF, dq, x0, s0, x1, True)
        norm_phase(nc, S, x1.rearrange("a p d -> (a p) d"), xnt1, "n1_")
        o1, wt1 = dram("o1", [NT, P, QK]), dram("wt1", [NT, EXPERTS, P])
        attention_phase(nc, S, xnt1, ins["wq"], ins["wkvr"], (ins["bq"], ins["bk"], ins["bv"]), o1, wt1)
        ffn_phase(nc, S, "e_", xnt1, MF, (ins["eg"], ins["eu"], ins["ed"]), x1, o1,
                  out.rearrange("b (a p) d -> (b a) p d", p=P), False, wt1)


def kernel(**inputs):
    import concourse.bacc as _bacc
    from concourse import mybir as _mybir
    from concourse.bass_utils import run_bass_kernel_spmd as _run

    f = {k: np.asarray(v) for k, v in inputs.items()}
    a = {"x": f["L0_attn_hidden_states"].reshape(T, DM)}
    w = f["L0_attn_in_proj_w"].T
    inner = HEADS * HD
    kd = lambda m: m.reshape(m.shape[0] // P, P, m.shape[1]).transpose(1, 0, 2)
    gate, xb = w[:, :inner], w[:, inner:2 * inner]
    bb, cc, dt = w[:, 2 * inner:2 * inner + GROUPS * P], w[:, 2 * inner + GROUPS * P:-HEADS], w[:, -HEADS:]
    a["wx"] = np.stack([kd(np.concatenate([xb[:, g * 512:(g + 1) * 512], bb[:, g * P:(g + 1) * P], cc[:, g * P:(g + 1) * P]], 1))
                        .reshape(P, KD, XBC, P).transpose(2, 0, 1, 3).reshape(XBC, P, KD * P) for g in range(GROUPS)])
    a["wg"] = np.stack([kd(gate[:, g * 512:(g + 1) * 512]) for g in range(GROUPS)])
    a["wdt"] = kd(dt)
    cw = np.concatenate([f["L0_attn_conv_weight"], f["L0_attn_conv_bias"][:, None]], 1)
    a["cp"] = np.stack([np.concatenate([cw[g * 512:(g + 1) * 512], cw[inner + g * P:inner + (g + 1) * P],
                                        cw[inner + (GROUPS + g) * P:inner + (GROUPS + g + 1) * P]]).reshape(XBC, P, 5).transpose(1, 0, 2)
                        for g in range(GROUPS)])
    owt = np.concatenate([f["L0_attn_out_proj_w"].T, f["L0_attn_norm_weight"][:, None]], 1)
    a["ow"] = np.stack([kd(owt[g * 512:(g + 1) * 512]) for g in range(GROUPS)])
    a["dt_bias"], a["A_log"], a["D"] = f["L0_attn_dt_bias"], f["L0_attn_A_log"], f["L0_attn_D"]
    w123 = np.zeros(QPIECES * P * QB * BLK, np.float32)
    w123[:3 * FF * DM] = np.concatenate([f["L0_ffn_w1"].ravel(), f["L0_ffn_w2"].ravel(), f["L0_ffn_w3"].ravel()])
    a["w123"] = w123.reshape(QPIECES, P, QB * BLK)
    a["wq"] = kd(f["L1_attn_Wq"].reshape(DM, DM))
    a["wkvr"] = kd(np.concatenate([f["L1_attn_Wk"][..., 0], f["L1_attn_Wv"][..., 0], f["L1_ffn_gate_w"].T], 1))
    a["bq"], a["bk"], a["bv"] = f["L1_attn_bq"].reshape(DM), f["L1_attn_bk"].reshape(QK), f["L1_attn_bv"].reshape(QK)
    a["eg"], a["eu"], a["ed"] = kd(f["L1_ffn_g"].T), kd(f["L1_ffn_u"].T), kd(f["L1_ffn_d"].T)
    a["desc"] = np.tile(np.arange(EXPERTS, 0, -1, dtype=np.float32), (P, 1))
    a["rep"] = np.repeat(np.eye(EXPERTS, dtype=np.float32), INTER, 1)
    eye = np.eye(P, dtype=np.float32)
    i = np.arange(P)
    a["ident"] = eye
    a["eye8"] = np.repeat(eye[:, None, :], HPG, 1)
    a["masks"] = np.stack([eye, (i[:, None] <= i[None]).astype(np.float32), (i[:, None] > i[None]).astype(np.float32),
                           np.ones((P, P), np.float32)], 1)
    nc = _bacc.Bacc("TRN2", target_bir_lowering=False, num_devices=1)
    arrays, ins = {}, {}
    for name, v in a.items():
        v = np.ascontiguousarray(v)
        arrays[f"in_{name}_dram"] = v
        ins[name] = nc.dram_tensor(f"in_{name}_dram", v.shape, _mybir.dt.from_np(v.dtype), kind="ExternalInput").ap()
    shape, dtype = _OUTS[0]
    out = nc.dram_tensor("out_0_dram", shape, _mybir.dt.from_np(np.dtype(dtype)), kind="ExternalOutput").ap()
    program(nc, ins, out)
    r = _run(nc, [arrays], core_ids=[0])
    return r.results[0]["out_0_dram"]
```

```python
from contextlib import ExitStack

import concourse.bass as bass
import numpy as np
from concourse import mybir

F32 = mybir.dt.float32
F32R = mybir.dt.float32r
ALU = mybir.AluOpType
ACT = mybir.ActivationFunctionType
AX_X = mybir.AxisListType.X

P = 128
T = 2048
DM = 512
KD = DM // P
SEQ = 512
NT = T // P
HEADS, HD, GROUPS = 64, 64, 8
HPG = HEADS // GROUPS
XBC = 6
HALVES = 2
HT = T // HALVES
SLOTS = HT // P
EPS = 1e-5
DT_, WDT_, EXC_, TOT_ = range(4)

NF4 = [-1.0, -0.6961928009986877, -0.5250730514526367, -0.39491748809814453, -0.28444138169288635,
       -0.18477343022823334, -0.09105003625154495, 0.0, 0.07958029955625534, 0.16093020141124725,
       0.24611230194568634, 0.33791524171829224, 0.44070982933044434, 0.5626170039176941,
       0.7229568362236023, 1.0]
BLK = 64
FF = 1376
QB = 9
QPIECES = 32
assert QPIECES * P * QB * BLK >= 3 * FF * DM
EXPERTS, INTER = 16, 56
MF = EXPERTS * INTER
MT = MF // P
QK = 16
NQ = 4 * QK
assert NQ == HEADS


def split3(pe, out, stat, mov, kt):
    n = 0
    for k in range(kt):
        for a, b in ((0, 0), (0, 1), (1, 0)):
            last = pe.matmul(out, stat(a, k), mov(b, k), start=(n == 0), stop=(n == 3 * kt - 1))
            n += 1
    return last


def plain_wait(eng, met_sem, met, sem, value):
    if isinstance(value, int):
        eng.wait_ge(sem, value)
        return
    eng.compute_val(value)
    eng.wait_ge(met_sem, met)
    eng.wait_ge(sem, value)


def start_at_one(eng, *sems):
    for sem in sems:
        eng.sem_inc(sem, 1)


def norm_phase(nc, S, src_dram, xnt_dram, tag, w_dram, b_drams, proj, head_drams=None):
    with ExitStack() as ctx:
        def sb(n, s, d=F32):
            return ctx.enter_context(nc.sbuf_tensor(tag + n, s, d))

        def sem(n):
            return S(tag + n)

        x = sb("x", [P, 4, DM])
        stat = sb("stat", [P, 2, 6])
        mv = sb("mv", [P, 2, 2])
        ve = sb("ve", [P, 2, 1])
        rstd = sb("rstd", [P, 2, 1])
        half = sb("half", [P, 1])
        xn = sb("xn", [P, 2, DM])
        xh = sb("xh", [P, 2, 2, DM], F32R)
        ident = sb("ident", [P, P])
        tp = [ctx.enter_context(nc.psum_tensor(f"{tag}tp{i}", [P, DM], F32)) for i in range(2)]
        wraw = sb("wraw", [P, KD, NQ])
        wsp = sb("wsp", [P, KD, 2, NQ], F32R)
        bias = sb("bias", [P, NQ])
        part = sb("part", [P, 2, NQ])
        if head_drams is not None:
            wq = sb("wq", [P, KD, QK, DM // QK])
            bq = sb("bq", [P, QK, DM // QK])
        pd = [ctx.enter_context(nc.psum_tensor(f"{tag}pd{i}", [P, 512], F32)) for i in range(2)]
        CONSTS = 16 * (1 + len(b_drams) + (2 if head_drams is not None else 0))
        LO = 0 if head_drams is None else QK
        loaded = [sem(f"loaded{i}") for i in range(4)]
        const_ld, id_ld = sem("const_ld"), sem("id_ld")
        wsplit, p_mm, p_sum = sem("wsplit"), sem("p_mm"), sem("p_sum")
        stats, mean_var, var_eps, rstd_ok = sem("stats"), sem("mean_var"), sem("var_eps"), sem("rstd_ok")
        normed, turned, hi_ok, lo_ok = sem("normed"), sem("turned"), sem("hi_ok"), sem("lo_ok")
        stored = [sem(f"stored{i}") for i in range(2)]
        block = ctx.enter_context(nc.Block())

        def walk(eng, step, last):
            step(0, 0, 0)
            step(1, 0, 1)
            with eng.Fori(0, NT // 4 - 1) as i:
                for k in range(2, 6):
                    step(4 * i + k, i, k)
            for k in range(2, 4):
                step(NT - 4 + k, NT // 4 - 1, k)
            last(NT, NT // 4 - 1, 4)

        @block.sync
        def _(sp):
            sp.dma_start(x[:, 0, :], src_dram[0:P, :]).then_inc(loaded[0], 16)
            sp.dma_start(ident[:], S.ident_dram).then_inc(id_ld, 16)
            for r in range(1, 4):
                sp.dma_start(x[:, r, :], src_dram[r * P:(r + 1) * P, :]).then_inc(loaded[r], 16)
            sp.dma_start(wraw[:, :, LO:], w_dram).then_inc(const_ld, 16)
            for j, b_dram in enumerate(b_drams):
                n = b_dram.shape[0]
                sp.dma_start(bias[:, LO + j * n:LO + j * n + n], b_dram.partition_broadcast(P)).then_inc(const_ld, 16)
            if head_drams is not None:
                sp.dma_start(wq[:].rearrange("p k d h -> p k (d h)"), head_drams[0]).then_inc(const_ld, 16)
                sp.dma_start(bq[:].rearrange("p d h -> p (d h)"), head_drams[1].partition_broadcast(P)).then_inc(const_ld, 16)

            def store(n, k):
                plain_wait(sp, id_ld, 16, lo_ok, n)
                sp.dma_start(xnt_dram[n - 1], xh[:, (k - 1) % 2, :, :].bitcast(F32)).then_inc(stored[(k - 1) % 2], 16)

            def step(n, i, k):
                if k > 0:
                    if not isinstance(n, int):
                        plain_wait(sp, id_ld, 16, normed, n - 1)
                        sp.dma_start(x[:, (k + 2) % 4, :], src_dram[bass.ds((n + 2) * P, P), :]).then_inc(loaded[(k + 2) % 4], 16)
                    store(n, k)

            walk(sp, step, lambda n, i, k: store(n, k))
            for r in range(2):
                sp.wait_ge(stored[r], 16 * NT // 2 + 1)

        @block.gpsimd
        def _(pool):
            pool.memset(half[:], -0.5).then_inc(var_eps, 1)
            pool.wait_ge(var_eps, 1)
            with pool.Fori(0, NT // 2) as i:
                for r in range(2):
                    plain_wait(pool, var_eps, 1, mean_var, 2 * i + r + 1)
                    pool.tensor_scalar(ve[:, r, :], mv[:, r, 1:2], EPS, 1.0, ALU.add, ALU.mult).then_inc(var_eps, 1)
                    pool.wait_ge(var_eps, 2 * i + r + 2)
                    pool.tensor_tensor(rstd[:, r, :], ve[:, r, :], half[:], ALU.pow).then_inc(rstd_ok, 1)

        @block.vector
        def _(dve):
            def step(n, i, k):
                r = k % 2
                dve.wait_ge(loaded[k % 4], 16 * (i + k // 4) + 16)
                dve.bn_stats(stat[:, r, :], x[:, k % 4, :]).then_inc(stats, 1)
                plain_wait(dve, loaded[0], 16, stats, n + 1)
                dve.bn_aggr(mv[:, r, :], stat[:, r, :]).then_inc(mean_var, 1)
                if k > 0:
                    low_part(n, k)
                dve.wait_ge(rstd_ok, n + 1)
                dve.tensor_scalar(xn[:, r, :], x[:, k % 4, :], mv[:, r, 0:1], rstd[:, r, :],
                                  ALU.subtract, ALU.mult).then_inc(normed, 1)
                if k > 1:
                    out_part(n - 1, k - 1)
                if k == 1:
                    split_weights()

            def split_weights():
                dve.wait_ge(const_ld, CONSTS)
                if head_drams is not None:
                    dve.tensor_reduce(wraw[:, :, 0:QK], wq[:], AX_X, ALU.add).then_inc(wsplit, 1)
                    dve.tensor_reduce(bias[:, 0:QK], bq[:], AX_X, ALU.add).then_inc(wsplit, 1)
                    dve.memset(bias[:, LO + len(b_drams) * QK:], 0.0).then_inc(wsplit, 1)
                    dve.wait_ge(wsplit, 3)
                done = 3 if head_drams is not None else 0
                dve.tensor_copy(wsp[:, :, 0, :], wraw[:]).then_inc(wsplit, 1)
                dve.wait_ge(wsplit, done + 1)
                dve.tensor_tensor(wsp[:, :, 1, :], wraw[:], wsp[:, :, 0, :].bitcast(F32), ALU.subtract).then_inc(wsplit, 1)

            def low_part(n, k):
                r = (k - 1) % 2
                dve.wait_ge(turned, n)
                dve.wait_ge(hi_ok, n)
                dve.tensor_tensor(xh[:, r, 1, :], tp[r][:], xh[:, r, 0, :].bitcast(F32), ALU.subtract).then_inc(lo_ok, 1)

            def out_part(n, k):
                r, row = (k - 1) % 2, lambda ap: ap.rearrange("p (o h) -> p o h", o=1)
                dve.wait_ge(p_mm, n)
                dve.tensor_tensor(part[:, r, :], pd[r][:, 0:NQ], bias[:], ALU.add).then_inc(p_sum, 1)
                dve.wait_ge(p_sum, n)
                dve.tensor_tensor(proj[:, bass.ds(n - 1, 1), :], row(part[:, r, :]), row(pd[r][:, NQ:2 * NQ]), ALU.add)

            def last(n, i, k):
                low_part(n, k)
                out_part(n - 1, k - 1)
                out_part(n, k)

            walk(dve, step, last)

        @block.scalar
        def _(act):
            start_at_one(act, *stored)
            with act.Fori(0, NT // 2) as i:
                for r in range(2):
                    act.wait_ge(turned, 2 * i + r + 1)
                    act.wait_ge(stored[r], 16 * i + 1)
                    act.activation(xh[:, r, 0, :], tp[r][:], ACT.Copy).then_inc(hi_ok, 1)

        @block.tensor
        def _(pe):
            def project(n, k):
                pe.wait_ge(lo_ok, n)
                r, both = (k - 1) % 2, 2 * NQ
                for j in range(KD):
                    pe.matmul(pd[r][:, 0:both], xh[:, r, 0, j * P:(j + 1) * P], wsp[:, j].rearrange("p b n -> p (b n)"),
                              start=(j == 0), stop=False)
                for j in range(KD):
                    last = pe.matmul(pd[r][:, 0:NQ], xh[:, r, 1, j * P:(j + 1) * P], wsp[:, j, 0, :],
                                     start=False, stop=(j == KD - 1))
                last.then_inc(p_mm, 1)

            def step(n, i, k):
                pe.wait_ge(normed, n + 1)
                for j in range(KD):
                    last = pe.transpose(tp[k % 2][:, j * P:(j + 1) * P], xn[:, k % 2, j * P:(j + 1) * P], ident[:])
                last.then_inc(turned, 1)
                if k == 1:
                    pe.wait_ge(wsplit, 2 if head_drams is None else 5)
                if k > 0:
                    project(n, k)

            pe.wait_ge(id_ld, 16)
            walk(pe, step, lambda n, i, k: project(n, k))


def step_phase(nc, S, dtr, alog_dram, par_dram, dat_dram):
    with ExitStack() as ctx:
        def sb(n, s, d=F32):
            return ctx.enter_context(nc.sbuf_tensor("st_" + n, s, d))

        N = NT * HEADS
        z = dtr[:].rearrange("p a h -> p (a h)")
        e, u, t1, t2, dt, a = (sb(n, [P, N]) for n in ("e", "u", "t1", "t2", "dt", "a"))
        al, an = sb("al", [P, HEADS]), sb("an", [P, HEADS])
        par = sb("par", [P, GROUPS, NT, 4, HPG])
        masks = sb("masks", [P, 4, P])
        dat = sb("dat", [HEADS, NT, P])
        pc = [ctx.enter_context(nc.psum_tensor(f"st_pc{i}", [P, 512], F32)) for i in range(6)]
        pt = [ctx.enter_context(nc.psum_tensor(f"st_pt{i}", [P, 512], F32)) for i in range(2)]
        ld, v, ac, mm, tr, dtc, out = (S("st_" + n) for n in ("ld", "v", "ac", "mm", "tr", "dtc", "out"))
        block = ctx.enter_context(nc.Block())

        def by_head(t):
            return t[:].rearrange("p (a g h) -> p a g h", a=NT, g=GROUPS)

        def par_of(i, lo=0, n=NT):
            return par[:, :, lo:lo + n, i, :].rearrange("p g a h -> p a g h")

        @block.sync
        def _(sp):
            sp.dma_start(al[:], alog_dram.partition_broadcast(P)).then_inc(ld, 16)
            sp.dma_start(masks[:], S.masks_dram).then_inc(ld, 16)
            sp.wait_ge(dtc, 5)
            sp.dma_start(dat_dram, dat[:].rearrange("h a t -> h (a t)")).then_inc(out, 16)
            sp.wait_ge(v, 13)
            sp.wait_ge(ac, 10)
            sp.dma_start(par_dram.rearrange("g p a k h -> p g (a k h)"),
                         par[:].rearrange("p g a k h -> p g (a k h)")).then_inc(out, 16)
            sp.wait_ge(out, 32)

        @block.vector
        def _(dve):
            dve.tensor_scalar(t1[:], z, -1.0, None, ALU.mult).then_inc(v, 1)
            dve.wait_ge(v, 1)
            dve.tensor_tensor(t1[:], t1[:], z, ALU.min).then_inc(v, 1)
            dve.wait_ge(ac, 1)
            dve.tensor_scalar(u[:], e[:], 1.0, None, ALU.add).then_inc(v, 1)
            dve.wait_ge(v, 3)
            dve.tensor_scalar(t2[:], u[:], -1.0, None, ALU.add).then_inc(v, 1)
            dve.wait_ge(v, 4)
            dve.tensor_tensor(t2[:], e[:], t2[:], ALU.subtract).then_inc(v, 1)
            dve.reciprocal(t1[:], u[:]).then_inc(v, 1)
            dve.wait_ge(v, 6)
            dve.tensor_tensor(t2[:], t2[:], t1[:], ALU.mult).then_inc(v, 1)
            dve.wait_ge(v, 7)
            dve.wait_ge(ac, 2)
            dve.tensor_tensor(t2[:], t2[:], dt[:], ALU.add).then_inc(v, 1)
            dve.wait_ge(v, 8)
            dve.scalar_tensor_tensor(out=dt[:], in0=z, scalar=0.0, in1=t2[:], op0=ALU.max, op1=ALU.add).then_inc(v, 1)
            dve.wait_ge(ac, 3)
            dve.tensor_scalar(al[:], an[:], -1.0, None, ALU.mult).then_inc(v, 1)
            dve.wait_ge(v, 10)
            dve.tensor_tensor(a[:].rearrange("p (a h) -> p a h", a=NT), dt[:].rearrange("p (a h) -> p a h", a=NT),
                              al[:].rearrange("p (o h) -> p o h", o=1).to_broadcast([P, NT, HEADS]), ALU.mult).then_inc(v, 1)
            dve.tensor_copy(par_of(DT_), by_head(dt)).then_inc(v, 1)
            for j in range(4):
                dve.wait_ge(tr, j + 1)
                dve.tensor_copy(dat[:, 4 * j:4 * j + 4, :].rearrange("h a t -> h (a t)"), pt[j % 2][0:HEADS, :]).then_inc(dtc, 1)
            dve.wait_ge(dtc, 4)
            dve.memset(dat[:, :, 0:1], 0.0).then_inc(dtc, 1)
            dve.wait_ge(ac, 6)
            dve.tensor_tensor(par_of(WDT_), by_head(t1), by_head(dt), ALU.mult).then_inc(v, 1)

        @block.scalar
        def _(act):
            act.wait_ge(v, 2)
            act.activation(e[:], t1[:], ACT.Exp).then_inc(ac, 1)
            act.wait_ge(v, 3)
            act.activation(dt[:], u[:], ACT.Ln).then_inc(ac, 1)
            act.wait_ge(ld, 32)
            act.activation(an[:], al[:], ACT.Exp).then_inc(ac, 1)
            act.wait_ge(v, 11)
            act.activation(e[:], a[:], ACT.Exp).then_inc(ac, 1)
            act.wait_ge(mm, 2)
            for h in range(2):
                act.activation(t1[:, h * 512:(h + 1) * 512], pc[h][:], ACT.Exp).then_inc(ac, 1)
            for i, kind in ((2, EXC_), (4, TOT_)):
                act.wait_ge(mm, i + 2)
                for h in range(2):
                    act.activation(par_of(kind, 8 * h, 8), pc[i + h][:].rearrange("p (a g h) -> p a g h", a=8, g=GROUPS),
                                   ACT.Exp).then_inc(ac, 1)

        @block.tensor
        def _(pe):
            pe.wait_ge(ld, 32)
            pe.wait_ge(v, 11)
            for i, m in ((0, 2), (2, 1), (4, 3)):
                for h in range(2):
                    pe.matmul(pc[i + h][:], masks[:, m, :], a[:, h * 512:(h + 1) * 512], start=True, stop=True).then_inc(mm, 1)
            pe.wait_ge(ac, 4)
            for j in range(4):
                if j >= 2:
                    pe.wait_ge(dtc, j - 1)
                for i in range(4):
                    last = pe.transpose(pt[j % 2][0:HEADS, i * P:(i + 1) * P],
                                        e[:, (4 * j + i) * HEADS:(4 * j + i + 1) * HEADS], masks[:, 0, :])
                last.then_inc(tr, 1)


PLAN = [([("x", 0)], [("x", 1)]), ([("x", 2), ("g", 3)], [("x", 3)]), ([("x", 4), ("x", 5)], [("g", 4)]),
        ([("g", 5)], [("g", 6)]), ([("g", 7), ("x", 0)], [("x", 1)]), ([("x", 2), ("x", 3)], [("x", 4)]),
        ([("x", 5)], [("g", 0)]), ([("g", 1)], [("g", 2)])]
GATES_AHEAD = 3
X_SPLIT, G_SPLIT = {2: (0, 1), 3: (2, 3), 4: (4, 5)}, {5: (0, 1), 6: (2, 3)}


def ssm_phase(nc, S, xnt_dram, wx_dram, wg_dram, ow_dram, cp_dram, d_dram, par_dram, dat_dram, s_dram, q_src, q_dst):
    with ExitStack() as ctx:
        def sb(n, s, d=F32):
            return ctx.enter_context(nc.sbuf_tensor("m_" + n, s, d))

        def ps(n):
            return ctx.enter_context(nc.psum_tensor("m_" + n, [P, 512], F32))

        def sem(n):
            return S("m_" + n)

        xn = sb("xn", [P, 2, KD, HT], F32R)
        wx = sb("wx", [P, 2, XBC, KD * P], F32R)
        wg = sb("wg", [P, 2, KD, 512], F32R)
        ow = sb("ow", [P, 2, KD, DM], F32R)
        raw = sb("raw", [P, 2, DM + 1])
        cp = sb("cp", [P, XBC, 5])
        par = sb("par", [P, 2, 4, 4, HPG])
        dpar = sb("dpar", [P, 2, HPG])
        cv = sb("cv", [P, 2, XBC, SEQ])
        sg = sb("sg", [P, 4, 512])
        dab = sb("dab", [P, 2, HPG * P])
        dec = sb("dec", [P, 2, HPG * P])
        eye8 = sb("eye8", [P, HPG, P])
        xs, dtx, xw, xd = (sb(n, [P, 2, 512]) for n in ("xs", "dtx", "xw", "xd"))
        bt = sb("bt", [P, 2, P])
        state = sb("state", [P, 512])
        t1 = sb("t1", [P, 512])
        y = sb("y", [P, 2, 512])
        junk = sb("junk", [P, 512])
        yt = sb("yt", [P, 2, KD * P], F32R)
        ss = sb("ss", [P, 2])
        ve = sb("ve", [P, 2])
        rs = sb("rs", [P, 2])
        half = sb("half", [P, 1])
        sacc = sb("sacc", [P, SLOTS, DM])
        q_w, q_mask = (sb(n, [P, 2, QB, BLK]) for n in ("q_w", "q_mask"))
        q_acc, q_res = (sb(n, [P, QB, BLK]) for n in ("q_acc", "q_res"))
        q_max, q_safe, q_inv = (sb(n, [P, QB]) for n in ("q_max", "q_safe", "q_inv"))
        ident = eye8[:, 0, :]

        p_in = [ps("p_in0"), ps("p_in1")]
        p_gate, p_turn, p_bg, p_yi, p_ye, p_ou = (ps(n) for n in ("p_gate", "p_turn", "p_bg", "p_yi", "p_ye", "p_ou"))

        eye_ld, cp_ld = sem("eye_ld"), sem("cp_ld")
        xn_ld = [sem(f"xn_ld{i}") for i in range(2)]
        raw_ld = [sem(f"raw_ld{i}") for i in range(2)]
        first_ld = [sem(f"first_ld{i}") for i in range(3)]
        w_hi, w_lo, o_lo = sem("w_hi"), sem("w_lo"), sem("o_lo")
        par_ld = [sem(f"par_ld{i}") for i in range(2)]
        dab_ld = [sem(f"dab_ld{i}") for i in range(2)]
        in_done, cev, ctap, silu_cv = sem("in_done"), sem("cev"), sem("ctap"), sem("silu_cv")
        a_done, xs_done, bt_done = sem("a_done"), sem("xs_done"), sem("bt_done")
        dtx_done, scan_done, m_done = sem("dtx_done"), sem("scan_done"), sem("m_done")
        xw_done, xd_done = sem("xw_done"), sem("xd_done")
        b_done, st_done, s_done = sem("b_done"), sem("st_done"), sem("s_done")
        t1_done, y0_done, y_done = sem("t1_done"), sem("y0_done"), sem("y_done")
        sq_done, ve_done, rs_done = sem("sq_done"), sem("ve_done"), sem("rs_done")
        g_done, sg_done, yn_done = sem("g_done"), sem("sg_done"), sem("yn_done")
        c_done, hi_done, lo_done, d_done = sem("c_done"), sem("hi_done"), sem("lo_done"), sem("d_done")
        sacc_done, sacc_zero, s_stored, half_ok = sem("sacc_done"), sem("sacc_zero"), sem("s_stored"), sem("half_ok")
        q_ld = [sem(f"q_ld{i}") for i in range(2)]
        q_seq, q_above, q_add, q_done, q_st = (sem(n) for n in ("q_seq", "q_above", "q_add", "q_done", "q_st"))
        block = ctx.enter_context(nc.Block())

        code = np.array(NF4, np.float32)
        bound = (code[:-1] + code[1:]) * np.float32(0.5)
        QM = len(bound) - 1
        q_plan = [((), (1, 2)), ((3, 4), (5, 6)), ((7, 8), (9, 10)), ((11, 12), (13, 14))]

        GU, GQ = SLOTS, 2
        HU, HQ = GROUPS * GU, GROUPS * GQ
        OWP, WP = KD, XBC + KD
        GP = OWP + WP

        def walk(eng, prologue, slot, drain):
            prologue()
            slot(0, 0, 0, "first")
            for hf in range(HALVES):
                with eng.Fori(0, GROUPS - 1) as g:
                    for s in range(1, SLOTS):
                        slot(hf, g, s, "")
                    slot(hf, g + 1, 0, "")
                for s in range(1, SLOTS):
                    slot(hf, GROUPS - 1, s, "last" if hf == HALVES - 1 else "switch")
                if hf < HALVES - 1:
                    slot(hf + 1, 0, 0, "head")
            drain(HALVES * HU - 1)

        def at(hf, g, s):
            return hf * HU + g * GU + s, hf * HQ + g * GQ + s // 4, hf * GROUPS + g

        def after(hf, g, kind):
            return (hf + 1, 0) if kind == "switch" else (hf, g + 1)

        def plan(s, kind):
            return [[w for w in part if not (kind == "last" and (s >= 5 or (s == 4 and w[0] == "x")))] for part in PLAN[s]]

        def gates_before(it, s, w):
            return GU * (it + (1 if s >= 6 else 0)) + w

        def has_next(s, kind):
            return not (kind == "last" and s == SLOTS - 1)

        def bc(ap, n):
            return ap.rearrange("p (a o) -> p a o", o=1).to_broadcast([P, ap.shape[1], n])

        def heads(ap):
            return ap.rearrange("p (h d) -> p h d", h=HPG)

        FIRST = 8

        def loaded(it, i):
            if it is None and i < FIRST:
                return first_ld[0 if i < 2 else 1 if i < XBC else 2], 16, sacc[:, i, :]
            count = 16 * (1 if it is None else GP // 2 * it + 1 + i // 2 + 1)
            return raw_ld[i % 2], count, raw[:, i % 2, :]

        def piece_of(it, i):
            i, before = (i, 0) if it is None else (i - OWP, WP * it + WP)
            dst = wx[:, :, i, :] if i < XBC else wg[:, :, i - XBC, :]
            return dst, before + i

        def split_at(s, kind):
            return [] if kind == "last" else [OWP + j for j in X_SPLIT.get(s, ())] + [OWP + XBC + j for j in G_SPLIT.get(s, ())]

        @block.sync
        def _(sp):
            start_at_one(sp, s_stored, q_st)

            def load_dab(hf, g, s):
                sp.dma_start(dab[:, s % 2, :].rearrange("p (h t) -> p h t", h=HPG),
                             dat_dram[bass.ds(g * HPG, HPG), bass.ds(hf * HT + s * P, P)].partition_broadcast(P))\
                    .then_inc(dab_ld[s % 2], 16)

            def load_par(hf, g, b):
                sp.dma_start(par[:, b, :, :, :].rearrange("p a k h -> p (a k h)"),
                             par_dram[g, :, bass.ds(hf * SLOTS + 4 * b, 4), :, :].rearrange("p a k h -> p (a k h)"))\
                    .then_inc(par_ld[b], 16)
                sp.dma_start(dpar[:, b, :], d_dram[bass.ds(g * HPG, HPG)].partition_broadcast(P)).then_inc(par_ld[b], 16)

            def load_xn(hf, b):
                for s in range(4 * b, 4 * b + 4):
                    sp.dma_start(xn[:, :, :, s * P:(s + 1) * P].bitcast(F32),
                                 xnt_dram[hf * SLOTS + s].rearrange("p a (k t) -> p a k t", k=KD)).then_inc(xn_ld[b], 16)

            def piece(it, i, src):
                if it is None:
                    pass
                elif i < 2:
                    plain_wait(sp, eye_ld, 16, w_lo, WP * it + WP - 1 + i + 1)
                elif i < OWP + 2:
                    plain_wait(sp, eye_ld, 16, o_lo, OWP * it + i - 1 + 1)
                else:
                    plain_wait(sp, eye_ld, 16, w_lo, WP * it + WP + i - OWP - 1 + 1)
                sp.dma_start(raw[:, i % 2, 0:src.shape[-1]], src).then_inc(raw_ld[i % 2], 16)

            def store_sum(hf, s, v):
                sp.wait_ge(sacc_done, v + 2)
                sp.wait_ge(s_stored, 16 * (hf * SLOTS + s) + 1)
                sp.dma_start(s_dram[hf * SLOTS + s], sacc[:, s, :]).then_inc(s_stored, 16)

            def prologue():
                sp.dma_start(sacc[:, 0:2, :], wx_dram[0, 0:2].rearrange("j p c -> p j c")).then_inc(first_ld[0], 16)
                load_xn(0, 0)
                sp.dma_start(sacc[:, 2:XBC, :], wx_dram[0, 2:XBC].rearrange("j p c -> p j c")).then_inc(first_ld[1], 16)
                sp.dma_start(cp[:], cp_dram[0]).then_inc(cp_ld, 16)
                sp.dma_start(eye8[:], S.eye8_dram).then_inc(eye_ld, 16)
                sp.dma_start(sacc[:, XBC:FIRST, :], wg_dram[0, :, 0:FIRST - XBC, :]).then_inc(first_ld[2], 16)
                for i in range(FIRST, WP):
                    piece(None, i, wg_dram[0, :, i - XBC, :])
                load_dab(0, 0, 0)
                load_dab(0, 0, 1)
                load_par(0, 0, 0)
                sp.dma_start(q_w[:, 0, :, :].rearrange("p b k -> p (b k)"), q_src[0]).then_inc(q_ld[0], 16)
                sp.wait_ge(scan_done, 1 + 1)
                load_dab(0, 0, 2)
                load_xn(0, 1)

            def slot(hf, g, s, kind):
                u, q, it = at(hf, g, s)
                hn, gn = after(hf, g, kind)
                if s == 1:
                    for i in range(2, OWP):
                        piece(it, i, ow_dram[g, :, i, :])
                if not (kind == "last" and s >= SLOTS - 3):
                    plain_wait(sp, eye_ld, 16, scan_done, u + 3)
                    load_dab(*((hf, g, s + 3) if s + 3 < SLOTS else (hn, gn, s + 3 - SLOTS)))
                if s == 1 or (s == 5 and kind != "last"):
                    plain_wait(sp, eye_ld, 16, yn_done, u)
                    load_par(*((hf, g, 1) if s == 1 else (hn, gn, 0)))
                if s == 0:
                    for i in range(2):
                        piece(it, i, ow_dram[g, :, i, :])
                if kind == "switch" and s in (2, 5):
                    sp.wait_ge(g_done, GU * it + (4 if s == 2 else 8) + 1)
                    sp.wait_ge(in_done, XBC * (GQ * it + (1 if s == 2 else 2)) + 1)
                    load_xn(hn, s // 4)
                if kind != "last":
                    if s == 3:
                        plain_wait(sp, eye_ld, 16, ctap, 3 * XBC * (q + 2) + 1)
                        sp.dma_start(cp[:], cp_dram[gn]).then_inc(cp_ld, 16)
                    for i in split_at(s + 1, kind):
                        piece(it, i, wx_dram[gn, i - OWP] if i < OWP + XBC else wg_dram[gn, :, i - OWP - XBC, :])
                if s % 4 == 0:
                    n, m = 2 * it + s // 4, 1 - s // 4
                    if kind != "first":
                        plain_wait(sp, eye_ld, 16, q_done, n + 1)
                        sp.dma_start(q_dst[n - 1], q_res[:].rearrange("p b k -> p (b k)")).then_inc(q_st, 16)
                    if not (kind == "last" and s == 4):
                        sp.dma_start(q_w[:, m, :, :].rearrange("p b k -> p (b k)"), q_src[n + 1]).then_inc(q_ld[m], 16)
                if kind in ("switch", "last") and s >= 2:
                    store_sum(hf, s - 2, u - 2)
                if kind == "head":
                    store_sum(hf - 1, SLOTS - 2, u - 2)
                    store_sum(hf - 1, SLOTS - 1, u - 1)

            def drain(v):
                sp.wait_ge(q_done, QPIECES + 1)
                sp.dma_start(q_dst[QPIECES - 1], q_res[:].rearrange("p b k -> p (b k)")).then_inc(q_st, 16)
                for s in (SLOTS - 2, SLOTS - 1):
                    store_sum(HALVES - 1, s, v - (SLOTS - 1 - s))

            walk(sp, prologue, slot, drain)
            sp.wait_ge(s_stored, 16 * NT + 1)
            sp.wait_ge(q_st, 16 * QPIECES + 1)

        @block.gpsimd
        def _(pool):
            start_at_one(pool, q_add, w_lo, xw_done, xd_done, st_done, y_done, ve_done, rs_done)
            pool.memset(half[:], -0.5).then_inc(half_ok, 1)
            pool.wait_ge(half_ok, 1)

            def low_piece(it, i):
                dst, n = piece_of(it, i)
                plain_wait(pool, half_ok, 1, w_hi, i + 1 if it is None else GP * it + WP + i + 1)
                pool.tensor_tensor(dst[:, 1], loaded(it, i)[2][:, 0:DM], dst[:, 0].bitcast(F32), ALU.subtract).then_inc(w_lo, 1)

            def q_adds(it, s, place):
                for j in q_plan[s % 4][place]:
                    m = QM * (2 * it + s // 4) + j - 1
                    pool.wait_ge(q_above, m + 2)
                    pool.wait_ge(q_add, m + 1)
                    pool.tensor_tensor(q_acc[:], q_acc[:], q_mask[:, j % 2, :, :], ALU.add).then_inc(q_add, 1)

            def x_parts(u, it, s):
                b, c, r = s // 4, s % 4, s % 2
                if c == 0:
                    pool.wait_ge(par_ld[b], 32 * it + 32)
                pool.wait_ge(xs_done, u + 2)
                pool.tensor_tensor(heads(xw[:, r, :]), heads(xs[:, r, :]), bc(par[:, b, c, WDT_, :], HD), ALU.mult).then_inc(xw_done, 1)
                pool.tensor_tensor(heads(xd[:, r, :]), heads(xs[:, r, :]), bc(dpar[:, b, :], HD), ALU.mult).then_inc(xd_done, 1)

            def prologue():
                for i in range(WP):
                    low_piece(None, i)
                x_parts(0, 0, 0)
                pool.memset(sacc[:], 0.0).then_inc(sacc_zero, 1)

            def slot(hf, g, s, kind):
                u, q, it = at(hf, g, s)
                b, c, r = s // 4, s % 4, s % 2
                if c in (1, 2):
                    pool.wait_ge(b_done, u + 2)
                    pool.wait_ge(s_done, 3 * q + c + 1)
                    pool.tensor_tensor(heads(state[:]), heads(state[:]), bc(par[:, b, c, TOT_, :], HD), ALU.mult).then_inc(st_done, 1)
                if c > 0:
                    pool.wait_ge(y0_done, u + 2)
                    pool.wait_ge(t1_done, 3 * q + c + 1)
                    pool.tensor_tensor(y[:, r, :], y[:, r, :], t1[:], ALU.add).then_inc(y_done, 1)
                for i in split_at(s, kind):
                    low_piece(it, i)
                plain_wait(pool, half_ok, 1, sq_done, u + 2)
                pool.tensor_scalar(ve[:, r:r + 1], ss[:, r:r + 1], 1.0 / 512, EPS, ALU.mult, ALU.add).then_inc(ve_done, 1)
                pool.wait_ge(ve_done, u + 2)
                pool.tensor_tensor(rs[:, r:r + 1], ve[:, r:r + 1], half[:], ALU.pow).then_inc(rs_done, 1)
                q_adds(it, s, 0)
                if has_next(s, kind):
                    x_parts(u + 1, it + (s + 1) // SLOTS, (s + 1) % SLOTS)
                q_adds(it, s, 1)
                for k in range(5, SLOTS) if kind == "head" else [s - 3] if kind == "switch" and s >= 3 else []:
                    pool.wait_ge(s_stored, 16 * (k + 1) + 1)
                    pool.memset(sacc[:, k, :], 0.0).then_inc(sacc_zero, 1)

            walk(pool, prologue, slot, lambda v: None)

        @block.vector
        def _(dve):
            start_at_one(dve, q_seq, q_above, q_done, ctap, dtx_done, scan_done, m_done, s_done, t1_done, y0_done, yn_done, lo_done, sacc_done, o_lo)

            def conv(q, j, b):
                m = XBC * q + j
                dve.wait_ge(cev, m + 2)
                for d in (1, 2, 3):
                    if d > 1:
                        dve.wait_ge(ctap, 3 * m + d)
                    dve.scalar_tensor_tensor(out=cv[:, b, j, d:SEQ], in0=p_in[j % 2][:, 0:SEQ - d],
                                             scalar=cp[:, j, 3 - d:4 - d], in1=cv[:, b, j, d:SEQ],
                                             op0=ALU.mult, op1=ALU.add).then_inc(ctap, 1)

            def scan(n, it, s, free):
                r = s % 2
                dve.wait_ge(dab_ld[r], it * (16 * GU // 2) + 16 * (s // 2 + 1))
                dve.wait_ge(b_done, free + 1)
                dve.tensor_tensor_scan(out=dec[:, r, :], data0=dab[:, r, :], data1=eye8[:].rearrange("p h t -> p (h t)"),
                                       initial=0.0, op0=ALU.mult, op1=ALU.add).then_inc(scan_done, 1)

            def x_and_m(u, it, s):
                b, c, r = s // 4, s % 4, s % 2
                dve.wait_ge(xs_done, u + 2)
                if c == 0:
                    dve.wait_ge(par_ld[b], 32 * it + 32)
                dve.tensor_tensor(heads(dtx[:, r, :]), heads(p_turn[:]), bc(par[:, b, c, DT_, :], HD), ALU.mult).then_inc(dtx_done, 1)
                dve.wait_ge(bt_done, u + 2)
                dve.wait_ge(scan_done, u + 2)
                d = dec[:, r, :].rearrange("p (h t) -> p h t", h=HPG)
                dve.tensor_tensor(d, d, p_bg[:, P:2 * P].rearrange("p (o t) -> p o t", o=1).to_broadcast([P, HPG, P]),
                                  ALU.mult).then_inc(m_done, 1)

            def low_part(v):
                dve.wait_ge(c_done, v + 2)
                dve.wait_ge(hi_done, v + 2)
                dve.tensor_tensor(yt[:, 1, :], p_turn[:], yt[:, 0, :].bitcast(F32), ALU.subtract).then_inc(lo_done, 1)

            def scales(vec):
                return vec[:].rearrange("p (b o) -> p b o", o=1).to_broadcast([P, QB, BLK])

            def q_masks(it, s, place):
                for j in q_plan[s % 4][place]:
                    m = QM * (2 * it + s // 4) + j - 1
                    dve.wait_ge(q_add, m)
                    dve.tensor_scalar(q_mask[:, j % 2, :, :], q_w[:, s // 4, :, :], float(bound[j]),
                                      float(code[j + 1] - code[j]), ALU.is_gt, ALU.mult).then_inc(q_above, 1)

            def q_end(n):
                dve.wait_ge(q_add, QM * (n + 1) + 1)
                dve.wait_ge(q_st, 16 * n + 1)
                dve.scalar_tensor_tensor(out=q_res[:], in0=q_acc[:], scalar=float(code[0]), in1=scales(q_max),
                                         op0=ALU.add, op1=ALU.mult).then_inc(q_done, 1)

            def q_scale(it, s):
                n = 2 * it + s // 4
                dve.wait_ge(q_ld[s // 4], 16 * it + 16)
                dve.wait_ge(q_done, n + 1)
                dve.tensor_reduce(q_max[:], q_w[:, s // 4, :, :], AX_X, ALU.max, apply_absolute_value=True).then_inc(q_seq, 1)
                dve.wait_ge(q_seq, 4 * n + 2)
                dve.scalar_tensor_tensor(out=q_safe[:], in0=q_max[:], scalar=0.0, in1=q_max[:],
                                         op0=ALU.is_equal, op1=ALU.add).then_inc(q_seq, 1)
                dve.wait_ge(q_seq, 4 * n + 3)
                dve.reciprocal(q_inv[:], q_safe[:]).then_inc(q_seq, 1)

            def q_start(it, s):
                n, w = 2 * it + s // 4, q_w[:, s // 4, :, :]
                dve.wait_ge(q_seq, 4 * n + 4)
                dve.tensor_tensor(w, w, scales(q_inv), ALU.mult).then_inc(q_seq, 1)
                dve.wait_ge(q_seq, 4 * n + 5)
                dve.tensor_scalar(q_acc[:], w, float(bound[0]), float(code[1] - code[0]), ALU.is_gt, ALU.mult)

            def add_out(v, s):
                dve.wait_ge(d_done, v + 2)
                dve.wait_ge(sacc_done, v + 1)
                dve.tensor_tensor(sacc[:, s, :], sacc[:, s, :], p_ou[:], ALU.add).then_inc(sacc_done, 1)

            def low_output(it, pieces):
                for i in pieces:
                    dve.wait_ge(w_hi, GP * it + WP + i + 1)
                    src = raw[:, i % 2, :]
                    dve.scalar_tensor_tensor(out=ow[:, 1, i, :], in0=src[:, 0:DM], scalar=src[:, DM:DM + 1],
                                             in1=ow[:, 0, i, :].bitcast(F32), op0=ALU.mult, op1=ALU.subtract).then_inc(o_lo, 1)

            def prologue():
                for j in range(XBC):
                    conv(0, j, 0)
                dve.wait_ge(eye_ld, 16)
                scan(0, 0, 0, 0)
                scan(1, 0, 1, 0)
                x_and_m(0, 0, 0)

            def slot(hf, g, s, kind):
                u, q, it = at(hf, g, s)
                b, c, r = s // 4, s % 4, s % 2
                mid, end = plan(s, kind)
                dve.wait_ge(b_done, u + 2)
                dve.wait_ge(xd_done, u + 2)
                dve.wait_ge(c_done, (u if kind == "first" else u - 1) + 1)
                dve.tensor_tensor(y[:, r, :], p_yi[:], xd[:, r, :], ALU.add).then_inc(y0_done, 1)
                if c > 0:
                    dve.wait_ge(y_done, 3 * q + c)
                    dve.tensor_tensor(heads(t1[:]), heads(p_ye[:]), bc(par[:, b, c, EXC_, :], HD), ALU.mult).then_inc(t1_done, 1)
                if kind != "first":
                    low_part(u - 1)
                if c == 0:
                    dve.wait_ge(s_done, 3 * q + 1)
                    dve.tensor_copy(state[:], p_ou[:]).then_inc(s_done, 1)
                elif c < 3:
                    dve.wait_ge(st_done, 2 * q + c + 1)
                    dve.tensor_tensor(state[:], state[:], p_ou[:], ALU.add).then_inc(s_done, 1)
                if s == 1:
                    low_output(it, (2, 3))
                q_masks(it, s, 0)
                if c == 0:
                    if kind != "first":
                        q_end(2 * it + s // 4 - 1)
                    q_scale(it, s)
                if not (kind == "last" and s >= SLOTS - 2):
                    scan(u + 2, it + (s + 2) // SLOTS, (s + 2) % SLOTS, u + 1)
                for what, j in mid:
                    if what == "x":
                        conv(q + 1, j, 1 - b)
                if has_next(s, kind):
                    x_and_m(u + 1, it + (s + 1) // SLOTS, (s + 1) % SLOTS)
                dve.wait_ge(rs_done, u + 2)
                dve.wait_ge(sg_done, u + 2)
                dve.scalar_tensor_tensor(out=y[:, r, :], in0=y[:, r, :], scalar=rs[:, r:r + 1], in1=sg[:, s % 4, :],
                                         op0=ALU.mult, op1=ALU.mult).then_inc(yn_done, 1)
                if kind != "first":
                    dve.wait_ge(sacc_zero, 1 if hf == 0 or s == 0 and kind == "head" else 1 + ((s - 1) % SLOTS + 1))
                    add_out(u - 1, (s - 1) % SLOTS)
                if s == 0:
                    low_output(it, (0, 1))
                if c == 0:
                    q_start(it, s)
                q_masks(it, s, 1)
                for what, j in end:
                    if what == "x":
                        conv(q + 1, j, 1 - b)

            def drain(v):
                q_end(QPIECES - 1)
                low_part(v)
                add_out(v, SLOTS - 1)

            walk(dve, prologue, slot, drain)

        @block.scalar
        def _(act):
            start_at_one(act, cev, silu_cv, xs_done, bt_done, sq_done, sg_done, hi_done)

            def high_piece(it, i):
                dst, _ = piece_of(it, i)
                arrived, count, src = loaded(it, i)
                act.wait_ge(arrived, count)
                act.activation(dst[:, 0], src[:, 0:DM], ACT.Copy).then_inc(w_hi, 1)

            def high_output(it, pieces):
                for i in pieces:
                    act.wait_ge(*loaded(it, i)[:2])
                    act.activation(ow[:, 0, i, :], raw[:, i % 2, 0:DM], ACT.Copy, scale=raw[:, i % 2, DM:DM + 1]).then_inc(w_hi, 1)

            def evac(q, j, b, free):
                act.wait_ge(in_done, XBC * q + j + 2)
                act.wait_ge(b_done, free + 1)
                act.activation(cv[:, b, j, :], p_in[j % 2][:], ACT.Identity, bias=cp[:, j, 4:5], scale=cp[:, j, 3:4])\
                    .then_inc(cev, 1)

            def silu_conv(q, b):
                act.wait_ge(ctap, 3 * XBC * q + 3 * XBC + 1)
                act.activation(cv[:, b, :, :], cv[:, b, :, :], ACT.Silu).then_inc(silu_cv, 1)

            def silu_gate(n, w):
                act.wait_ge(g_done, n + 2)
                act.wait_ge(yn_done, max(n - 3, 0) + 1 if isinstance(n, int) else n - 3 + 1)
                act.activation(sg[:, w % 4, :], p_gate[:], ACT.Silu).then_inc(sg_done, 1)

            def tokens(u, s, free):
                r = s % 2
                act.wait_ge(a_done, u + 2)
                act.wait_ge(xw_done, free + 1)
                act.wait_ge(xd_done, free + 1)
                act.activation(xs[:, r, :], p_turn[:], ACT.Copy).then_inc(xs_done, 1)
                act.wait_ge(b_done, free + 1)
                act.activation(bt[:, r, :], p_bg[:, 0:P], ACT.Copy).then_inc(bt_done, 1)

            def high_part(v):
                act.wait_ge(c_done, v + 2)
                act.wait_ge(d_done, v + 1)
                act.activation(yt[:, 0, :], p_turn[:], ACT.Copy).then_inc(hi_done, 1)

            def prologue():
                for i in range(XBC):
                    high_piece(None, i)
                act.wait_ge(cp_ld, 16)
                for j in range(XBC):
                    evac(0, j, 0, 0)
                    if XBC + j < WP:
                        high_piece(None, XBC + j)
                silu_conv(0, 0)
                silu_gate(0, 0)
                tokens(0, 0, 0)
                for w in range(1, GATES_AHEAD):
                    silu_gate(w, w)

            def slot(hf, g, s, kind):
                u, q, it = at(hf, g, s)
                b, c, r = s // 4, s % 4, s % 2
                mid, end = plan(s, kind)

                def extra(part):
                    for what, j in part:
                        if what == "x":
                            if s == 4:
                                act.wait_ge(cp_ld, 16 * it + 32)
                            evac(q + 1, j, 1 - b, u)
                        else:
                            silu_gate(gates_before(it, s, j), j)

                if s == 1:
                    high_output(it, (2, 3))
                for i in split_at(s, kind):
                    if i < OWP + XBC:
                        act.wait_ge(in_done, XBC * (GQ * it + 1) + i - OWP + 2)
                    else:
                        act.wait_ge(g_done, GU * it + GU + 1)
                    high_piece(it, i)
                if kind != "first":
                    high_part(u - 1)
                if c > 0:
                    act.wait_ge(y_done, 3 * q + c + 1)
                else:
                    act.wait_ge(y0_done, u + 2)
                act.wait_ge(ve_done, (u if kind == "first" else u - 1) + 1)
                act.activation(junk[:], y[:, r, :], ACT.Square, accum_out=ss[:, r:r + 1]).then_inc(sq_done, 1)
                extra(mid)
                if has_next(s, kind):
                    tokens(u + 1, (s + 1) % SLOTS, u)
                if ("x", XBC - 1) in mid:
                    silu_conv(q + 1, 1 - b)
                if s == 0:
                    act.wait_ge(d_done, u + 1)
                    high_output(it, (0, 1))
                extra(end)

            walk(act, prologue, slot, high_part)

        @block.tensor
        def _(pe):
            start_at_one(pe, in_done, a_done, b_done, g_done, c_done, d_done)

            def conv_in(q, it, j, b, free):
                if b == 0:
                    pe.wait_ge(w_lo, WP * it + j + 1 + 1)
                pe.wait_ge(ctap, free + 1)
                split3(pe, p_in[j % 2][:], lambda a, k: wx[:, a, j, k * P:(k + 1) * P],
                       lambda a, k: xn[:, a, k, b * SEQ:(b + 1) * SEQ], KD).then_inc(in_done, 1)

            def gate(n, it, w):
                if w == 0:
                    pe.wait_ge(w_lo, WP * it + WP + 1)
                pe.wait_ge(sg_done, n + 1)
                split3(pe, p_gate[:], lambda a, k: xn[:, a, k, w * P:(w + 1) * P],
                       lambda a, k: wg[:, a, k, :], KD).then_inc(g_done, 1)

            def turn_in(u, q, s, turned):
                b, c = s // 4, s % 4
                ch = slice(c * P, (c + 1) * P)
                pe.wait_ge(silu_cv, q + 2)
                pe.wait_ge(hi_done, turned + 1)
                pe.wait_ge(lo_done, turned + 1)
                pe.wait_ge(xs_done, u + 1)
                pe.wait_ge(dtx_done, u + 1)
                for k in range(4):
                    pe.transpose(p_turn[:, k * P:(k + 1) * P], cv[:, b, k, ch], ident)
                pe.wait_ge(m_done, u + 1)
                pe.wait_ge(bt_done, u + 1)
                pe.transpose(p_bg[:, 0:P], cv[:, b, 4, ch], ident)
                pe.matmul(p_bg[:, P:2 * P], cv[:, b, 4, ch], cv[:, b, 5, ch], start=True, stop=True).then_inc(a_done, 1)

            def turn_out(v, s):
                pe.wait_ge(yn_done, v + 2)
                for k in range(KD):
                    last = pe.transpose(p_turn[:, k * P:(k + 1) * P], y[:, s % 2, k * P:(k + 1) * P], ident)
                last.then_inc(c_done, 1)

            def project(v, it):
                pe.wait_ge(hi_done, v + 2)
                pe.wait_ge(lo_done, v + 2)
                pe.wait_ge(o_lo, OWP * it + OWP + 1)
                split3(pe, p_ou[:], lambda a, k: yt[:, a, k * P:(k + 1) * P], lambda a, k: ow[:, a, k, :], KD).then_inc(d_done, 1)

            def prologue():
                pe.wait_ge(xn_ld[0], 16 * 4)
                for j in range(XBC):
                    conv_in(0, 0, j, 0, max(3 * (j - 1), 0))
                gate(0, 0, 0)
                pe.wait_ge(eye_ld, 16)
                turn_in(0, 0, 0, 0)
                for w in range(1, GATES_AHEAD):
                    gate(w, 0, w)

            def slot(hf, g, s, kind):
                u, q, it = at(hf, g, s)
                b, c, r = s // 4, s % 4, s % 2
                mid, end = plan(s, kind)

                def extra(part):
                    for what, j in part:
                        if what == "x":
                            conv_in(q + 1, it + b, j, 1 - b, 3 * (XBC * (q + 1) + j - 1))
                        else:
                            gate(gates_before(it, s, j), it + (1 if s >= 6 else 0), j)

                if kind == "switch" and s == 4:
                    pe.wait_ge(xn_ld[0], 16 * 4 * (hf + 2))
                if kind in ("first", "head"):
                    pe.wait_ge(xn_ld[1], 16 * 4 * (hf + 1))
                pe.wait_ge(m_done, u + 2)
                pe.wait_ge(dtx_done, u + 2)
                pe.wait_ge(y0_done, u + 1)
                for h in range(HPG):
                    last = pe.matmul(p_yi[:, h * HD:(h + 1) * HD], dec[:, r, h * P:(h + 1) * P], dtx[:, r, h * HD:(h + 1) * HD],
                                     start=True, stop=True)
                if c > 0:
                    pe.wait_ge(s_done, 3 * q + c + 1)
                    pe.wait_ge(t1_done, 3 * q + c)
                    last = pe.matmul(p_ye[:], cv[:, b, 5, c * P:(c + 1) * P], state[:], start=True, stop=True)
                if c < 3:
                    pe.wait_ge(bt_done, u + 2)
                    pe.wait_ge(xw_done, u + 2)
                    pe.wait_ge(sacc_done, (u if kind == "first" else u - 1) + 1)
                    last = pe.matmul(p_ou[:], bt[:, r, :], xw[:, r, :], start=True, stop=True)
                last.then_inc(b_done, 1)
                if kind != "first":
                    pe.wait_ge(xs_done, u + 2)
                    pe.wait_ge(dtx_done, u + 2)
                    turn_out(u - 1, (s - 1) % SLOTS)
                extra(mid)
                if has_next(s, kind):
                    turn_in(u + 1, hf * HQ + g * GQ + (s + 1) // 4, (s + 1) % SLOTS, u)
                if kind != "first":
                    pe.wait_ge(s_done, 3 * q + min(c + 1, 3) + 1)
                    pe.wait_ge(sacc_done, u)
                    project(u - 1, it - (1 if s == 0 else 0))
                extra(end)

            def drain(v):
                turn_out(v, SLOTS - 1)
                pe.wait_ge(sacc_done, v + 1)
                project(v, HALVES * GROUPS - 1)

            walk(pe, prologue, slot, drain)


def ffn_phase(nc, S, tag, xnt_dram, hidden, weights, x_dram, s_dram, out_dram, turn, experts=None):
    gate_dram, up_dram, down_dram = weights
    nf = -(-hidden // P)
    width = [min(P, hidden - f * P) for f in range(nf)]
    with ExitStack() as ctx:
        def sb(n, s, d=F32):
            return ctx.enter_context(nc.sbuf_tensor(tag + n, s, d))

        def sem(n):
            return S(tag + n)

        wg = sb("wg", [P, 2, nf, KD * P], F32R)
        wu = sb("wu", [P, 2, nf, KD * P], F32R)
        wd = sb("wd", [P, 2, nf, DM], F32R)
        raw = sb("raw", [P, 3, DM])
        xn = sb("xn", [P, 2, 2, KD, SEQ], F32R)
        gs = sb("gs", [P, 2, SEQ])
        h = sb("h", [P, 2, SEQ])
        ht = sb("ht", [P, 2, 2, SEQ], F32R)
        xi, xo = (sb(n, [P, 2, DM]) for n in ("xi", "xo"))
        ge = sb("ge", [P, 4, DM])
        si = sb("si", [P, 2, s_dram.shape[-1]])
        ident = sb("ident", [P, P])
        bank = [ctx.enter_context(nc.psum_tensor(f"{tag}bank{i}", [P, 512], F32)) for i in range(8)]
        pg, pu, pw, po = bank[0:2], bank[2], bank[3], bank[4:8]
        if experts is not None:
            rep = sb("rep", [EXPERTS, hidden], F32R)
            rep_raw = sb("rep_raw", [EXPERTS, hidden])
            wt = sb("wt", [EXPERTS, 2, 2, SEQ], F32R)
        raw_ld = [sem(f"raw_ld{i}") for i in range(3)]
        id_ld, w_hi, w_lo = sem("id_ld"), sem("w_hi"), sem("w_lo")
        if turn:
            turned = sem("turned")
        xn_ld = [sem(f"xn_ld{i}") for i in range(2)]
        in_ld = [sem(f"in_ld{i}") for i in range(2)]
        stored = [sem(f"stored{i}") for i in range(2)]
        g_done, u_done, silu_ok, h_ok = sem("g_done"), sem("u_done"), sem("silu_ok"), sem("h_ok")
        if experts is not None:
            w_done, hw_ok = sem("w_done"), sem("hw_ok")
        hi_ok, lo_ok, d_done = sem("hi_ok"), sem("lo_ok"), sem("d_done")
        ge_ok, sg_ok, res_ok = sem("ge_ok"), sem("sg_ok"), sem("res_ok")
        block = ctx.enter_context(nc.Block())

        LX = 16 * 4 * (2 if experts is not None else 1)
        order = [("g", 0), ("u", 0)]
        for f in range(nf):
            order += [("g", f + 1), ("u", f + 1)] * (f + 1 < nf) + [("d", f)]
        place = {piece: n for n, piece in enumerate(order)}

        def cut(bank, w):
            return bank.rearrange("p (k n) -> p k n", k=KD)[:, :, 0:w]

        def piece_views(n):
            kind, f = order[n]
            w, buf = width[f], raw[:, n % 3, :]
            if kind == "d":
                dst = wd[0:w, :, f, :]
                if turn:
                    return (down_dram[:, f * P:f * P + w].rearrange("(k p) n -> p k n", p=P),
                            buf[:, 0:KD * w].rearrange("p (k n) -> p k n", k=KD), pw[0:w, :], dst[:, 0], dst[:, 1])
                return down_dram[:, f, :], buf, buf, dst[:, 0], dst[:, 1]
            dram, dst = (gate_dram, wg) if kind == "g" else (up_dram, wu)
            if turn:
                return dram[f * P:f * P + w, :], raw[0:w, n % 3, :], cut(pw[:], w), cut(dst[:, 0, f, :], w), cut(dst[:, 1, f, :], w)
            return dram[f], buf, buf, dst[:, 0, f, :], dst[:, 1, f, :]

        NSEQ = T // SEQ

        @block.sync
        def _(sp):
            sp.dma_start(ident[:], S.ident_dram).then_inc(id_ld, 16)
            start_at_one(sp, *xn_ld, *in_ld, *stored)
            if experts is not None:
                sp.dma_start(rep_raw[:], S.rep_dram).then_inc(id_ld, 16)

            def load_xn(tile, r):
                for c in range(4):
                    sp.dma_start(xn[:, r, :, :, c * P:(c + 1) * P].bitcast(F32),
                                 xnt_dram[tile + c].rearrange("p a (k t) -> p a k t", k=KD)).then_inc(xn_ld[r], 16)
                    if experts is not None:
                        sp.dma_start(wt[:, r, :, c * P:(c + 1) * P].bitcast(F32), experts[tile + c]).then_inc(xn_ld[r], 16)

            for n in range(len(order)):
                if n >= 3:
                    sp.wait_ge(w_lo, n - 2)
                src, dst, _, _, _ = piece_views(n)
                sp.dma_start(dst, src).then_inc(raw_ld[n % 3], 16)
                if n == 2:
                    load_xn(0, 0)
                if n == 8:
                    load_xn(4, 1)
            for q in range(NSEQ):
                for c in range(4):
                    t = 4 * q + c
                    sp.wait_ge(res_ok, max(t - 2, -1) + 1 + 1)
                    sp.dma_start(xi[:, c % 2, :], x_dram[t]).then_inc(in_ld[c % 2], 16)
                    sp.dma_start(si[:, c % 2, :], s_dram[t]).then_inc(in_ld[c % 2], 16)
                    if t >= 1:
                        sp.wait_ge(res_ok, t + 1)
                        sp.dma_start(out_dram[t - 1], xo[:, (t - 1) % 2, :]).then_inc(stored[(t - 1) % 2], 16)
                if q + 2 < NSEQ:
                    sp.wait_ge(d_done, (q + 1) * nf + 1)
                    load_xn(4 * (q + 2), q % 2)
            sp.wait_ge(res_ok, NT + 1)
            sp.dma_start(out_dram[NT - 1], xo[:, 1, :]).then_inc(stored[1], 16)
            for r in range(2):
                sp.wait_ge(stored[r], 16 * NT // 2 + 1)

        @block.scalar
        def _(act):
            start_at_one(act, silu_ok, hi_ok, ge_ok)

            def high_weight(kind, f):
                n = place[kind, f]
                _, _, src, dst, _ = piece_views(n)
                if turn:
                    act.wait_ge(turned, n + 1)
                else:
                    act.wait_ge(raw_ld[n % 3], 16 * (n // 3 + 1))
                act.activation(dst, src, ACT.Copy).then_inc(w_hi, 1)

            def high(n, f):
                act.wait_ge(hw_ok if experts is not None else h_ok, n + 1 + 1)
                act.wait_ge(d_done, max(n - 1, 0) + 1)
                act.activation(ht[0:width[f], n % 2, 0, :], h[0:width[f], n % 2, :], ACT.Copy).then_inc(hi_ok, 1)

            def silu_sums(q):
                for c in range(4):
                    act.wait_ge(d_done, q * nf + nf + 1)
                    act.wait_ge(res_ok, max(4 * q + c - 3, 0) + 1)
                    act.activation(ge[:, c, :], po[c][:], ACT.Silu).then_inc(ge_ok, 1)

            high_weight("g", 0)
            high_weight("u", 0)
            for q in range(NSEQ):
                n0 = q * nf
                for f in range(nf):
                    if n0 + f >= 1:
                        high(n0 + f - 1, (f - 1) % nf)
                    act.wait_ge(g_done, n0 + f + 1 + 1)
                    act.wait_ge(h_ok, max(n0 + f - 1, 0) + 1)
                    act.activation(gs[0:width[f], (n0 + f) % 2, :], pg[(n0 + f) % 2][0:width[f], :], ACT.Silu).then_inc(silu_ok, 1)
                    if q == 0:
                        if f + 1 < nf:
                            high_weight("g", f + 1)
                            high_weight("u", f + 1)
                        high_weight("d", f)
                    if f == 0 and q >= 1:
                        silu_sums(q - 1)
            high(NSEQ * nf - 1, nf - 1)
            silu_sums(NSEQ - 1)

        @block.vector
        def _(dve):
            start_at_one(dve, h_ok, lo_ok, sg_ok, res_ok, *([hw_ok] if experts is not None else []))

            def low_weight(kind, f):
                n = place[kind, f]
                _, _, src, high, low = piece_views(n)
                dve.wait_ge(w_hi, n + 1)
                dve.tensor_tensor(low, src, high.bitcast(F32), ALU.subtract).then_inc(w_lo, 1)

            def low(n, f):
                dve.wait_ge(hi_ok, n + 1 + 1)
                w = width[f]
                dve.tensor_tensor(ht[0:w, n % 2, 1, :], h[0:w, n % 2, :], ht[0:w, n % 2, 0, :].bitcast(F32), ALU.subtract)\
                    .then_inc(lo_ok, 1)

            low_weight("g", 0)
            if experts is not None:
                dve.wait_ge(id_ld, 32)
                dve.tensor_copy(rep[:], rep_raw[:])
            low_weight("u", 0)
            def residual(t):
                c, r = t % 4, t % 2
                dve.wait_ge(ge_ok, t + 1 + 1)
                dve.wait_ge(in_ld[r], 32 * (t // 2 + 1) + 1)
                g3, s3 = ge[:, c, :], si[:, r, :]
                if experts is not None:
                    g3 = g3.rearrange("p (d h) -> p d h", d=QK)
                    s3 = s3.rearrange("p (d o) -> p d o", o=1).to_broadcast([P, QK, DM // QK])
                dve.tensor_tensor(g3, g3, s3, ALU.mult).then_inc(sg_ok, 1)
                dve.wait_ge(sg_ok, t + 1 + 1)
                dve.wait_ge(stored[r], 16 * (t // 2) + 1)
                dve.tensor_tensor(xo[:, r, :], ge[:, c, :], xi[:, r, :], ALU.add).then_inc(res_ok, 1)

            for q in range(NSEQ):
                for f in range(nf):
                    w, n = width[f], q * nf + f
                    if n >= 1:
                        low(n - 1, (f - 1) % nf)
                    if q == 0 and f + 1 < nf:
                        low_weight("g", f + 1)
                    dve.wait_ge(silu_ok, n + 1 + 1)
                    dve.wait_ge(u_done, n + 1 + 1)
                    dve.wait_ge(lo_ok, max(n - 1, 0) + 1)
                    dve.tensor_tensor(h[0:w, n % 2, :], pu[0:w, :], gs[0:w, n % 2, :], ALU.mult).then_inc(h_ok, 1)
                    if experts is not None:
                        dve.wait_ge(w_done, n + 1 + 1)
                        dve.wait_ge(h_ok, n + 1 + 1)
                        dve.tensor_tensor(h[0:w, n % 2, :], pw[0:w, :], h[0:w, n % 2, :], ALU.mult).then_inc(hw_ok, 1)
                    if q == 0:
                        if f + 1 < nf:
                            low_weight("u", f + 1)
                        low_weight("d", f)
                    elif 1 <= f <= 4:
                        residual(4 * (q - 1) + f - 1)
            low(NSEQ * nf - 1, nf - 1)
            for c in range(4):
                residual(4 * (NSEQ - 1) + c)

        @block.tensor
        def _(pe):
            start_at_one(pe, g_done, u_done, d_done, *([w_done] if experts is not None else []))
            pe.wait_ge(id_ld, 32 if experts is not None else 16)

            def turn_weight(kind, f):
                if turn and f < nf:
                    n, w = place[kind, f], width[f]
                    pe.wait_ge(raw_ld[n % 3], 16 * (n // 3 + 1))
                    if n >= 1:
                        pe.wait_ge(w_lo, n)
                    for k in range(KD):
                        if kind == "d":
                            last = pe.transpose(pw[0:w, k * P:(k + 1) * P], raw[:, n % 3, k * w:(k + 1) * w], ident[:])
                        else:
                            last = pe.transpose(pw[:, k * P:k * P + w], raw[0:w, n % 3, k * P:(k + 1) * P], ident[0:w, 0:w])
                    last.then_inc(turned, 1)

            def products(out, kind, weights, q, f, done):
                if q == 0:
                    pe.wait_ge(w_lo, place[kind, f] + 1)
                split3(pe, out, lambda a, k: weights[:, a, f, k * P:k * P + width[f]],
                       lambda a, k: xn[:, q % 2, a, k, :], KD).then_inc(done, 1)

            def hidden_in(q, f):
                w, n = width[f], q * nf + f
                pe.wait_ge(silu_ok, max(n - 1, 0) + 1)
                products(pg[n % 2][0:w, :], "g", wg, q, f, g_done)
                if q == 0:
                    turn_weight("g", f + 1)
                pe.wait_ge(h_ok, n + 1)
                products(pu[0:w, :], "u", wu, q, f, u_done)
                if experts is not None:
                    pe.wait_ge(hw_ok, n + 1)
                    for a in range(2):
                        last = pe.matmul(pw[0:w, :], rep[:, f * P:f * P + w], wt[:, q % 2, a, :], start=(a == 0), stop=(a == 1))
                    last.then_inc(w_done, 1)
                if q == 0:
                    turn_weight("u", f + 1)

            def hidden_out(q, f):
                w, n = width[f], q * nf + f
                pe.wait_ge(hi_ok, n + 1 + 1)
                pe.wait_ge(lo_ok, n + 1 + 1)
                if f == 0:
                    pe.wait_ge(ge_ok, 4 * q + 1)
                if q == 0:
                    pe.wait_ge(w_lo, place["d", f] + 1)
                for c in range(4):
                    for m, (a, b) in enumerate(((0, 0), (0, 1), (1, 0))):
                        last = pe.matmul(po[c][:], ht[0:w, n % 2, a, c * P:(c + 1) * P], wd[0:w, b, f, :],
                                         start=(f == 0 and m == 0), stop=(f == nf - 1 and m == 2))
                last.then_inc(d_done, 1)

            turn_weight("g", 0)
            turn_weight("u", 0)
            for q in range(NSEQ):
                pe.wait_ge(xn_ld[q % 2], LX * (q // 2 + 1) + 1)
                for f in range(nf):
                    hidden_in(q, f)
                    if f >= 1:
                        hidden_out(q, f - 1)
                    elif q >= 1:
                        hidden_out(q - 1, nf - 1)
                    if q == 0:
                        turn_weight("d", f)
            hidden_out(NSEQ - 1, nf - 1)


def attention_phase(nc, S, qkvr, o_dram, wt_dram):
    GT = 4
    with ExitStack() as ctx:
        def sb(n, s, d=F32):
            return ctx.enter_context(nc.sbuf_tensor("a_" + n, s, d))

        sc, sv = (sb(n, [P, NT, QK, QK]) for n in ("sc", "sv"))
        mx, m2, sm, so = (sb(n, [P, NT, QK]) for n in ("mx", "m2", "sm", "so"))
        pr, one, eq, p2 = (sb(n, [P, NT, EXPERTS]) for n in ("pr", "one", "eq", "p2"))
        top, kmax, kmin = (sb(n, [P, NT]) for n in ("top", "kmax", "kmin"))
        desc = sb("desc", [P, EXPERTS])
        ident = sb("ident", [P, P])
        wt = sb("wt", [EXPERTS, NT, 2, P], F32R)
        pt = [ctx.enter_context(nc.psum_tensor(f"a_pt{i}", [P, 512], F32)) for i in range(4)]
        ld, seq, less_max, expd, with_v, summed, result, tr, wt_ok, out = (
            S("a_" + n) for n in ("ld", "seq", "less_max", "expd", "with_v", "summed", "result", "tr", "wt_ok", "out"))
        block = ctx.enter_context(nc.Block())
        q, k, v, lg = (qkvr[:, :, i * QK:(i + 1) * QK] for i in range(4))

        def pair(ap):
            return ap.rearrange("p a (d o) -> p a d o", o=1).to_broadcast([P, ap.shape[1], QK, QK])

        def along(ap):
            return ap.rearrange("p a (o e) -> p a o e", o=1).to_broadcast([P, ap.shape[1], QK, QK])

        def per_tile(ap):
            return ap.rearrange("p (a o) -> p a o", o=1).to_broadcast([P, NT, EXPERTS])

        def group(ap, j):
            return ap[:, GT * j:GT * j + GT]

        @block.sync
        def _(sp):
            sp.dma_start(desc[:], S.desc_dram).then_inc(ld, 16)
            sp.dma_start(ident[:], S.ident_dram).then_inc(ld, 16)
            sp.wait_ge(wt_ok, 8)
            sp.dma_start(wt_dram.rearrange("a e b t -> e a b t"), wt[:].bitcast(F32)).then_inc(out, 16)
            sp.wait_ge(result, 2)
            sp.dma_start(o_dram.rearrange("a p d -> p a d"), so[:]).then_inc(out, 16)
            sp.wait_ge(out, 32)

        @block.vector
        def _(dve):
            dve.tensor_reduce(top[:], lg, AX_X, ALU.max).then_inc(seq, 1)
            dve.tensor_reduce(kmax[:], k, AX_X, ALU.max).then_inc(seq, 1)
            dve.tensor_reduce(kmin[:], k, AX_X, ALU.min).then_inc(seq, 1)
            dve.wait_ge(seq, 1)
            dve.tensor_tensor(pr[:], lg, per_tile(top[:]), ALU.subtract).then_inc(less_max, 1)
            dve.wait_ge(seq, 3)
            dve.tensor_tensor(mx[:], q, per_tile(kmax[:]), ALU.mult).then_inc(seq, 1)
            dve.tensor_tensor(m2[:], q, per_tile(kmin[:]), ALU.mult).then_inc(seq, 1)
            dve.wait_ge(seq, 5)
            dve.tensor_tensor(mx[:], mx[:], m2[:], ALU.max).then_inc(seq, 1)
            n = 6
            for j in range(NT // GT):
                dve.tensor_tensor(group(sc, j), pair(group(q, j)), along(group(k, j)), ALU.mult).then_inc(seq, 1)
                dve.wait_ge(seq, n + 1)
                dve.tensor_tensor(group(sc, j), group(sc, j), pair(group(mx, j)), ALU.subtract).then_inc(less_max, 1)
                n += 1
            dve.wait_ge(ld, 32)
            dve.wait_ge(expd, 1)
            dve.tensor_reduce(top[:], pr[:], AX_X, ALU.add).then_inc(seq, 1)
            dve.wait_ge(seq, n + 1)
            dve.reciprocal(top[:], top[:]).then_inc(seq, 1)
            dve.wait_ge(seq, n + 2)
            dve.tensor_tensor(pr[:], pr[:], per_tile(top[:]), ALU.mult).then_inc(seq, 1)
            n += 3
            first = desc[:].rearrange("p (o e) -> p o e", o=1).to_broadcast([P, NT, EXPERTS])
            for rank, (left, mark) in enumerate(((pr, one), (p2, eq))):
                dve.wait_ge(seq, n)
                dve.tensor_reduce(top[:], left[:], AX_X, ALU.max).then_inc(seq, 1)
                dve.wait_ge(seq, n + 1)
                dve.tensor_tensor(mark[:], left[:], per_tile(top[:]), ALU.is_ge).then_inc(seq, 1)
                dve.wait_ge(seq, n + 2)
                dve.tensor_tensor(mark[:], mark[:], first, ALU.mult).then_inc(seq, 1)
                dve.wait_ge(seq, n + 3)
                dve.tensor_reduce(top[:], mark[:], AX_X, ALU.max).then_inc(seq, 1)
                dve.wait_ge(seq, n + 4)
                dve.tensor_tensor(mark[:], mark[:], per_tile(top[:]), ALU.is_equal).then_inc(seq, 1)
                n += 5
                if rank == 0:
                    dve.wait_ge(seq, n)
                    dve.scalar_tensor_tensor(out=p2[:], in0=one[:], scalar=-4.0, in1=pr[:], op0=ALU.mult, op1=ALU.add).then_inc(seq, 1)
                    n += 1
            dve.wait_ge(seq, n)
            dve.tensor_tensor(one[:], one[:], eq[:], ALU.add).then_inc(seq, 1)
            dve.wait_ge(seq, n + 1)
            dve.tensor_tensor(pr[:], pr[:], one[:], ALU.mult).then_inc(seq, 1)
            dve.wait_ge(seq, n + 2)
            dve.tensor_reduce(top[:], pr[:], AX_X, ALU.add).then_inc(seq, 1)
            dve.wait_ge(seq, n + 3)
            dve.reciprocal(top[:], top[:]).then_inc(seq, 1)
            dve.wait_ge(seq, n + 4)
            dve.tensor_tensor(pr[:], pr[:], per_tile(top[:]), ALU.mult).then_inc(result, 1)
            n += 4
            for j in range(NT // GT):
                dve.wait_ge(expd, j + 2)
                dve.tensor_reduce(group(sm, j), group(sc, j), AX_X, ALU.add).then_inc(summed, 1)
            for j in range(4):
                high, low = wt[:, 4 * j:4 * j + 4, 0, :], wt[:, 4 * j:4 * j + 4, 1, :]
                turned = pt[j][0:EXPERTS, :].rearrange("e (a t) -> e a t", a=4)
                dve.wait_ge(tr, j + 1)
                dve.tensor_copy(high, turned).then_inc(wt_ok, 1)
                dve.wait_ge(wt_ok, 2 * j + 1)
                dve.tensor_tensor(low, turned, high.bitcast(F32), ALU.subtract).then_inc(wt_ok, 1)
            dve.wait_ge(summed, NT // GT)
            dve.reciprocal(m2[:], sm[:]).then_inc(seq, 1)
            for j in range(NT // GT):
                dve.wait_ge(with_v, j + 1)
                dve.tensor_reduce(group(so, j), group(sv, j), AX_X, ALU.add).then_inc(summed, 1)
            dve.wait_ge(seq, n + 1)
            dve.wait_ge(summed, 2 * NT // GT)
            dve.tensor_tensor(so[:], so[:], m2[:], ALU.mult).then_inc(result, 1)

        @block.gpsimd
        def _(pool):
            for j in range(NT // GT):
                pool.wait_ge(expd, j + 2)
                pool.tensor_tensor(group(sv, j), group(sc, j), along(group(v, j)), ALU.mult).then_inc(with_v, 1)

        @block.scalar
        def _(act):
            act.wait_ge(less_max, 1)
            act.activation(pr[:], pr[:], ACT.Exp).then_inc(expd, 1)
            for j in range(NT // GT):
                act.wait_ge(less_max, j + 2)
                act.activation(group(sc, j), group(sc, j), ACT.Exp, scale=float(QK) ** -0.5).then_inc(expd, 1)

        @block.tensor
        def _(pe):
            pe.wait_ge(ld, 32)
            pe.wait_ge(result, 1)
            for j in range(4):
                for c in range(4):
                    last = pe.transpose(pt[j][0:EXPERTS, c * P:(c + 1) * P], pr[:, 4 * j + c, :], ident[:])
                last.then_inc(tr, 1)


_OUTS = [((4, 512, 512), 'float32')]


class Scope:

    def __init__(self, nc, ctx):
        self.nc, self.ctx = nc, ctx

    def __call__(self, name):
        return self.ctx.enter_context(self.nc.semaphore(name))


def program(nc, ins, out):
    with ExitStack() as ctx:
        S = Scope(nc, ctx)
        S.ident_dram, S.masks_dram, S.eye8_dram = ins["ident"], ins["masks"], ins["eye8"]
        S.desc_dram, S.rep_dram = ins["desc"], ins["rep"]

        def dram(n, s, d=F32):
            return nc.dram_tensor(n, s, d, kind="Internal").ap()

        xnt = dram("xnt", [NT, P, 2, DM])
        par = dram("par", [GROUPS, P, NT, 4, HPG])
        dat = dram("dat", [HEADS, T])
        with nc.sbuf_tensor("dtr", [P, NT, HEADS], F32) as dtr:
            norm_phase(nc, S, ins["x"], xnt, "n0_", ins["wdt"], (ins["dt_bias"],), dtr)
            step_phase(nc, S, dtr, ins["A_log"], par, dat)
        x0 = ins["x"].rearrange("(a p) d -> a p d", p=P)
        s0, x1, xnt1 = dram("s0", [NT, P, DM]), dram("x1", [NT, P, DM]), dram("xnt1", [NT, P, 2, DM])
        dq_all = dram("dq", [QPIECES, P, QB * BLK])
        ssm_phase(nc, S, xnt, ins["wx"], ins["wg"], ins["ow"], ins["cp"], ins["D"], par, dat, s0, ins["w123"], dq_all)
        flat = dq_all.rearrange("n p k -> (n p k)")
        dq = [flat[i * FF * DM:(i + 1) * FF * DM].rearrange("(r c) -> r c", c=c) for i, c in enumerate((DM, DM, FF))]
        ffn_phase(nc, S, "f_", xnt, FF, dq, x0, s0, x1, True)
        o1, wt1 = dram("o1", [NT, P, QK]), dram("wt1", [NT, EXPERTS, 2, P])
        with nc.sbuf_tensor("qkvr", [P, NT, NQ], F32) as qkvr:
            norm_phase(nc, S, x1.rearrange("a p d -> (a p) d"), xnt1, "n1_", ins["wkvr"], (ins["bk"], ins["bv"]), qkvr,
                       (ins["wq"], ins["bq"]))
            attention_phase(nc, S, qkvr, o1, wt1)
        ffn_phase(nc, S, "e_", xnt1, MF, (ins["eg"], ins["eu"], ins["ed"]), x1, o1,
                  out.rearrange("b (a p) d -> (b a) p d", p=P), False, wt1)


def kernel(**inputs):
    import concourse.bacc as _bacc
    from concourse import mybir as _mybir
    from concourse.bass_utils import run_bass_kernel_spmd as _run

    f = {k: np.asarray(v) for k, v in inputs.items()}
    a = {"x": f["L0_attn_hidden_states"].reshape(T, DM)}
    w = f["L0_attn_in_proj_w"].T
    inner = HEADS * HD
    kd = lambda m: m.reshape(m.shape[0] // P, P, m.shape[1]).transpose(1, 0, 2)
    gate, xb = w[:, :inner], w[:, inner:2 * inner]
    bb, cc, dt = w[:, 2 * inner:2 * inner + GROUPS * P], w[:, 2 * inner + GROUPS * P:-HEADS], w[:, -HEADS:]
    a["wx"] = np.stack([kd(np.concatenate([xb[:, g * 512:(g + 1) * 512], bb[:, g * P:(g + 1) * P], cc[:, g * P:(g + 1) * P]], 1))
                        .reshape(P, KD, XBC, P).transpose(2, 0, 1, 3).reshape(XBC, P, KD * P) for g in range(GROUPS)])
    a["wg"] = np.stack([kd(gate[:, g * 512:(g + 1) * 512]) for g in range(GROUPS)])
    a["wdt"] = kd(dt)
    cw = np.concatenate([f["L0_attn_conv_weight"], f["L0_attn_conv_bias"][:, None]], 1)
    a["cp"] = np.stack([np.concatenate([cw[g * 512:(g + 1) * 512], cw[inner + g * P:inner + (g + 1) * P],
                                        cw[inner + (GROUPS + g) * P:inner + (GROUPS + g + 1) * P]]).reshape(XBC, P, 5).transpose(1, 0, 2)
                        for g in range(GROUPS)])
    owt = np.concatenate([f["L0_attn_out_proj_w"].T, f["L0_attn_norm_weight"][:, None]], 1)
    a["ow"] = np.stack([kd(owt[g * 512:(g + 1) * 512]) for g in range(GROUPS)])
    a["dt_bias"], a["A_log"], a["D"] = f["L0_attn_dt_bias"], f["L0_attn_A_log"], f["L0_attn_D"]
    w123 = np.zeros(QPIECES * P * QB * BLK, np.float32)
    w123[:3 * FF * DM] = np.concatenate([f["L0_ffn_w1"].ravel(), f["L0_ffn_w2"].ravel(), f["L0_ffn_w3"].ravel()])
    a["w123"] = w123.reshape(QPIECES, P, QB * BLK)
    a["wq"] = kd(f["L1_attn_Wq"].reshape(DM, DM))
    a["wkvr"] = kd(np.concatenate([f["L1_attn_Wk"][..., 0], f["L1_attn_Wv"][..., 0], f["L1_ffn_gate_w"].T], 1))
    a["bq"], a["bk"], a["bv"] = f["L1_attn_bq"].reshape(DM), f["L1_attn_bk"].reshape(QK), f["L1_attn_bv"].reshape(QK)
    tiles = lambda m: kd(m).reshape(P, KD, MT, P).transpose(2, 0, 1, 3).reshape(MT, P, KD * P)
    a["eg"], a["eu"], a["ed"] = tiles(f["L1_ffn_g"].T), tiles(f["L1_ffn_u"].T), kd(f["L1_ffn_d"].T)
    a["desc"] = np.tile(np.arange(EXPERTS, 0, -1, dtype=np.float32), (P, 1))
    a["rep"] = np.repeat(np.eye(EXPERTS, dtype=np.float32), INTER, 1)
    eye = np.eye(P, dtype=np.float32)
    i = np.arange(P)
    a["ident"] = eye
    a["eye8"] = np.repeat(eye[:, None, :], HPG, 1)
    a["masks"] = np.stack([eye, (i[:, None] <= i[None]).astype(np.float32), (i[:, None] > i[None]).astype(np.float32),
                           np.ones((P, P), np.float32)], 1)
    nc = _bacc.Bacc("TRN2", target_bir_lowering=False, num_devices=1)
    arrays, ins = {}, {}
    for name, v in a.items():
        v = np.ascontiguousarray(v)
        arrays[f"in_{name}_dram"] = v
        ins[name] = nc.dram_tensor(f"in_{name}_dram", v.shape, _mybir.dt.from_np(v.dtype), kind="ExternalInput").ap()
    shape, dtype = _OUTS[0]
    out = nc.dram_tensor("out_0_dram", shape, _mybir.dt.from_np(np.dtype(dtype)), kind="ExternalOutput").ap()
    program(nc, ins, out)
    r = _run(nc, [arrays], core_ids=[0])
    return r.results[0]["out_0_dram"]
```
